# Optimizing a Trainium2 kernel written in Bass

```python
import numpy as np
import jax
import jax.numpy as jnp

def _softmax(x, axis=-1):
    return jax.nn.softmax(x, axis=axis)

def _gelu(x):
    return jax.nn.gelu(x, approximate=True)

def _silu(x):
    return jax.nn.silu(x)

def _sigmoid(x):
    return jax.nn.sigmoid(x)

def _layernorm(x, axis=-1, eps=1e-05):
    m = jnp.mean(x, axis=axis, keepdims=True)
    v = jnp.var(x, axis=axis, keepdims=True)
    return (x - m) / jnp.sqrt(v + eps)

def _scatter_add(tgt, idx, src, axis=0):
    return tgt.at[idx].add(src)

def _segment_sum(src, seg, n):
    return jax.ops.segment_sum(src, seg, n)
kernel_name = 'mk_vit_tower_cls_d1_tok_img256_r4_22a362'

def setup_inputs(seed: int=0):
    np.random.seed(seed)
    _w = jnp.asarray

    def _rec_inputs():
        import jax
        import jax.numpy as jnp
        _rk = jax.random.key(seed)
        x = 7.22013e-05 + 1.00017 * jax.random.normal(jax.random.fold_in(_rk, 1), (4, 64, 64, 64), jnp.float32)
        cls_tok = 0.02 * jax.random.normal(jax.random.fold_in(_rk, 5), (1, 1, 64), jnp.float32)
        return (x, cls_tok)
    x, cls_tok = _rec_inputs()

    def _L0_tok_setup():
        import jax, jax.numpy as jnp
        import numpy as np
        K = 3
        PAD = (K - 1) // 2
        BN_EPS = 1e-05

        def _unfold(x):
            b, c, h, w = x.shape
            xp = jnp.pad(x, ((0, 0), (0, 0), (PAD, PAD), (PAD, PAD)))
            shifts = [xp[:, :, i:i + h, j:j + w] for i in range(K) for j in range(K)]
            return jnp.stack(shifts, axis=2)
        key = jax.random.key(seed)
        ks = jax.random.split(key, 4)
        b, c, h, w = (8, 64, 64, 64)
        cr = c // 4
        x = jax.random.normal(ks[0], (b, c, h, w), dtype=jnp.float32)
        conv1_w = jax.random.normal(ks[1], (cr, c), dtype=jnp.float32) * (1.0 / np.sqrt(c))
        conv1_b = jnp.zeros((cr,), dtype=jnp.float32)
        bn_gamma = jnp.ones((cr,), dtype=jnp.float32)
        bn_beta = jnp.zeros((cr,), dtype=jnp.float32)
        bn_mean = jnp.zeros((cr,), dtype=jnp.float32)
        bn_var = jnp.ones((cr,), dtype=jnp.float32)
        conv2_w = jax.random.normal(ks[2], (K * K, cr), dtype=jnp.float32) * (1.0 / np.sqrt(cr))
        conv2_b = jnp.zeros((K * K,), dtype=jnp.float32)
        return {'x': x, 'conv1_w': conv1_w, 'conv1_b': conv1_b, 'bn_gamma': bn_gamma, 'bn_beta': bn_beta, 'bn_mean': bn_mean, 'bn_var': bn_var, 'conv2_w': conv2_w, 'conv2_b': conv2_b}
    _L0_tok_all = _L0_tok_setup()
    _L0_tok_in = {k: v for k, v in _L0_tok_all.items() if k in ('conv1_w', 'conv1_b', 'bn_gamma', 'bn_beta', 'bn_mean', 'bn_var', 'conv2_w', 'conv2_b')}
    del _L0_tok_all

    def _L0_attn_setup():
        import jax, jax.numpy as jnp
        import numpy as np
        B, L, H, P = (4, 2048, 64, 64)

        def discretize(log_real, imag, log_Delta, B_real, B_imag):
            Lr = -jnp.exp(log_real)
            Li = imag
            Delta = jnp.exp(log_Delta)
            ad = Lr * Delta
            bd = Li * Delta
            exp_ad = jnp.exp(ad)
            Lbar_r = exp_ad * jnp.cos(bd)
            Lbar_i = exp_ad * jnp.sin(bd)
            denom = jnp.maximum(Lr * Lr + Li * Li, 1e-12)
            inv_Lr = Lr / denom
            inv_Li = -Li / denom
            diff_r = Lbar_r - 1.0
            diff_i = Lbar_i
            coeff_r = inv_Lr * diff_r - inv_Li * diff_i
            coeff_i = inv_Lr * diff_i + inv_Li * diff_r
            B_bar_r = coeff_r[:, None] * B_real - coeff_i[:, None] * B_imag
            B_bar_i = coeff_r[:, None] * B_imag + coeff_i[:, None] * B_real
            return (Lbar_r, Lbar_i, B_bar_r, B_bar_i)

        def binop(ei, ej):
            Ar_i, Ai_i, xr_i, xi_i = ei
            Ar_j, Ai_j, xr_j, xi_j = ej
            return (Ar_j * Ar_i - Ai_j * Ai_i, Ar_j * Ai_i + Ai_j * Ar_i, Ar_j * xr_i - Ai_j * xi_i + xr_j, Ar_j * xi_i + Ai_j * xr_i + xi_j)

        def apply_ssm(Lbar_r, Lbar_i, B_bar_r, B_bar_i, C_real, C_imag, D, x):
            Bu_r = jnp.einsum('blh,ph->blp', x, B_bar_r)
            Bu_i = jnp.einsum('blh,ph->blp', x, B_bar_i)
            A_r = jnp.broadcast_to(Lbar_r, Bu_r.shape)
            A_i = jnp.broadcast_to(Lbar_i, Bu_i.shape)
            _, _, xs_r, xs_i = jax.lax.associative_scan(binop, (A_r, A_i, Bu_r, Bu_i), axis=1)
            ys = jnp.einsum('blp,hp->blh', xs_r, C_real) - jnp.einsum('blp,hp->blh', xs_i, C_imag)
            return ys + D * x

        def s5(log_real, imag, log_Delta, B_real, B_imag, C_real, C_imag, D, x):
            Lbar_r, Lbar_i, B_bar_r, B_bar_i = discretize(log_real, imag, log_Delta, B_real, B_imag)
            y = apply_ssm(Lbar_r, Lbar_i, B_bar_r, B_bar_i, C_real, C_imag, D, x)
            return jax.nn.gelu(y, approximate=False)
        key = jax.random.key(seed)
        ks = jax.random.split(key, 17)
        std_b = 1.0 / H ** 0.5
        std_c = 1.0 / P ** 0.5

        def params(ki):
            k = jax.random.split(ks[ki], 8)
            return dict(log_real=jax.random.normal(k[0], (P,), jnp.float32) * 0.5, imag=jax.random.normal(k[1], (P,), jnp.float32), log_Delta=jnp.zeros((P,), jnp.float32), B_real=jax.random.normal(k[2], (P, H), jnp.float32) * std_b, B_imag=jax.random.normal(k[3], (P, H), jnp.float32) * std_b, C_real=jax.random.normal(k[4], (H, P), jnp.float32) * std_c, C_imag=jax.random.normal(k[5], (H, P), jnp.float32) * std_c, D=jnp.ones((H,), jnp.float32))
        f = params(1)
        b = params(2)
        inp = {'x': jax.random.normal(ks[0], (B, L, H), jnp.float32)}
        for name, v in f.items():
            inp['fwd_' + name] = v
        for name, v in b.items():
            inp['bwd_' + name] = v
        return inp
    _L0_attn_all = _L0_attn_setup()
    _L0_attn_in = {k: v for k, v in _L0_attn_all.items() if k in ('fwd_log_real', 'fwd_imag', 'fwd_log_Delta', 'fwd_B_real', 'fwd_B_imag', 'fwd_C_real', 'fwd_C_imag', 'fwd_D', 'bwd_log_real', 'bwd_imag', 'bwd_log_Delta', 'bwd_B_real', 'bwd_B_imag', 'bwd_C_real', 'bwd_C_imag', 'bwd_D')}
    del _L0_attn_all

    def _L0_ffn_setup():
        import jax, jax.numpy as jnp
        import numpy as np
        C = 64
        HID = 256
        E = 8
        TEMP = 1.0
        key = jax.random.key(seed)
        ks = jax.random.split(key, 7)
        x = jax.random.normal(ks[0], (8, 4096, C), dtype=jnp.float32)
        W1 = jax.random.normal(ks[1], (C, HID), dtype=jnp.float32) * 0.02
        b1 = jnp.zeros((HID,), dtype=jnp.float32)
        Wg = jax.random.normal(ks[2], (HID, E), dtype=jnp.float32) * 0.02
        bg = jnp.zeros((E,), dtype=jnp.float32)
        Wd = jax.random.normal(ks[3], (E, HID, C), dtype=jnp.float32) * 0.02
        bd = jnp.zeros((E, C), dtype=jnp.float32)
        return {'x': x, 'W1': W1, 'b1': b1, 'Wg': Wg, 'bg': bg, 'Wd': Wd, 'bd': bd}
    _L0_ffn_all = _L0_ffn_setup()
    _L0_ffn_in = {k: v for k, v in _L0_ffn_all.items() if k in ('W1', 'b1', 'Wg', 'bg', 'Wd', 'bd')}
    del _L0_ffn_all
    return {'x': x, 'cls_tok': cls_tok, 'L0_tok_conv1_w': _L0_tok_in['conv1_w'], 'L0_tok_conv1_b': _L0_tok_in['conv1_b'], 'L0_tok_bn_gamma': _L0_tok_in['bn_gamma'], 'L0_tok_bn_beta': _L0_tok_in['bn_beta'], 'L0_tok_bn_mean': _L0_tok_in['bn_mean'], 'L0_tok_bn_var': _L0_tok_in['bn_var'], 'L0_tok_conv2_w': _L0_tok_in['conv2_w'], 'L0_tok_conv2_b': _L0_tok_in['conv2_b'], 'L0_attn_fwd_log_real': _L0_attn_in['fwd_log_real'], 'L0_attn_fwd_imag': _L0_attn_in['fwd_imag'], 'L0_attn_fwd_log_Delta': _L0_attn_in['fwd_log_Delta'], 'L0_attn_fwd_B_real': _L0_attn_in['fwd_B_real'], 'L0_attn_fwd_B_imag': _L0_attn_in['fwd_B_imag'], 'L0_attn_fwd_C_real': _L0_attn_in['fwd_C_real'], 'L0_attn_fwd_C_imag': _L0_attn_in['fwd_C_imag'], 'L0_attn_fwd_D': _L0_attn_in['fwd_D'], 'L0_attn_bwd_log_real': _L0_attn_in['bwd_log_real'], 'L0_attn_bwd_imag': _L0_attn_in['bwd_imag'], 'L0_attn_bwd_log_Delta': _L0_attn_in['bwd_log_Delta'], 'L0_attn_bwd_B_real': _L0_attn_in['bwd_B_real'], 'L0_attn_bwd_B_imag': _L0_attn_in['bwd_B_imag'], 'L0_attn_bwd_C_real': _L0_attn_in['bwd_C_real'], 'L0_attn_bwd_C_imag': _L0_attn_in['bwd_C_imag'], 'L0_attn_bwd_D': _L0_attn_in['bwd_D'], 'L0_ffn_W1': _L0_ffn_in['W1'], 'L0_ffn_b1': _L0_ffn_in['b1'], 'L0_ffn_Wg': _L0_ffn_in['Wg'], 'L0_ffn_bg': _L0_ffn_in['bg'], 'L0_ffn_Wd': _L0_ffn_in['Wd'], 'L0_ffn_bd': _L0_ffn_in['bd']}

def reference(x, cls_tok, L0_tok_conv1_w, L0_tok_conv1_b, L0_tok_bn_gamma, L0_tok_bn_beta, L0_tok_bn_mean, L0_tok_bn_var, L0_tok_conv2_w, L0_tok_conv2_b, L0_attn_fwd_log_real, L0_attn_fwd_imag, L0_attn_fwd_log_Delta, L0_attn_fwd_B_real, L0_attn_fwd_B_imag, L0_attn_fwd_C_real, L0_attn_fwd_C_imag, L0_attn_fwd_D, L0_attn_bwd_log_real, L0_attn_bwd_imag, L0_attn_bwd_log_Delta, L0_attn_bwd_B_real, L0_attn_bwd_B_imag, L0_attn_bwd_C_real, L0_attn_bwd_C_imag, L0_attn_bwd_D, L0_ffn_W1, L0_ffn_b1, L0_ffn_Wg, L0_ffn_bg, L0_ffn_Wd, L0_ffn_bd):
    import jax
    import jax.numpy as jnp

    def _L0_tok_ref(x, conv1_w, conv1_b, bn_gamma, bn_beta, bn_mean, bn_var, conv2_w, conv2_b):
        import jax, jax.numpy as jnp
        import numpy as np
        K = 3
        PAD = (K - 1) // 2
        BN_EPS = 1e-05

        def _unfold(x):
            b, c, h, w = x.shape
            xp = jnp.pad(x, ((0, 0), (0, 0), (PAD, PAD), (PAD, PAD)))
            shifts = [xp[:, :, i:i + h, j:j + w] for i in range(K) for j in range(K)]
            return jnp.stack(shifts, axis=2)
        b, c, h, w = x.shape
        y = jnp.einsum('oc,bchw->bohw', conv1_w, x) + conv1_b[None, :, None, None]
        y = (y - bn_mean[None, :, None, None]) * (bn_gamma[None, :, None, None] * jax.lax.rsqrt(bn_var + BN_EPS)[None, :, None, None]) + bn_beta[None, :, None, None]
        y = jax.nn.relu(y)
        wdyn = jnp.einsum('ok,bkhw->bohw', conv2_w, y) + conv2_b[None, :, None, None]
        patches = _unfold(x)
        out = jnp.einsum('bckhw,bkhw->bchw', patches, wdyn)
        return out.reshape(b, h * w, c)

    def _L0_attn_ref(x, fwd_log_real, fwd_imag, fwd_log_Delta, fwd_B_real, fwd_B_imag, fwd_C_real, fwd_C_imag, fwd_D, bwd_log_real, bwd_imag, bwd_log_Delta, bwd_B_real, bwd_B_imag, bwd_C_real, bwd_C_imag, bwd_D):
        import jax, jax.numpy as jnp
        import numpy as np
        B, L, H, P = (4, 2048, 64, 64)

        def discretize(log_real, imag, log_Delta, B_real, B_imag):
            Lr = -jnp.exp(log_real)
            Li = imag
            Delta = jnp.exp(log_Delta)
            ad = Lr * Delta
            bd = Li * Delta
            exp_ad = jnp.exp(ad)
            Lbar_r = exp_ad * jnp.cos(bd)
            Lbar_i = exp_ad * jnp.sin(bd)
            denom = jnp.maximum(Lr * Lr + Li * Li, 1e-12)
            inv_Lr = Lr / denom
            inv_Li = -Li / denom
            diff_r = Lbar_r - 1.0
            diff_i = Lbar_i
            coeff_r = inv_Lr * diff_r - inv_Li * diff_i
            coeff_i = inv_Lr * diff_i + inv_Li * diff_r
            B_bar_r = coeff_r[:, None] * B_real - coeff_i[:, None] * B_imag
            B_bar_i = coeff_r[:, None] * B_imag + coeff_i[:, None] * B_real
            return (Lbar_r, Lbar_i, B_bar_r, B_bar_i)

        def binop(ei, ej):
            Ar_i, Ai_i, xr_i, xi_i = ei
            Ar_j, Ai_j, xr_j, xi_j = ej
            return (Ar_j * Ar_i - Ai_j * Ai_i, Ar_j * Ai_i + Ai_j * Ar_i, Ar_j * xr_i - Ai_j * xi_i + xr_j, Ar_j * xi_i + Ai_j * xr_i + xi_j)

        def apply_ssm(Lbar_r, Lbar_i, B_bar_r, B_bar_i, C_real, C_imag, D, x):
            Bu_r = jnp.einsum('blh,ph->blp', x, B_bar_r)
            Bu_i = jnp.einsum('blh,ph->blp', x, B_bar_i)
            A_r = jnp.broadcast_to(Lbar_r, Bu_r.shape)
            A_i = jnp.broadcast_to(Lbar_i, Bu_i.shape)
            _, _, xs_r, xs_i = jax.lax.associative_scan(binop, (A_r, A_i, Bu_r, Bu_i), axis=1)
            ys = jnp.einsum('blp,hp->blh', xs_r, C_real) - jnp.einsum('blp,hp->blh', xs_i, C_imag)
            return ys + D * x

        def s5(log_real, imag, log_Delta, B_real, B_imag, C_real, C_imag, D, x):
            Lbar_r, Lbar_i, B_bar_r, B_bar_i = discretize(log_real, imag, log_Delta, B_real, B_imag)
            y = apply_ssm(Lbar_r, Lbar_i, B_bar_r, B_bar_i, C_real, C_imag, D, x)
            return jax.nn.gelu(y, approximate=False)
        x_flip = jnp.flip(x, axis=1)
        y_f = s5(fwd_log_real, fwd_imag, fwd_log_Delta, fwd_B_real, fwd_B_imag, fwd_C_real, fwd_C_imag, fwd_D, x)
        y_b = s5(bwd_log_real, bwd_imag, bwd_log_Delta, bwd_B_real, bwd_B_imag, bwd_C_real, bwd_C_imag, bwd_D, x_flip)
        return y_f + jnp.flip(y_b, axis=1)

    def _L0_ffn_ref(x, W1, b1, Wg, bg, Wd, bd):
        import jax, jax.numpy as jnp
        import numpy as np
        C = 64
        HID = 256
        E = 8
        TEMP = 1.0
        orig_shape = x.shape
        xf = x.reshape(-1, orig_shape[-1])
        H = jax.nn.gelu(xf @ W1 + b1, approximate=False)
        probs = jax.nn.softmax((H @ Wg + bg) / TEMP, axis=-1)
        assign = jnp.argmax(probs, axis=-1)
        out = jnp.zeros_like(xf)
        for e in range(Wd.shape[0]):
            y = H @ Wd[e] + bd[e]
            sel = (assign == e)[:, None]
            out = out + jnp.where(sel, probs[:, e:e + 1] * y, 0.0)
        return out.reshape(orig_shape)
    h = _L0_tok_ref(x, L0_tok_conv1_w, L0_tok_conv1_b, L0_tok_bn_gamma, L0_tok_bn_beta, L0_tok_bn_mean, L0_tok_bn_var, L0_tok_conv2_w, L0_tok_conv2_b)
    h = jnp.concatenate([jnp.broadcast_to(cls_tok, (h.shape[0], 1, h.shape[2])), h], axis=1)
    h = h + _L0_attn_ref(_layernorm(h, axis=-1), L0_attn_fwd_log_real, L0_attn_fwd_imag, L0_attn_fwd_log_Delta, L0_attn_fwd_B_real, L0_attn_fwd_B_imag, L0_attn_fwd_C_real, L0_attn_fwd_C_imag, L0_attn_fwd_D, L0_attn_bwd_log_real, L0_attn_bwd_imag, L0_attn_bwd_log_Delta, L0_attn_bwd_B_real, L0_attn_bwd_B_imag, L0_attn_bwd_C_real, L0_attn_bwd_C_imag, L0_attn_bwd_D)
    h = h + _L0_ffn_ref(_layernorm(h, axis=-1), L0_ffn_W1, L0_ffn_b1, L0_ffn_Wg, L0_ffn_bg, L0_ffn_Wd, L0_ffn_bd)
    return h

_drawn_inputs = setup_inputs


def setup_inputs(seed=0):
    import zlib

    import numpy as np

    out = dict(_drawn_inputs(seed))
    spreads = {'L0_tok_conv1_b': (0.0, 0.1),
     'L0_tok_bn_gamma': (1.0, 0.2),
     'L0_tok_bn_beta': (0.0, 0.1),
     'L0_tok_bn_mean': (0.0, 0.1),
     'L0_tok_bn_var': (1.0, 0.2),
     'L0_tok_conv2_b': (0.0, 0.1),
     'L0_attn_fwd_log_Delta': (0.0, 0.441),
     'L0_attn_fwd_D': (1.0, 0.2),
     'L0_attn_bwd_log_Delta': (0.0, 0.388),
     'L0_attn_bwd_D': (1.0, 0.2),
     'L0_ffn_b1': (0.0, 0.8),
     'L0_ffn_bg': (0.0, 0.8),
     'L0_ffn_bd': (0.0, 0.8)}
    factors = {'cls_tok': 200.0, 'L0_ffn_W1': 8.0, 'L0_ffn_Wg': 8.0, 'L0_ffn_Wd': 8.0}
    for name, (base, spread) in spreads.items():
        noise = np.random.default_rng([zlib.crc32(name.encode()), seed]).standard_normal(out[name].shape)
        drawn = base * np.exp(spread * noise) if base else spread * noise
        out[name] = jnp.asarray(drawn.astype(out[name].dtype))
    for name, factor in factors.items():
        out[name] = (out[name] * factor).astype(out[name].dtype)
    return out
```

```python
from contextlib import ExitStack

import numpy as np
import concourse.bass as bass
from concourse import mybir

ALU = mybir.AluOpType
ACT = mybir.ActivationFunctionType
AX = mybir.AxisListType
F32 = mybir.dt.float32
BF16 = mybir.dt.bfloat16

B, C, HW = 4, 64, 64
CR, TAPS = 16, 9
F = HW
NS = 64
HID, EX = 256, 8
PAIRS = C * HW // 2
CH = 512
NCH = B * PAIRS // CH
QUADS = PAIRS // 2
GRP = 4
PROW = (HW + 2) * HW
BN_EPS = LN_EPS = 1e-5
FWD, BWD = 0, 1


class Tower:

    def __init__(self, nc, ctx, arrays, out):
        (self.x, self.cls_tok, self.conv1_w, self.conv1_b, self.bn_gamma, self.bn_beta, self.bn_mean, self.bn_var,
         self.conv2_w, self.conv2_b) = arrays[:10]
        self.ssm_f, self.ssm_b = arrays[10:18], arrays[18:26]
        self.W1, self.b1, self.Wg, self.bg, self.Wd, self.bd = arrays[26:]
        self.out = out

        def sb(name, shape, dt=F32):
            return ctx.enter_context(nc.sbuf_tensor(name, shape, dt))

        self.img = sb("img", [128, 2, PROW])
        self.hT = sb("hT", [128, B * QUADS, 2])
        self.uT = sb("uT", [128, B * QUADS, 2])
        self.hC = sb("hC", [128, B])
        self.uC = sb("uC", [128, B])
        self.ident = sb("ident", [128, 128])
        self.ones = sb("ones", [128, 128])
        self.center = sb("center", [128, 128])
        self.mean2 = sb("mean2", [128, 2])
        self.conv1L = sb("conv1L", [128, 2 * CR])
        self.conv2L = sb("conv2L", [2 * CR + 1, TAPS, 128])
        self.ysc = sb("ysc", [2 * CR, 8])
        self.eps = sb("eps", [128, 2])
        self.var = sb("var", [128, NCH * 8 + 2])
        self.rstd = sb("rstd", [128, NCH * 8 + 2])
        self.nwt = sb("nwt", [128, NCH * 8 + 2])
        self.LV = sb("LV", [128, 12, 128])
        self.N1 = sb("N1", [128, 2, 5, F])
        self.N2 = sb("N2", [128, 2, 5, F])
        self.KI = sb("KI", [128, 2, 2, 2, F])
        self.decay = sb("decay", [128, 2])
        self.turn = sb("turn", [128, 10, 2, 2])
        self.tab = sb("tab", [128, 2, 2, QUADS])
        self.W1z = sb("W1z", [128, 2, HID])
        self.b1c = sb("b1c", [128, 2])
        self.WgT = sb("WgT", [128, 2, EX])
        self.WdT = sb("WdT", [128, 2, EX, F])
        self.bias3 = sb("bias3", [3, EX * F + EX], BF16)
        self.ones3 = sb("ones3", [3, 128], BF16)
        self.rank = sb("rank", [128, EX])


def vit_tower(nc, arrays, out):
    with ExitStack() as ctx:
        g = Tower(nc, ctx, arrays, out)
        setup(nc, g)
        involution(nc, g)
        layer_norm(nc, g, "1")
        state_space(nc, g)
        layer_norm(nc, g, "2")
        experts(nc, g)


def setup(nc, g):
    with ExitStack() as ctx:
        def sb(name, shape, dt=F32):
            return ctx.enter_context(nc.sbuf_tensor("s0_" + name, shape, dt))

        def ps(name, shape):
            return ctx.enter_context(nc.psum_tensor("p0_" + name, shape, F32))

        def sem(name):
            return ctx.enter_context(nc.semaphore("s0_" + name))

        raw = sb("raw", [128, 2, 3])
        Bm = sb("Bm", [128, 2, 2, F])
        Cin = sb("Cin", [F, 2, 3, NS])
        Dv = sb("Dv", [128, 2])
        S = sb("S", [128, 40, 2])
        M = sb("M", [128, 2, 2, 6, F])
        M0 = sb("M0", [128, 2, 2, F])
        K0 = sb("K0", [128, 2, F])
        tmp = sb("tmp", [128, 2, F])
        sgn = sb("sgn", [128, 1])
        w2 = sb("w2", [2 * CR + 1, TAPS])
        mask2 = sb("mask2", [2 * CR + 1, 128])
        bfull = sb("bfull", [3, EX * F + EX])
        bpart = sb("bpart", [3, 3, EX * F + EX], BF16)
        brest = sb("brest", [3, 2, EX * F + EX])
        bsel = sb("bsel", [3, EX * F + EX])
        pT = [ps(f"T{i}", [128, 4, 128]) for i in range(3)]
        pC = ps("C", [128, 4, F])
        pK = ps("K", [128, 2, 4, F])

        img_in = sem("img_in")
        ssm_in = sem("ssm_in")
        conv_in = sem("conv_in")
        ffn_in = sem("ffn_in")
        zeroed = sem("zeroed")
        pool_const = sem("pool_const")
        dve = sem("dve")
        exped = sem("exped")
        sined = sem("sined")
        c_turned = sem("c_turned")
        m_turned = sem("m_turned")
        k_made = sem("k_made")
        consts = {}
        img, hT, uT = g.img, g.hT, g.uT

        with nc.Block() as block:
            vec = nc.vector
            steps = [0]

            def count(name):
                consts[name] = steps[0]

            @block.vector
            def _(v):
                def link(ins):
                    steps[0] += 1
                    ins.then_inc(dve, 1)
                    v.wait_ge(dve, steps[0])

                def tt(o, a, b, op):
                    link(vec.tensor_tensor(o, a, b, op))

                def ts(o, a, s1, s2, op0, op1=ALU.bypass):
                    link(vec.tensor_scalar(o, a, s1, s2, op0, op1) if s2 is not None
                         else vec.tensor_scalar(o, a, s1, None, op0))

                def stt(o, a, s, b, op0, op1):
                    link(vec.scalar_tensor_tensor(out=o, in0=a, scalar=s, in1=b, op0=op0, op1=op1))

                def copy(o, a):
                    link(vec.tensor_copy(o, a))

                def fill(o, c):
                    link(vec.memset(o, c))

                v.wait_ge(ssm_in, 16 * 30)
                fill(g.ones[:], 1.0)
                fill(g.eps[:], LN_EPS)
                fill(sgn[0:64], 1.0)
                fill(sgn[64:128], -1.0)
                fill(g.ones3[:], 1.0)
                fill(g.mean2[:], 0.0)
                fill(g.mean2[0:64, 0:1], 1.0 / F)
                fill(g.mean2[64:128, 1:2], 1.0 / F)
                fill(g.var[:], 1.0)
                fill(M[:, :, :, 5, :], 0.0)
                fill(g.KI[:], 0.0)
                v.wait_ge(pool_const, 8)
                copy(g.center[:], g.ident[:])
                for h in range(2):
                    s = slice(64 * h, 64 * h + 64)
                    ts(g.center[s, s], g.ident[s, s], -1.0 / F, None, ALU.add)
                s = lambda n: S[:, n, :]
                v.wait_ge(exped, 2)
                stt(s(2), s(0), -1.0, s(1), ALU.mult, ALU.mult)
                count("ad")
                tt(s(3), raw[:, :, 1], s(1), ALU.mult)
                magic = 1.5 * 2.0 ** 23
                ts(s(5), s(3), 1.0 / (2 * np.pi), magic, ALU.mult, ALU.add)
                ts(s(6), s(5), -magic, None, ALU.add)
                p1 = 6.28125
                p2 = float(np.float32(2 * np.pi - p1))
                p3 = float(2 * np.pi - p1 - p2)
                stt(s(7), s(6), -p1, s(3), ALU.mult, ALU.add)
                stt(s(7), s(6), -p2, s(7), ALU.mult, ALU.add)
                stt(s(7), s(6), -p3, s(7), ALU.mult, ALU.add)
                edge = float(np.nextafter(np.float32(np.pi), np.float32(0)))
                ts(s(7), s(7), edge, -edge, ALU.min, ALU.max)
                count("angle")
                v.wait_ge(exped, 3)
                v.wait_ge(sined, 2)
                tt(s(10), s(9), s(9), ALU.mult)
                ts(s(10), s(10), -2.0, 1.0, ALU.mult, ALU.add)
                tt(s(11), s(4), s(10), ALU.mult)
                tt(s(12), s(4), s(8), ALU.mult)
                ts(s(13), s(0), -1.0, None, ALU.mult)
                tt(s(14), s(13), s(13), ALU.mult)
                tt(s(15), raw[:, :, 1], raw[:, :, 1], ALU.mult)
                tt(s(14), s(14), s(15), ALU.add)
                ts(s(14), s(14), 1e-12, None, ALU.max)
                link(vec.reciprocal(s(15), s(14)))
                tt(s(16), s(13), s(15), ALU.mult)
                stt(s(17), raw[:, :, 1], -1.0, s(15), ALU.mult, ALU.mult)
                ts(s(18), s(11), -1.0, None, ALU.add)
                tt(s(19), s(16), s(18), ALU.mult)
                tt(s(20), s(17), s(12), ALU.mult)
                tt(s(19), s(19), s(20), ALU.subtract)
                tt(s(20), s(16), s(12), ALU.mult)
                tt(s(21), s(17), s(18), ALU.mult)
                tt(s(20), s(20), s(21), ALU.add)
                tt(s(21), s(4), s(4), ALU.mult)
                tt(g.decay[:], s(21), s(21), ALU.mult)

                def square(co, so, c, sn):
                    tt(s(30), c, c, ALU.mult)
                    tt(s(31), sn, sn, ALU.mult)
                    tt(s(32), c, sn, ALU.mult)
                    tt(s(33), s(30), s(31), ALU.subtract)
                    tt(s(34), s(30), s(31), ALU.add)
                    ts(s(34), s(34), -1.0, 2.0, ALU.mult, ALU.add)
                    tt(co, s(33), s(34), ALU.mult)
                    stt(so, s(32), 2.0, s(34), ALU.mult, ALU.mult)

                square(s(22), s(23), s(10), s(8))
                square(g.turn[:, 0, 0, :], g.turn[:, 0, 1, :], s(22), s(23))
                for k in range(9):
                    square(g.turn[:, k + 1, 0, :], g.turn[:, k + 1, 1, :], g.turn[:, k, 0, :], g.turn[:, k, 1, :])

                for d in range(2):
                    ts(Bm[64:128, d, 1, :], Bm[64:128, d, 1, :], -1.0, None, ALU.mult)
                    col = lambda n: S[:, n, d:d + 1]
                    slot = (lambda e: 4 - e) if d == FWD else (lambda e: e)
                    at = lambda n, e: M[:, d, n, slot(e), :]

                    def times(o1, o2, a1, a2, cr, ci):
                        ts(tmp[:, 0, :], a2, ci, None, ALU.mult)
                        ts(tmp[:, 1, :], a1, ci, None, ALU.mult)
                        stt(o1, a1, cr, tmp[:, 0, :], ALU.mult, ALU.subtract)
                        stt(o2, a2, cr, tmp[:, 1, :], ALU.mult, ALU.add)

                    times(at(0, 0), at(1, 0), Bm[:, d, 0, :], Bm[:, d, 1, :], col(19), col(20))
                    for e in range(4):
                        times(at(0, e + 1), at(1, e + 1), at(0, e), at(1, e), col(11), col(12))
                    copy(M0[:, d, 0, :], at(0, 0))
                    copy(M0[:, d, 1, :], at(0, 0))
                count("M")
                v.wait_ge(c_turned, 1)
                for d in range(2):
                    col = lambda n: S[:, n, d:d + 1]
                    slot = (lambda k: k) if d == FWD else (lambda k: 4 - k)
                    n1 = lambda k: g.N1[:, d, slot(k), :]
                    n2 = lambda k: g.N2[:, d, slot(k), :]
                    ts(n1(0), pC[:, 2 * d, :], sgn[:, 0:1], None, ALU.mult)
                    ts(n2(0), pC[:, 2 * d + 1, :], -1.0, None, ALU.mult)
                    for k in range(4):
                        ts(tmp[:, 0, :], n2(k), col(12), None, ALU.mult)
                        ts(tmp[:, 1, :], n1(k), col(12), None, ALU.mult)
                        stt(n1(k + 1), n1(k), col(11), tmp[:, 0, :], ALU.mult, ALU.add)
                        stt(n2(k + 1), n2(k), col(11), tmp[:, 1, :], ALU.mult, ALU.subtract)
                count("N")
                v.wait_ge(conv_in, 16 * 15)
                cb, ga, be, mu, va = (g.ysc[:, n:n + 1] for n in range(5))
                ts(g.ysc[:, 5:6], va, BN_EPS, None, ALU.add)
                count("bnvar")
                v.wait_ge(sined, 3)
                link(vec.reciprocal(g.ysc[:, 7:8], g.ysc[:, 6:7]))
                tt(g.ysc[:, 6:7], ga, g.ysc[:, 7:8], ALU.mult)
                tt(g.ysc[:, 7:8], cb, mu, ALU.subtract)
                stt(g.ysc[:, 7:8], g.ysc[:, 7:8], g.ysc[:, 6:7], be, ALU.mult, ALU.add)
                tt(g.conv2L[:], w2[:, :].unsqueeze(2).broadcast_to([2 * CR + 1, TAPS, 128]),
                   mask2[:, :].unsqueeze(1).broadcast_to([2 * CR + 1, TAPS, 128]), ALU.mult)
                v.wait_ge(m_turned, 1)
                for n in range(3):
                    k = 4 if n < 2 else 3
                    copy(g.LV[:, 4 * n:4 * n + k, :], pT[n][:, 0:k, :])
                v.wait_ge(k_made, 1)
                for d in range(2):
                    kk = (lambda k: pK[:, FWD, k, :]) if d == FWD else (lambda k: pK[:, BWD, 3 - k, :])
                    for h in range(2):
                        r = slice(64 * h, 64 * h + 64)
                        stt(K0[r, d, :], g.ident[r, r], Dv[r, d:d + 1], kk(0)[r], ALU.mult, ALU.add)
                    lo, hi = slice(0, 64), slice(64, 128)
                    if d == FWD:
                        plan = [(lo, 0, 0, 0), (lo, 0, 1, 1), (hi, 0, 1, 0), (lo, 1, 0, 2), (lo, 1, 1, 3), (hi, 1, 0, 1), (hi, 1, 1, 2)]
                    else:
                        plan = [(lo, 0, 0, 0), (hi, 0, 0, 1), (hi, 0, 1, 0), (lo, 1, 0, 2), (lo, 1, 1, 1), (hi, 1, 0, 3), (hi, 1, 1, 2)]
                    for r, which, j, k in plan:
                        copy(g.KI[r, d, which, j, :], K0[r, d, :] if k == 0 else kk(k)[r])
                v.wait_ge(ffn_in, 16 * 13)
                for col in range(1, B):
                    copy(g.hC[0:F, col:col + 1], g.hC[0:F, 0:1])
                copy(bpart[:, 0, :], bfull[:])
                tt(brest[:, 0, :], bfull[:], bpart[:, 0, :], ALU.subtract)
                copy(bpart[:, 1, :], brest[:, 0, :])
                tt(brest[:, 1, :], brest[:, 0, :], bpart[:, 1, :], ALU.subtract)
                copy(bpart[:, 2, :], brest[:, 1, :])
                ts(bsel[:], bpart[:, 0, :], g.ident[0:3, 0:1], None, ALU.mult)
                stt(bsel[:], bpart[:, 1, :], g.ident[0:3, 1:2], bsel[:], ALU.mult, ALU.add)
                stt(g.bias3[:], bpart[:, 2, :], g.ident[0:3, 2:3], bsel[:], ALU.mult, ALU.add)

            @block.sync
            def _(sp):
                dirs = (g.ssm_f, g.ssm_b)
                for d, (lr, im, ld, Br, Bi, Cr, Ci, D) in enumerate(dirs):
                    for half in (slice(0, 64), slice(64, 128)):
                        for n, v in enumerate((lr, im, ld)):
                            sp.dma_start(raw[half, d, n:n + 1], v.rearrange("(p a) -> p a", a=1)).then_inc(ssm_in, 16)
                        sp.dma_start(Dv[half, d:d + 1], D.rearrange("(p a) -> p a", a=1)).then_inc(ssm_in, 16)
                    sp.dma_start(Bm[0:64, d, 0, :], Br).then_inc(ssm_in, 16)
                    sp.dma_start(Bm[64:128, d, 0, :], Bi).then_inc(ssm_in, 16)
                    sp.dma_start(Bm[0:64, d, 1, :], Bi).then_inc(ssm_in, 16)
                    sp.dma_start(Bm[64:128, d, 1, :], Br).then_inc(ssm_in, 16)
                    sp.dma_start(Cin[:, d, 0, :], Cr).then_inc(ssm_in, 16)
                    sp.dma_start(Cin[:, d, 1, :], Ci).then_inc(ssm_in, 16)
                    sp.dma_start(Cin[:, d, 2, :], Cr).then_inc(ssm_in, 16)
                for bp in range(2):
                    sp.dma_start(img[:, bp, HW:HW + HW * HW],
                                 g.x[2 * bp:2 * bp + 2].rearrange("b c h w -> (b c) (h w)")).then_inc(img_in, 16)
                sp.wait_ge(img_in, 32)

            @block.gpsimd
            def _(pool):
                nc.gpsimd.memset(g.conv1L[:], 0.0).then_inc(zeroed, 1)
                nc.gpsimd.memset(g.W1z[:], 0.0).then_inc(zeroed, 1)
                nc.gpsimd.memset(g.hC[:], 0.0).then_inc(zeroed, 1)
                nc.gpsimd.memset(g.ident[:], 0.0).then_inc(pool_const, 1)
                nc.gpsimd.memset(mask2[:], 1.0).then_inc(pool_const, 1)
                pool.wait_ge(pool_const, 2)
                nc.gpsimd.affine_select(out=g.ident[:], in_=g.ident[:], compare_op=ALU.not_equal, fill=1.0,
                                        base=0, pattern=[[-1, 128]], channel_multiplier=1).then_inc(pool_const, 1)
                m_even, m_odd = mask2[0:2 * CR, 0:C], mask2[0:2 * CR, C:2 * C]
                nc.gpsimd.affine_select(out=m_even, in_=m_even, compare_op=ALU.is_ge, fill=0.0, base=CR - 1,
                                        pattern=[[0, C]], channel_multiplier=-1).then_inc(pool_const, 1)
                nc.gpsimd.affine_select(out=m_odd, in_=m_odd, compare_op=ALU.is_ge, fill=0.0, base=-CR,
                                        pattern=[[0, C]], channel_multiplier=1).then_inc(pool_const, 1)
                nc.gpsimd.iota(g.rank[:], pattern=[[-1, EX]], base=EX, channel_multiplier=0,
                               allow_small_or_imprecise_dtypes=True).then_inc(pool_const, 1)
                for bp in range(2):
                    nc.gpsimd.memset(img[:, bp, 0:HW], 0.0)
                    nc.gpsimd.memset(img[:, bp, PROW - HW:PROW], 0.0).then_inc(pool_const, 1)

            @block.scalar
            def _(act):
                act.wait_ge(zeroed, 3)
                for b2 in range(2):
                    act.dma_start(g.conv1L[C * b2:C * b2 + C, CR * b2:CR * b2 + CR],
                                  g.conv1_w.rearrange("o c -> c o"), allow_slow_non_contiguous=True).then_inc(conv_in, 16)
                    act.dma_start(w2[CR * b2:CR * b2 + CR, :], g.conv2_w.rearrange("k o -> o k"), allow_slow_non_contiguous=True).then_inc(conv_in, 16)
                    for n, v in enumerate((g.conv1_b, g.bn_gamma, g.bn_beta, g.bn_mean, g.bn_var)):
                        act.dma_start(g.ysc[CR * b2:CR * b2 + CR, n:n + 1],
                                      v.rearrange("(p a) -> p a", a=1)).then_inc(conv_in, 16)
                act.dma_start(w2[2 * CR:2 * CR + 1, :], g.conv2_b.rearrange("(a k) -> a k", a=1)).then_inc(conv_in, 16)
                act.wait_ge(ssm_in, 16 * 30)
                nc.scalar.activation(S[:, 0, :], raw[:, :, 0], ACT.Exp).then_inc(exped, 1)
                nc.scalar.activation(S[:, 1, :], raw[:, :, 2], ACT.Exp).then_inc(exped, 1)
                act.wait_ge(dve, consts["ad"])
                nc.scalar.activation(S[:, 4, :], S[:, 2, :], ACT.Exp).then_inc(exped, 1)
                act.wait_ge(dve, consts["angle"])
                nc.scalar.activation(S[:, 8, :], S[:, 7, :], ACT.Sin).then_inc(sined, 1)
                nc.scalar.activation(S[:, 9, :], S[:, 7, :], ACT.Sin, scale=0.5).then_inc(sined, 1)
                act.wait_ge(dve, consts["bnvar"])
                nc.scalar.activation(g.ysc[:, 6:7], g.ysc[:, 5:6], ACT.Sqrt).then_inc(sined, 1)
                act.wait_ge(zeroed, 3)
                for par in range(2):
                    act.dma_start(g.W1z[F * par:F * par + F, par, :], g.W1).then_inc(ffn_in, 16)
                act.dma_start(g.hC[0:F, 0:1], g.cls_tok.rearrange("a b f -> f (a b)")).then_inc(ffn_in, 16)
                act.dma_start(g.b1c[:], g.b1.rearrange("(h p) -> p h", p=128), allow_slow_non_contiguous=True).then_inc(ffn_in, 16)
                act.dma_start(g.WgT[:], g.Wg.rearrange("(h p) e -> p h e", p=128)).then_inc(ffn_in, 16)
                for h in range(2):
                    act.dma_start(g.WdT[:, h], g.Wd[:, 128 * h:128 * h + 128, :].rearrange("e p f -> p e f")).then_inc(ffn_in, 16)
                for r in range(3):
                    act.dma_start(bfull[r:r + 1, 0:EX * F], g.bd.rearrange("(a e) f -> a (e f)", a=1)).then_inc(ffn_in, 16)
                    act.dma_start(bfull[r:r + 1, EX * F:], g.bg.rearrange("(a e) -> a e", a=1)).then_inc(ffn_in, 16)
                act.wait_ge(ffn_in, 16 * 13)

            @block.tensor
            def _(pe):
                pe.wait_ge(ssm_in, 16 * 30)
                pe.wait_ge(pool_const, 3)
                for d in range(2):
                    nc.tensor.transpose(pC[:, 2 * d, :], Cin[:, d, 0:2, :], g.ident[0:F, 0:F])
                    last = nc.tensor.transpose(pC[:, 2 * d + 1, :], Cin[:, d, 1:3, :], g.ident[0:F, 0:F])
                last.then_inc(c_turned, 1)
                pe.wait_ge(dve, consts["M"])
                for n, (d, which, slot) in enumerate(LV_PLAN):
                    last = nc.tensor.transpose(pT[n // 4][:, n % 4, :], M[:, d, which, slot:slot + 2, :], g.ident[:])
                last.then_inc(m_turned, 1)
                pe.wait_ge(dve, consts["N"])
                for d in range(2):
                    first = 0 if d == FWD else 1
                    last = nc.tensor.matmul(pK[:, d, :, :], M0[:, d, :, :], g.N1[:, d, first:first + 4, :],
                                            start=(d == 0), stop=(d == 1), skip_group_check=True)
                last.then_inc(k_made, 1)


LV_PLAN = [(FWD, 0, 1), (FWD, 0, 3), (FWD, 1, 1), (FWD, 1, 3),
           (BWD, 0, 0), (BWD, 0, 2), (BWD, 1, 0), (BWD, 1, 2),
           (FWD, 0, 0), (FWD, 1, 0), (FWD, 0, 4)]
LV_CARRY, LV_CARRY_TURNED, LV_FIRST = 8, 9, 10



def involution(nc, g):
    CPI = HW * HW // CH
    ROWS = CH // HW
    NW = 3
    with ExitStack() as ctx:
        def sem(name):
            return ctx.enter_context(nc.semaphore("inv_" + name))

        prod = ctx.enter_context(nc.sbuf_tensor("inv_prod", [128, TAPS, ROWS, HW], F32))
        ysb = ctx.enter_context(nc.sbuf_tensor("inv_ysb", [2 * CR + 1, CH], F32))
        pY = ctx.enter_context(nc.psum_tensor("inv_pY", [2 * CR, CH], F32))
        pW = [ctx.enter_context(nc.psum_tensor(f"inv_pW{n}", [128, ROWS, HW], F32)) for n in range(NW)]
        pS = ctx.enter_context(nc.psum_tensor("inv_pS", [128, CH], F32))
        turned = ctx.enter_context(nc.sbuf_tensor("inv_turned", [128, 2, 2, 2, QUADS // 2], F32))
        doubled = sem("doubled")
        multiplied = sem("multiplied")
        reduced = sem("reduced")
        relued = sem("relued")
        weighed = sem("weighed")
        filtered = sem("filtered")
        added = sem("added")
        moved = sem("moved")
        edged = sem("edged")
        onesrow = sem("onesrow")

        def tap(k):
            dh, dw = k // 3 - 1, k % 3 - 1
            lo, hi = max(0, -dw), HW - max(0, dw)
            return dh, dw, lo, hi

        def starts(bp, hc):
            return bp == 0 and isinstance(hc, int) and hc == 0

        with nc.Block() as block:
            @block.tensor
            def _(pe):
                def reduce(bp, hc):
                    n = bp * CPI + hc
                    pe.wait_ge(relued, n)
                    nc.tensor.matmul(pY[:], g.conv1L[:], g.img[:, bp, bass.ds(HW + hc * CH, CH)],
                                     start=True, stop=True).then_inc(reduced, 1)

                def weigh(bp, hc, k):
                    n = bp * CPI + hc
                    if k == 0:
                        pe.wait_ge(relued, n + 1)
                    if k >= NW or not starts(bp, hc):
                        pe.wait_ge(filtered, n * TAPS + k - NW + 1)
                    nc.tensor.matmul(pW[k % NW][:], g.conv2L[:, k, :], ysb[:], start=True, stop=True).then_inc(weighed, 1)

                def body(bp, hc, more):
                    n = bp * CPI + hc
                    for k in range(TAPS):
                        if k == 0 and more:
                            reduce(bp, hc + 1)
                        pe.wait_ge(filtered, n * TAPS + k + 1)
                        if k == 0:
                            pe.wait_ge(moved, n)
                        for j in range(4):
                            last = nc.tensor.matmul(pS[:, 128 * j:128 * j + 128], prod[:, k, 2 * j:2 * j + 2, :], g.ident[:],
                                                    is_transpose=True, start=(k == 0 and j == 0),
                                                    stop=(k == TAPS - 1 and j == 3))
                        last.then_inc(added, 1)
                        if k + NW < TAPS:
                            weigh(bp, hc, k + NW)
                        elif more:
                            weigh(bp, hc + 1, k + NW - TAPS)

                for bp in range(2):
                    reduce(bp, 0)
                    for k in range(NW):
                        weigh(bp, 0, k)
                    body(bp, 0, True)
                    with pe.Fori(1, CPI - 1) as hc:
                        body(bp, hc, True)
                    body(bp, CPI - 1, False)

            @block.scalar
            def _(act):
                act.wait_ge(onesrow, 1)

                def relu(bp, hc):
                    n = bp * CPI + hc
                    act.wait_ge(reduced, n + 1)
                    act.wait_ge(weighed, n * TAPS)
                    nc.scalar.activation(ysb[0:2 * CR, :], pY[:], ACT.Relu, bias=g.ysc[:, 7:8],
                                         scale=g.ysc[:, 6:7]).then_inc(relued, 1)

                def body(bp, hc, more):
                    n = bp * CPI + hc
                    if more:
                        relu(bp, hc + 1)
                    act.wait_ge(added, (n + 1) * TAPS)
                    src = pS[:].rearrange("p (j b c) -> p b c j", j=4, b=2)
                    dst = g.hT[:].rearrange("p (b c h) r -> p b c (h r)", b=B, c=C)
                    nc.scalar.copy(dst[:, 2 * bp:2 * bp + 2, :, bass.ds(4 * hc, 4)], src).then_inc(moved, 1)

                for bp in range(2):
                    relu(bp, 0)
                    body(bp, 0, True)
                    with act.Fori(1, CPI - 1) as hc:
                        body(bp, hc, True)
                    body(bp, CPI - 1, False)

            @block.vector
            def _(v):
                for k in range(TAPS):
                    _, dw, lo, hi = tap(k)
                    if dw:
                        edge = prod[:, k, :, 0:1] if dw < 0 else prod[:, k, :, HW - 1:HW]
                        nc.vector.memset(edge, 0.0)
                nc.vector.memset(ysb[2 * CR:2 * CR + 1, :], 1.0).then_inc(onesrow, 1)

                def body(bp, hc, more):
                    n = bp * CPI + hc
                    for k in range(TAPS):
                        dh, dw, lo, hi = tap(k)
                        v.wait_ge(weighed, n * TAPS + k + 1)
                        if not starts(bp, hc):
                            v.wait_ge(added, (n - 1) * TAPS + k + 1)
                        rows = g.img[:, bp, bass.ds(hc * CH + (1 + dh) * HW, CH)].rearrange("p (r w) -> p r w", w=HW)
                        nc.vector.tensor_tensor(prod[:, k, :, lo:hi], pW[k % NW][:, :, lo:hi],
                                                rows[:, :, lo + dw:hi + dw], ALU.mult).then_inc(filtered, 1)

                body(0, 0, True)
                with v.Fori(1, CPI) as hc:
                    body(0, hc, True)
                with v.Fori(0, CPI) as hc:
                    body(1, hc, True)

            @block.gpsimd
            def _(pool):
                nc.gpsimd.memset(g.tab[:, :, 0, 0:1], 1.0)
                nc.gpsimd.memset(g.tab[:, :, 1, 0:1], 0.0).then_inc(doubled, 1)
                for k in range(QUADS.bit_length() - 1):
                    m = 2 ** k
                    for d in range(2):
                        half = [turned[:, d, i, :, 0:m] for i in range(2)]
                        for i in range(2):
                            pool.wait_ge(doubled, 3 * k + 1)
                            nc.gpsimd.tensor_scalar(half[i], g.tab[:, d, :, 0:m], g.turn[:, k, i, d:d + 1], None,
                                                    ALU.mult).then_inc(multiplied, 1)
                        pool.wait_ge(multiplied, 4 * k + 2 * d + 2)
                        nc.gpsimd.tensor_tensor(g.tab[:, d, 0, m:2 * m], half[0][:, 0], half[1][:, 1], ALU.subtract)
                        nc.gpsimd.tensor_tensor(g.tab[:, d, 1, m:2 * m], half[0][:, 1], half[1][:, 0],
                                                ALU.add).then_inc(doubled, 1 + d)


def layer_norm(nc, g, which):
    with ExitStack() as ctx:
        def sem(name):
            return ctx.enter_context(nc.semaphore(f"ln{which}_{name}"))

        sq = [ctx.enter_context(nc.sbuf_tensor(f"ln{which}_sq{n}", [128, CH], F32)) for n in range(2)]
        st = [ctx.enter_context(nc.sbuf_tensor(f"ln{which}_st{n}", [128, 4, 2 * F], F32)) for n in range(2)]
        wide = [ctx.enter_context(nc.sbuf_tensor(f"ln{which}_w{n}", [128, 8], F32)) for n in range(2)]
        pCn = [ctx.enter_context(nc.psum_tensor(f"ln{which}_c{n}", [128, CH], F32)) for n in range(2)]
        pV = [ctx.enter_context(nc.psum_tensor(f"ln{which}_v{n}", [128, 8], F32)) for n in range(2)]
        pR = [ctx.enter_context(nc.psum_tensor(f"ln{which}_r{n}", [128, CH], F32)) for n in range(2)]
        pX = ctx.enter_context(nc.psum_tensor(f"ln{which}_x", [128, 16], F32))
        centered = sem("centered")
        squared = sem("squared")
        summed = sem("summed")
        kept = sem("kept")
        cls_c, cls_s, cls_v, cls_r, cls_t = (sem(n) for n in ("cls_c", "cls_s", "cls_v", "cls_r", "cls_t"))
        rooted = sem("rooted")
        dv = sem("dv")
        picked = sem("picked")
        spread = sem("spread")
        scaled = sem("scaled")
        h2 = g.hT[:].rearrange("p (n a) r -> p n (a r)", n=NCH)
        u2 = g.uT[:].rearrange("p (n a) r -> p n (a r)", n=NCH)
        hflat = g.hT[:].rearrange("p a r -> p (a r)")
        uflat = g.uT[:].rearrange("p a r -> p (a r)")
        NC8 = NCH * 8

        with nc.Block() as block:
            @block.tensor
            def _(pe):
                nc.tensor.matmul(pX[:, 0:B], g.center[:], g.hC[:], start=True, stop=True).then_inc(cls_c, 1)

                def body(i, first):
                    for n in range(2):
                        if not first:
                            pe.wait_ge(squared, 2 * i + n - 1)
                        nc.tensor.matmul(pCn[n][:], g.center[:], hflat[:, bass.ds((2 * i + n) * CH, CH)],
                                         start=True, stop=True).then_inc(centered, 1)
                    for n in range(2):
                        pe.wait_ge(squared, 2 * i + n + 1)
                        if not first:
                            pe.wait_ge(kept, 2 * i + n - 1)
                        for j in range(4):
                            last = nc.tensor.matmul(pV[n][:, 2 * j:2 * j + 2], sq[n][:, 128 * j:128 * j + 128], g.mean2[:],
                                                    start=True, stop=True)
                        last.then_inc(summed, 1)

                body(0, True)
                with pe.Fori(1, NCH // 2) as i:
                    body(i, False)
                pe.wait_ge(cls_s, 1)
                nc.tensor.matmul(pX[0:B, 8:10], sq[0][:, 0:B], g.mean2[:], start=True, stop=True).then_inc(cls_v, 1)
                pe.wait_ge(cls_r, 1)
                nc.tensor.transpose(pX[:, 0:B], sq[1][0:B, 0:128], g.ident[0:B, 0:B]).then_inc(cls_t, 1)

                def apply(i, first):
                    for n in range(2):
                        pe.wait_ge(picked, 2 * i + n + 1)
                        if not first:
                            pe.wait_ge(scaled, 2 * i + n - 1)
                        for j in range(4):
                            last = nc.tensor.transpose(pR[n][:, 128 * j:128 * j + 128], st[n][:, j, :], g.ident[:])
                        last.then_inc(spread, 1)

                apply(0, True)
                with pe.Fori(1, NCH // 2) as i:
                    apply(i, False)

            @block.scalar
            def _(act):
                act.wait_ge(cls_c, 1)
                nc.scalar.copy(g.uC[:], pX[:, 0:B])

                def body(i, first):
                    for n in range(2):
                        act.wait_ge(centered, 2 * i + n + 1)
                        if not first:
                            act.wait_ge(summed, 2 * i + n - 1)
                        nc.scalar.copy(uflat[:, bass.ds((2 * i + n) * CH, CH)], pCn[n][:])
                        nc.scalar.activation(sq[n][:], pCn[n][:], ACT.Square).then_inc(squared, 1)

                body(0, True)
                with act.Fori(1, NCH // 2) as i:
                    body(i, False)
                act.wait_ge(summed, NCH)
                nc.scalar.activation(sq[0][:, 0:B], pX[:, 0:B], ACT.Square).then_inc(cls_s, 1)
                act.wait_ge(dv, 1)
                nc.scalar.activation(g.rstd[:], g.var[:], ACT.Sqrt).then_inc(rooted, 1)
                act.wait_ge(dv, 6)

                def pick(i, first):
                    for n in range(2):
                        if not first:
                            act.wait_ge(spread, 2 * i + n - 1)
                        nc.scalar.copy(st[n][:].rearrange("p j (r f) -> p (j r) f", r=2),
                                       g.rstd[:, bass.ds((2 * i + n) * 8, 8)].unsqueeze(2).broadcast_to([128, 8, F])
                                       ).then_inc(picked, 1)

                pick(0, True)
                with act.Fori(1, NCH // 2) as i:
                    pick(i, False)

            @block.vector
            def _(v):
                def body(i, first):
                    for n in range(2):
                        v.wait_ge(summed, 2 * i + n + 1)
                        nc.vector.tensor_copy(g.var[:, bass.ds((2 * i + n) * 8, 8)], pV[n][:]).then_inc(kept, 1)

                with v.Fori(0, NCH // 2) as i:
                    body(i, False)
                v.wait_ge(cls_v, 1)
                nc.vector.tensor_copy(g.var[0:B, NC8:NC8 + 2], pX[0:B, 8:10]).then_inc(kept, 1)
                v.wait_ge(kept, NCH + 1)
                nc.vector.tensor_scalar(g.var[:], g.var[:], LN_EPS, None, ALU.add).then_inc(dv, 1)
                v.wait_ge(rooted, 1)
                v.wait_ge(dv, 1)
                nc.vector.reciprocal(g.rstd[:], g.rstd[:]).then_inc(dv, 1)
                v.wait_ge(dv, 2)
                nc.vector.tensor_tensor(g.nwt[:], g.rstd[:], g.rstd[:], ALU.mult).then_inc(dv, 1)
                v.wait_ge(dv, 3)
                nc.vector.tensor_tensor(g.nwt[:], g.nwt[:], g.var[:], ALU.mult).then_inc(dv, 1)
                v.wait_ge(dv, 4)
                nc.vector.tensor_scalar(g.nwt[:], g.nwt[:], -0.5, 1.5, ALU.mult, ALU.add).then_inc(dv, 1)
                v.wait_ge(dv, 5)
                nc.vector.tensor_tensor(g.rstd[:], g.rstd[:], g.nwt[:], ALU.mult).then_inc(dv, 1)
                v.wait_ge(dv, 6)
                nc.vector.tensor_copy(sq[1][0:B, 0:128].rearrange("p (r f) -> p r f", r=2),
                                      g.rstd[0:B, NC8:NC8 + 2].unsqueeze(2).broadcast_to([B, 2, F])).then_inc(cls_r, 1)
                v.wait_ge(cls_t, 1)
                nc.vector.tensor_tensor(g.uC[:], pX[:, 0:B], g.uC[:], ALU.mult)

                def apply(i, first):
                    for n in range(2):
                        v.wait_ge(spread, 2 * i + n + 1)
                        u = uflat[:, bass.ds((2 * i + n) * CH, CH)]
                        nc.vector.tensor_tensor(u, pR[n][:], u, ALU.mult).then_inc(scaled, 1)

                with v.Fori(0, NCH // 2) as i:
                    apply(i, False)


def state_space(nc, g):
    HALVES = QUADS // CH
    STEPS = 2 * HALVES
    YPB = 2 * STEPS + 1
    with ExitStack() as ctx:
        def sem(name):
            return ctx.enter_context(nc.semaphore("ssm_" + name))

        def sb(name, shape):
            return ctx.enter_context(nc.sbuf_tensor("ssm_" + name, shape, F32))

        pV = [[ctx.enter_context(nc.psum_tensor(f"ssm_v{n}{t}", [128, CH], F32)) for t in range(2)] for n in range(2)]
        pY = [ctx.enter_context(nc.psum_tensor(f"ssm_y{n}", [128, CH], F32)) for n in range(4)]
        rot = [sb(f"rot{n}", [128, 2, CH]) for n in range(2)]
        z = [sb(f"z{n}", [128, CH]) for n in range(2)]
        zc = sb("zc", [128, 2, QUADS + 1])
        zs = sb("zs", [128, 2, QUADS + 1])
        act_y = [sb(f"gelu{n}", [128, CH]) for n in range(4)]
        act_c = sb("geluc", [F, 2])
        entered = sem("entered")
        x0_made = sem("x0_made")
        turned = sem("turned")
        freed = sem("freed")
        scanned = sem("scanned")
        stated = sem("stated")
        yielded = sem("yielded")
        gelued = sem("gelued")
        summed = sem("summed")
        cls_y, cls_g, cls_a = sem("cls_y"), sem("cls_g"), sem("cls_a")
        start = sem("start")

        def part(d, h):
            return (h if d == FWD else HALVES - 1 - h) * CH

        def cols(t, b, d, h, q):
            return t[:, bass.ds(b * QUADS + part(d, h), CH), q]

        def scan_order(a, d):
            return a if d == FWD else a[:, ::-1]

        def before(t, d, h):
            a = part(d, h) + (0 if d == FWD else 1)
            return t[:, d, a:a + CH]

        def after(t, d, h):
            a = part(d, h) + (1 if d == FWD else 0)
            return scan_order(t[:, d, a:a + CH], d)

        ORDER = [(d, h) for d in (FWD, BWD) for h in range(HALVES)]
        LVI = {FWD: ((0, 1), (2, 3)), BWD: ((4, 5), (6, 7))}

        with nc.Block() as block:
            @block.tensor
            def _(pe):
                def enter(b, s, wait):
                    d, h = ORDER[s]
                    if wait:
                        pe.wait_ge(freed, b * STEPS + s - 1)
                    for t in range(2):
                        out = pV[s % 2][t]
                        carry = d == FWD and h == 0
                        for q in range(2):
                            last = nc.tensor.matmul(out[:], g.LV[:, LVI[d][t][q], :], cols(g.uT, b, d, h, q),
                                                    start=(q == 0), stop=(q == 1 and not carry))
                        if carry:
                            last = nc.tensor.matmul(out[:, 0:1], g.LV[:, (LV_CARRY, LV_CARRY_TURNED)[t], :], g.uC[:, 0:1],
                                                    start=False, stop=True)
                    last.then_inc(entered, 1)

                def leave(b, s):
                    d, h = ORDER[s]
                    for q in range(2):
                        n = 2 * s + q
                        out = pY[n % 4][:]
                        if isinstance(b, int) and b == 0:
                            if n >= 4:
                                pe.wait_ge(gelued, n - 3)
                        else:
                            pe.wait_ge(gelued, b * YPB + (n - 3 if n >= 4 else (0 if n == 0 else n - 4)))
                        nc.tensor.matmul(out, g.KI[:, d, 0, :, :], cols(g.uT, b, d, h, q), start=True, stop=False)
                        if q == (1 if d == FWD else 0):
                            nc.tensor.matmul(out, g.KI[:, d, 1, :, :], cols(g.uT, b, d, h, 1 - q), start=False, stop=False)
                        if q == 0:
                            pe.wait_ge(stated, b * STEPS + s + 1)
                        first = 1 + 2 * q if d == FWD else 2 * q
                        nc.tensor.matmul(out, g.N1[:, d, first:first + 2, :], before(zc, d, h),
                                         start=False, stop=False)
                        nc.tensor.matmul(out, g.N2[:, d, first:first + 2, :], before(zs, d, h),
                                         start=False, stop=True).then_inc(yielded, 1)

                def leave_class(b):
                    out = pY[0][0:F, 0:1]
                    pe.wait_ge(gelued, b * YPB + 2 * STEPS - 3)
                    nc.tensor.matmul(out, g.KI[:, BWD, 0, 0, :], g.uC[:, 0:1], start=True, stop=False)
                    nc.tensor.matmul(out, g.N1[:, BWD, 3, :], zc[:, BWD, 0:1], start=False, stop=False)
                    nc.tensor.matmul(out, g.N2[:, BWD, 3, :], zs[:, BWD, 0:1],
                                     start=False, stop=True).then_inc(yielded, 1)

                def batch(b, more):
                    for s in range(STEPS):
                        if s + 1 < STEPS:
                            enter(b, s + 1, not (isinstance(b, int) and b == 0 and s + 1 < 2))
                        elif more:
                            enter(b + 1, 0, True)
                        leave(b, s)
                    leave_class(b)

                nc.tensor.matmul(pY[0][:, 0:1], g.LV[:, LV_FIRST, :], g.uC[:, 0:1], start=True, stop=True)
                nc.tensor.matmul(pY[1][0:F, 0:1], g.KI[:, FWD, 0, 0, :], g.uC[:, 0:1],
                                 start=True, stop=True).then_inc(cls_y, 1)
                enter(0, 0, False)
                pe.wait_ge(cls_g, 2)
                batch(0, True)
                with pe.Fori(1, B - 1) as b:
                    batch(b, True)
                batch(B - 1, False)

            @block.vector
            def _(v):
                nc.vector.memset(zc[:, BWD, QUADS:], 0.0)
                nc.vector.memset(zs[:, BWD, QUADS:], 0.0)
                nc.vector.memset(zs[:, FWD, 0:1], 0.0).then_inc(start, 1)

                def step(b, s, n0):
                    d, h = ORDER[s]
                    n = b * STEPS + s
                    r, zz = rot[s % 2], z[s % 2]
                    cos, sin = (g.tab[:, d, k, h * CH:(h + 1) * CH] for k in range(2))
                    v.wait_ge(entered, n + 1)
                    nc.vector.tensor_tensor(r[:, 0, :], scan_order(pV[s % 2][0][:], d), cos, ALU.mult)
                    nc.vector.tensor_tensor(r[:, 1, :], scan_order(pV[s % 2][1][:], d), sin, ALU.mult).then_inc(freed, 1)
                    v.wait_ge(freed, n + 1)
                    nc.vector.tensor_tensor(r[:, 0, :], r[:, 0, :], r[:, 1, :], ALU.add).then_inc(turned, 1)
                    v.wait_ge(turned, n + 1)
                    initial = 0.0 if h == 0 else z[(s - 1) % 2][:, CH - 1:CH]
                    nc.vector.tensor_tensor_scan(zz[:], g.decay[:, d:d + 1].broadcast_to([128, CH]), r[:, 0, :], initial,
                                                 ALU.mult, ALU.add).then_inc(scanned, 1)
                    v.wait_ge(scanned, n + 1)
                    if not n0:
                        v.wait_ge(yielded, (b - 1) * YPB + min(2 * (s + 2), YPB) if s % 2 == 0 else (b - 1) * YPB + min(2 * (s + 1) + 1, YPB))
                    nc.vector.tensor_tensor(after(zc, d, h), zz[:], cos, ALU.mult)
                    nc.vector.tensor_tensor(after(zs, d, h), zz[:], sin, ALU.mult).then_inc(stated, 1)

                v.wait_ge(cls_g, 2)
                v.wait_ge(start, 1)
                for s in range(STEPS):
                    step(0, s, True)
                with v.Fori(1, B) as b:
                    for s in range(STEPS):
                        step(b, s, False)

            @block.scalar
            def _(act):
                act.wait_ge(cls_y, 1)
                nc.scalar.copy(zc[:, FWD, 0:1], pY[0][:, 0:1]).then_inc(cls_g, 1)
                nc.scalar.activation(act_c[:, 0:1], pY[1][0:F, 0:1], ACT.Gelu).then_inc(cls_g, 1)

                def batch(b, first):
                    for n in range(YPB):
                        act.wait_ge(yielded, b * YPB + n + 1)
                        if n < YPB - 1:
                            if first:
                                if n >= 4:
                                    act.wait_ge(summed, n - 3)
                            else:
                                act.wait_ge(summed, b * YPB + n - 3 - (1 if n < 4 else 0))
                            nc.scalar.activation(act_y[n % 4][:], pY[n % 4][:], ACT.Gelu).then_inc(gelued, 1)
                        else:
                            if not first:
                                act.wait_ge(summed, b * YPB)
                            nc.scalar.activation(act_c[:, 1:2], pY[0][0:F, 0:1], ACT.Gelu).then_inc(gelued, 1)

                batch(0, True)
                with act.Fori(1, B) as b:
                    batch(b, False)

            @block.gpsimd
            def _(pool):
                pool.wait_ge(cls_g, 2)
                nc.gpsimd.tensor_tensor(g.hC[0:F, :], g.hC[0:F, :], act_c[:, 0:1].broadcast_to([F, B]), ALU.add).then_inc(cls_a, 1)
                pool.wait_ge(cls_a, 1)

                def batch(b):
                    for n in range(YPB):
                        pool.wait_ge(gelued, b * YPB + n + 1)
                        if n < YPB - 1:
                            d, h = ORDER[n // 2]
                            if n == 2 * HALVES:
                                pool.wait_ge(summed, b * YPB + n)
                            t = cols(g.hT, b, d, h, n % 2)
                            nc.gpsimd.tensor_tensor(t, t, act_y[n % 4][:], ALU.add).then_inc(summed, 1)
                        else:
                            c = g.hC[0:F, bass.ds(b, 1)]
                            nc.gpsimd.tensor_tensor(c, c, act_c[:, 1:2], ALU.add).then_inc(summed, 1)

                for b in range(B):
                    batch(b)


def experts(nc, g):
    TILES = CH // 128
    with ExitStack() as ctx:
        def sem(name):
            return ctx.enter_context(nc.semaphore("ex_" + name))

        def sb(name, shape, dt=F32):
            return ctx.enter_context(nc.sbuf_tensor("ex_" + name, shape, dt))

        def ps(name, shape):
            return ctx.enter_context(nc.psum_tensor("ex_p" + name, shape, F32))

        pH = [ps(f"H{n}", [128, CH]) for n in range(2)]
        pE = [ps(f"E{n}", [128, EX, F]) for n in range(2)]
        pL = [ps(f"L{n}", [128, TILES, EX]) for n in range(2)]
        pR = ps("R", [128, TILES, 128])
        pZ = ps("Z", [128, 64])
        hid = [sb(f"hid{n}", [128, 2, CH]) for n in range(2)]
        hst = [sb(f"hst{n}", [128, CH]) for n in range(1)][0]
        gl = sb("gl", [128, 12, TILES, EX])
        gs = sb("gs", [128, 4, TILES])
        ms = [sb(f"ms{n}", [128, EX, F]) for n in range(2)]
        s4 = [sb(f"s4{n}", [128, 4, F]) for n in range(2)]
        s2 = [sb(f"s2{n}", [128, 2, F]) for n in range(2)]
        picked = [sb(f"picked{n}", [128, TILES, F]) for n in range(2)]
        res = [sb(f"res{n}", [128, TILES, 2, F]) for n in range(2)]
        clsr = sb("clsr", [B, F])
        hidden = sem("hidden")
        gelued = sem("gelued")
        staged = sem("staged")
        rested = sem("rested")
        gated = sem("gated")
        shifted = sem("shifted")
        tanhed = sem("tanhed")
        dv = sem("dv")
        spoke = sem("spoke")
        chosen = sem("chosen")
        pl = sem("pl")
        reduced = sem("reduced")
        finished = sem("finished")
        stored = [sem(f"stored{n}") for n in range(2)]
        cls_sem = sem("cls")
        GATE = 12
        uflat = g.uT[:].rearrange("p a r -> p (a r)")
        hflat = g.hT[:].rearrange("p a r -> p (a r)")
        bd3, bg3 = g.bias3[:, 0:EX * F], g.bias3[:, EX * F:]

        def gate(v, logits, base, P, T, tanh):
            G = lambda n: gl[0:P, n, 0:T, :]
            s = lambda n: gs[0:P, n, 0:T]
            wide = lambda a: a.unsqueeze(2).broadcast_to([P, T, EX])
            k = [0]

            def link(ins):
                k[0] += 1
                ins.then_inc(dv, 1)
                v.wait_ge(dv, base + k[0])

            link(nc.vector.tensor_reduce(s(0), logits, AX.X, ALU.max))
            k[0] += 1
            nc.vector.tensor_tensor(G(0), logits, wide(s(0)), ALU.subtract).then_inc(dv, 1)
            v.wait_ge(dv, base + k[0])
            link(nc.vector.tensor_scalar(G(1), G(0), 0.0, None, ALU.is_ge))
            link(nc.vector.tensor_tensor(G(1), G(1), g.rank[0:P, :].unsqueeze(1).broadcast_to([P, T, EX]), ALU.mult))
            link(nc.vector.tensor_reduce(s(1), G(1), AX.X, ALU.max))
            link(nc.vector.tensor_tensor(G(1), G(1), wide(s(1)), ALU.is_equal))
            v.wait_ge(tanhed, tanh)
            link(nc.vector.tensor_scalar(G(3), G(2), -0.5, 0.5, ALU.mult, ALU.add))
            link(nc.vector.reciprocal(G(3), G(3)))
            link(nc.vector.tensor_reduce(s(2), G(3), AX.X, ALU.add))
            link(nc.vector.tensor_scalar(s(2), s(2), -float(EX), None, ALU.add))
            link(nc.vector.reciprocal(s(3), s(2)))
            link(nc.vector.tensor_tensor(G(4), G(1), wide(s(3)), ALU.mult))
            assert k[0] == GATE


        with nc.Block() as block:
            @block.tensor
            def _(pe):
                def hide(i, par, first):
                    n = 2 * i + par
                    for h in range(2):
                        if not first:
                            pe.wait_ge(gelued, 2 * (n - 1) + h + 1)
                        nc.tensor.matmul(pH[h][:], g.W1z[:, par, 128 * h:128 * h + 128], uflat[:, bass.ds(i * CH, CH)],
                                         start=True, stop=True).then_inc(hidden, 1)

                def rest(i, first):
                    pe.wait_ge(staged, i + 1)
                    if not first:
                        pe.wait_ge(finished, 2 * i)
                    for j in range(TILES):
                        last = nc.tensor.transpose(pR[:, j, :], hst[:, 128 * j:128 * j + 128], g.ident[:])
                    last.then_inc(rested, 1)

                def gates(i, par, first):
                    n = 2 * i + par
                    pe.wait_ge(gelued, 2 * n + 2)
                    if not first:
                        pe.wait_ge(dv, (n - 1) * GATE)
                    for j in range(TILES):
                        o = pL[par][:, j, :]
                        nc.tensor.matmul(o, g.ones3[:], bg3, start=True, stop=False)
                        for h in range(2):
                            last = nc.tensor.matmul(o, hid[par][:, h, 128 * j:128 * j + 128], g.WgT[:, h, :],
                                                    start=False, stop=(h == 1))
                    last.then_inc(gated, 1)

                def speak(i, par, first):
                    n = 2 * i + par
                    for j in range(TILES):
                        if not (first and j < 2):
                            pe.wait_ge(chosen, n * TILES + j - 1)
                        o = pE[j % 2][:]
                        nc.tensor.matmul(o, g.ones3[:], bd3, start=True, stop=False)
                        for h in range(2):
                            last = nc.tensor.matmul(o, hid[par][:, h, 128 * j:128 * j + 128], g.WdT[:, h, :, :],
                                                    start=False, stop=(h == 1))
                        last.then_inc(spoke, 1)

                def chunk(i, first, more):
                    for par in range(2):
                        gates(i, par, first and par == 0)
                        if par == 0:
                            rest(i, first)
                            hide(i, 1, False)
                        elif more:
                            hide(i + 1, 0, False)
                        speak(i, par, first and par == 0)

                hide(0, 0, True)
                chunk(0, True, True)
                with pe.Fori(1, NCH - 1) as i:
                    chunk(i, False, True)
                chunk(NCH - 1, False, False)
                pe.wait_ge(gelued, 4 * NCH)
                for h in range(2):
                    nc.tensor.matmul(pZ[:, 4 * h:4 * h + B], g.W1z[:, 0, 128 * h:128 * h + 128], g.uC[:],
                                     start=(h == 0), stop=(h == 1), skip_group_check=True).then_inc(cls_sem, 1)
                pe.wait_ge(cls_sem, 4)
                pe.wait_ge(finished, 2 * NCH)
                o = pL[0][0:B, 0, :]
                nc.tensor.matmul(o, g.ones3[:, 0:B], bg3, start=True, stop=False)
                for h in range(2):
                    last = nc.tensor.matmul(o, hid[0][:, h, 0:B], g.WgT[:, h, :], start=False, stop=(h == 1))
                last.then_inc(gated, 1)
                nc.tensor.matmul(pE[0][0:B], g.ones3[:, 0:B], bd3, start=True, stop=False)
                for h in range(2):
                    last = nc.tensor.matmul(pE[0][0:B], hid[0][:, h, 0:B], g.WdT[:, h, :, :], start=False, stop=(h == 1))
                last.then_inc(spoke, 1)
                nc.tensor.transpose(pR[0:B, 0, :], g.hC[:], g.ident[:]).then_inc(rested, 1)

            @block.scalar
            def _(act):
                def stage(i):
                    act.wait_ge(rested, i)
                    nc.scalar.copy(hst[:], hflat[:, bass.ds(i * CH, CH)]).then_inc(staged, 1)

                def gelu(i, par, first):
                    n = 2 * i + par
                    for h in range(2):
                        act.wait_ge(hidden, 2 * n + h + 1)
                        if not first:
                            act.wait_ge(spoke, (n - 1) * TILES)
                        nc.scalar.activation(hid[par][:, h, :], pH[h][:], ACT.Gelu, bias=g.b1c[:, h:h + 1]).then_inc(gelued, 1)

                def tanh(i, par):
                    n = 2 * i + par
                    act.wait_ge(dv, n * GATE + 2)
                    nc.scalar.activation(gl[:, 2], gl[:, 0], ACT.Tanh, scale=0.5).then_inc(tanhed, 1)

                def chunk(i, first, more):
                    stage(i)
                    gelu(i, 1, first)
                    tanh(i, 0)
                    if more:
                        gelu(i + 1, 0, False)
                    tanh(i, 1)

                gelu(0, 0, True)
                chunk(0, True, True)
                with act.Fori(1, NCH - 1) as i:
                    chunk(i, False, True)
                chunk(NCH - 1, False, False)
                act.wait_ge(cls_sem, 2)
                act.wait_ge(spoke, 2 * NCH * TILES)
                for h in range(2):
                    nc.scalar.activation(hid[0][:, h, 0:B], pZ[:, 4 * h:4 * h + B], ACT.Gelu,
                                         bias=g.b1c[:, h:h + 1]).then_inc(cls_sem, 1)
                act.wait_ge(dv, 2 * NCH * GATE + 2)
                nc.scalar.activation(gl[0:B, 2, 0:1], gl[0:B, 0, 0:1], ACT.Tanh, scale=0.5).then_inc(tanhed, 1)

            @block.vector
            def _(v):
                def unit(i, par, first):
                    n = 2 * i + par
                    v.wait_ge(gated, n + 1)
                    gate(v, pL[par][:], n * GATE, 128, TILES, n + 1)
                    for j in range(TILES):
                        v.wait_ge(spoke, n * TILES + j + 1)
                        if not (first and j < 2):
                            v.wait_ge(reduced, n * TILES + j - 1)
                        nc.vector.tensor_tensor(ms[j % 2][:], pE[j % 2][:],
                                                gl[:, 4, j, :].unsqueeze(2).broadcast_to([128, EX, F]), ALU.mult).then_inc(chosen, 1)

                def two(k, first):
                    for m in range(2):
                        i = 2 * k + m
                        for par in range(2):
                            unit(i, par, first and m == 0 and par == 0)
                            n = 2 * i + par
                            v.wait_ge(reduced, (n + 1) * TILES)
                            if par == 0:
                                v.wait_ge(rested, i + 1)
                                if not first:
                                    v.wait_ge(stored[m], 16 * k)
                            nc.vector.tensor_tensor(res[m][:, :, par, :], pR[:, :, F * par:F * par + F], picked[par][:],
                                                    ALU.add).then_inc(finished, 1)

                two(0, True)
                with v.Fori(1, NCH // 2) as k:
                    two(k, False)
                v.wait_ge(gated, 2 * NCH + 1)
                gate(v, pL[0][0:B, 0:1, :], 2 * NCH * GATE, B, 1, 2 * NCH + 1)
                v.wait_ge(spoke, 2 * NCH * TILES + 1)
                nc.vector.tensor_tensor(ms[0][0:B], pE[0][0:B], gl[0:B, 4, 0, :].unsqueeze(2).broadcast_to([B, EX, F]), ALU.mult).then_inc(chosen, 1)
                v.wait_ge(reduced, 2 * NCH * TILES + 1)
                v.wait_ge(rested, NCH + 1)
                nc.vector.tensor_tensor(clsr[:], pR[0:B, 0, 0:F], picked[0][0:B, 0, :], ALU.add).then_inc(finished, 1)

            @block.gpsimd
            def _(pool):
                def tile(n, j, slot, par, P):
                    pool.wait_ge(chosen, n + 1)
                    m = ms[slot][0:P]
                    nc.gpsimd.tensor_tensor(s4[slot][0:P], m[:, 0:4], m[:, 4:8], ALU.add).then_inc(pl, 1)
                    pool.wait_ge(pl, 2 * n + 1)
                    nc.gpsimd.tensor_tensor(s2[slot][0:P], s4[slot][0:P, 0:2], s4[slot][0:P, 2:4], ALU.add).then_inc(pl, 1)
                    pool.wait_ge(pl, 2 * n + 2)
                    nc.gpsimd.tensor_tensor(picked[par][0:P, j, :], s2[slot][0:P, 0], s2[slot][0:P, 1], ALU.add).then_inc(reduced, 1)

                def unit(i, par, first):
                    n = 2 * i + par
                    if not first:
                        pool.wait_ge(finished, n - 1)
                    for j in range(TILES):
                        tile(n * TILES + j, j, j % 2, par, 128)

                for par in range(2):
                    unit(0, par, True)
                with pool.Fori(1, NCH) as i:
                    for par in range(2):
                        unit(i, par, False)
                tile(2 * NCH * TILES, 0, 0, 0, B)

            @block.sync
            def _(sp):
                rows = g.out[:, 1:, :].rearrange("b (q j p r) c -> b q p j (r c)", q=4, j=TILES, p=128, r=2)
                with sp.Fori(0, B) as b:
                    for q in range(4):
                        sp.wait_ge(finished, 8 * b + 2 * q + 2)
                        sp.dma_start(rows[bass.ds(b, 1), q].rearrange("b p j x -> (b p) j x"),
                                     res[q % 2][:].rearrange("p j r c -> p j (r c)")).then_inc(stored[q % 2], 16)
                sp.wait_ge(finished, 2 * NCH + 1)
                sp.dma_start(g.out[:, 0, :], clsr[:]).then_inc(cls_sem, 16)
                sp.wait_ge(cls_sem, 20)
                for n in range(2):
                    sp.wait_ge(stored[n], 16 * NCH // 2)


SSM_NAMES = ["log_real", "imag", "log_Delta", "B_real", "B_imag", "C_real", "C_imag", "D"]
_INS = (["x", "cls_tok"]
        + ["L0_tok_" + n for n in ("conv1_w", "conv1_b", "bn_gamma", "bn_beta", "bn_mean", "bn_var", "conv2_w", "conv2_b")]
        + ["L0_attn_fwd_" + n for n in SSM_NAMES] + ["L0_attn_bwd_" + n for n in SSM_NAMES]
        + ["L0_ffn_" + n for n in ("W1", "b1", "Wg", "bg", "Wd", "bd")])
_OUT = (B, C * HW + 1, F)


def kernel(**inputs):
    import concourse.bacc as bacc
    from concourse.bass_utils import run_bass_kernel_spmd

    nc = bacc.Bacc("TRN2", target_bir_lowering=False, num_devices=1)
    arrays, aps = {}, []
    for name in _INS:
        a = np.ascontiguousarray(inputs[name])
        arrays["in_" + name] = a
        aps.append(nc.dram_tensor("in_" + name, a.shape, mybir.dt.from_np(a.dtype), kind="ExternalInput").ap())
    out = nc.dram_tensor("out_0", _OUT, F32, kind="ExternalOutput").ap()
    vit_tower(nc, aps, out)
    r = run_bass_kernel_spmd(nc, [arrays], core_ids=[0])
    return r.results[0]["out_0"]
```

```python
from contextlib import ExitStack

import numpy as np
import concourse.bass as bass
from concourse import mybir

ALU = mybir.AluOpType
ACT = mybir.ActivationFunctionType
AX = mybir.AxisListType
F32 = mybir.dt.float32
F32R = mybir.dt.float32r

B, C, HW = 4, 64, 64
CR, TAPS = 16, 9
F = HW
NS = 64
HID, EX = 256, 8
PAIRS = C * HW // 2
CH = 512
NCH = B * PAIRS // CH
QUADS = PAIRS // 2
GRP = 4
PROW = (HW + 2) * HW
BN_EPS = LN_EPS = 1e-5
FWD, BWD = 0, 1
YROWS = 3 * 2 * CR + 2


class Tower:

    def __init__(self, nc, ctx, arrays, out):
        (self.x, self.cls_tok, self.conv1_w, self.conv1_b, self.bn_gamma, self.bn_beta, self.bn_mean, self.bn_var,
         self.conv2_w, self.conv2_b) = arrays[:10]
        self.ssm_f, self.ssm_b = arrays[10:18], arrays[18:26]
        self.W1, self.b1, self.Wg, self.bg, self.Wd, self.bd = arrays[26:]
        self.out = out

        def sb(name, shape, dt=F32):
            return ctx.enter_context(nc.sbuf_tensor(name, shape, dt))

        self.img = sb("img", [128, 2, PROW])
        self.hT = sb("hT", [128, B * QUADS, 2])
        self.uT = sb("uT", [128, B * QUADS, 2])
        self.hC = sb("hC", [128, B])
        self.uC = sb("uC", [128, B])
        self.ident = sb("ident", [128, 128])
        self.ones = sb("ones", [128, 128])
        self.center = sb("center", [128, 128])
        self.mean2 = sb("mean2", [128, 2])
        self.conv1L = sb("conv1L", [128, 3, 2 * CR])
        self.conv2L = sb("conv2L", [YROWS, TAPS, 128], F32R)
        self.ysc = sb("ysc", [3 * 2 * CR, 8])
        self.eps = sb("eps", [128, 2])
        self.LV = sb("LV", [128, 12, 128])
        self.N1 = sb("N1", [128, 2, 5, F])
        self.N2 = sb("N2", [128, 2, 5, F])
        self.KI = sb("KI", [128, 2, 2, 2, F])
        self.decay = sb("decay", [128, 2])
        self.turn = sb("turn", [128, 10, 2, 2])
        self.tab = sb("tab", [128, 2, 2, QUADS])
        self.W1z = sb("W1z", [128, 2, HID])
        self.b1c = sb("b1c", [128, 2])
        self.WgT = sb("WgT", [128, 2, EX])
        self.WdT = sb("WdT", [128, 2, EX, F])
        self.WdP = [sb(f"WdP{n}", [128, 2, EX, F], F32R) for n in range(2)]
        self.bias2 = sb("bias2", [2, EX * F + 4 * EX], F32R)
        self.ones2 = sb("ones2", [2, 128], F32R)
        self.rank = sb("rank", [128, EX])


def vit_tower(nc, arrays, out):
    with ExitStack() as ctx:
        g = Tower(nc, ctx, arrays, out)
        setup(nc, g)
        involution(nc, g)
        layer_norm(nc, g, "1")
        state_space(nc, g)
        layer_norm(nc, g, "2")
        experts(nc, g)


def setup(nc, g):
    with ExitStack() as ctx:
        def sb(name, shape, dt=F32):
            return ctx.enter_context(nc.sbuf_tensor("s0_" + name, shape, dt))

        def ps(name, shape):
            return ctx.enter_context(nc.psum_tensor("p0_" + name, shape, F32))

        def sem(name):
            return ctx.enter_context(nc.semaphore("s0_" + name))

        raw = sb("raw", [128, 2, 3])
        Bm = sb("Bm", [128, 2, 2, F])
        Cin = sb("Cin", [F, 2, 3, NS])
        Dv = sb("Dv", [128, 2])
        S = sb("S", [128, 40, 2])
        M = sb("M", [128, 2, 2, 6, F])
        M0 = sb("M0", [128, 2, 2, F])
        K0 = sb("K0", [128, 2, F])
        tmp = sb("tmp", [128, 2, F])
        sgn = sb("sgn", [128, 1])
        w2 = sb("w2", [YROWS, TAPS])
        w2p = sb("w2p", [YROWS, 2, TAPS], F32R)
        w2s = sb("w2s", [YROWS, TAPS])
        own = sb("own", [YROWS, 2])
        w1o = sb("w1o", [CR, C])
        wk = sb("wk", [TAPS, CR + 1])
        w1d = sb("w1d", [CR, 2, C])
        wkd = sb("wkd", [TAPS, YROWS])
        bn5 = sb("bn5", [CR, 5])
        spread6 = sb("spread6", [CR, 6, CR])
        bfull = sb("bfull", [2, EX * F + 4 * EX])
        bpart = sb("bpart", [2, 2, EX * F + 4 * EX], F32R)
        bsel = sb("bsel", [2, EX * F + 4 * EX])
        pT = [ps(f"T{i}", [128, 4, 128]) for i in range(3)]
        pC = ps("C", [128, 4, F])
        pA = ps("A", [128, CR])
        pB = ps("B", [YROWS, TAPS])
        pN = ps("N", [3 * 2 * CR, 5])
        pK = ps("K", [128, 2, 4, F])

        img_in = sem("img_in")
        ssm_in = sem("ssm_in")
        conv_in = sem("conv_in")
        ffn_in = sem("ffn_in")
        zeroed = sem("zeroed")
        pool_const = sem("pool_const")
        dve = sem("dve")
        exped = sem("exped")
        sined = sem("sined")
        c_turned = sem("c_turned")
        m_turned = sem("m_turned")
        k_made = sem("k_made")
        w_spread = sem("w_spread")
        consts = {}
        img, hT, uT = g.img, g.hT, g.uT

        with nc.Block() as block:
            vec = nc.vector
            steps = [0]

            def count(name):
                consts[name] = steps[0]

            @block.vector
            def _(v):
                def link(ins):
                    steps[0] += 1
                    ins.then_inc(dve, 1)
                    v.wait_ge(dve, steps[0])

                def tt(o, a, b, op):
                    link(vec.tensor_tensor(o, a, b, op))

                def ts(o, a, s1, s2, op0, op1=ALU.bypass):
                    link(vec.tensor_scalar(o, a, s1, s2, op0, op1) if s2 is not None
                         else vec.tensor_scalar(o, a, s1, None, op0))

                def stt(o, a, s, b, op0, op1):
                    link(vec.scalar_tensor_tensor(out=o, in0=a, scalar=s, in1=b, op0=op0, op1=op1))

                def copy(o, a):
                    link(vec.tensor_copy(o, a))

                def fill(o, c):
                    link(vec.memset(o, c))

                v.wait_ge(ssm_in, 16 * 30)
                fill(g.ones[:], 1.0)
                fill(g.eps[:], LN_EPS)
                fill(sgn[0:64], 1.0)
                fill(sgn[64:128], -1.0)
                fill(g.ones2[:].bitcast(F32), 1.0)
                fill(g.mean2[:], 0.0)
                fill(g.mean2[0:64, 0:1], 1.0 / F)
                fill(g.mean2[64:128, 1:2], 1.0 / F)
                fill(M[:, :, :, 5, :], 0.0)
                fill(g.KI[:], 0.0)
                v.wait_ge(pool_const, 5)
                copy(g.center[:], g.ident[:])
                for h in range(2):
                    s = slice(64 * h, 64 * h + 64)
                    ts(g.center[s, s], g.ident[s, s], -1.0 / F, None, ALU.add)
                s = lambda n: S[:, n, :]
                v.wait_ge(exped, 2)
                stt(s(2), s(0), -1.0, s(1), ALU.mult, ALU.mult)
                count("ad")
                tt(s(3), raw[:, :, 1], s(1), ALU.mult)
                magic = 1.5 * 2.0 ** 23
                ts(s(5), s(3), 1.0 / (2 * np.pi), magic, ALU.mult, ALU.add)
                ts(s(6), s(5), -magic, None, ALU.add)
                p1 = 6.28125
                p2 = float(np.float32(2 * np.pi - p1))
                p3 = float(2 * np.pi - p1 - p2)
                stt(s(7), s(6), -p1, s(3), ALU.mult, ALU.add)
                stt(s(7), s(6), -p2, s(7), ALU.mult, ALU.add)
                stt(s(7), s(6), -p3, s(7), ALU.mult, ALU.add)
                edge = float(np.nextafter(np.float32(np.pi), np.float32(0)))
                ts(s(7), s(7), edge, -edge, ALU.min, ALU.max)
                count("angle")
                v.wait_ge(exped, 3)
                v.wait_ge(sined, 2)
                tt(s(10), s(9), s(9), ALU.mult)
                ts(s(10), s(10), -2.0, 1.0, ALU.mult, ALU.add)
                tt(s(11), s(4), s(10), ALU.mult)
                tt(s(12), s(4), s(8), ALU.mult)
                ts(s(13), s(0), -1.0, None, ALU.mult)
                tt(s(14), s(13), s(13), ALU.mult)
                tt(s(15), raw[:, :, 1], raw[:, :, 1], ALU.mult)
                tt(s(14), s(14), s(15), ALU.add)
                ts(s(14), s(14), 1e-12, None, ALU.max)
                link(vec.reciprocal(s(15), s(14)))
                tt(s(16), s(13), s(15), ALU.mult)
                stt(s(17), raw[:, :, 1], -1.0, s(15), ALU.mult, ALU.mult)
                ts(s(18), s(11), -1.0, None, ALU.add)
                tt(s(19), s(16), s(18), ALU.mult)
                tt(s(20), s(17), s(12), ALU.mult)
                tt(s(19), s(19), s(20), ALU.subtract)
                tt(s(20), s(16), s(12), ALU.mult)
                tt(s(21), s(17), s(18), ALU.mult)
                tt(s(20), s(20), s(21), ALU.add)
                tt(s(21), s(4), s(4), ALU.mult)
                tt(g.decay[:], s(21), s(21), ALU.mult)

                def square(co, so, c, sn):
                    tt(s(30), c, c, ALU.mult)
                    tt(s(31), sn, sn, ALU.mult)
                    tt(s(32), c, sn, ALU.mult)
                    tt(s(33), s(30), s(31), ALU.subtract)
                    tt(s(34), s(30), s(31), ALU.add)
                    ts(s(34), s(34), -1.0, 2.0, ALU.mult, ALU.add)
                    tt(co, s(33), s(34), ALU.mult)
                    stt(so, s(32), 2.0, s(34), ALU.mult, ALU.mult)

                square(s(22), s(23), s(10), s(8))
                square(g.turn[:, 0, 0, :], g.turn[:, 0, 1, :], s(22), s(23))
                for k in range(9):
                    square(g.turn[:, k + 1, 0, :], g.turn[:, k + 1, 1, :], g.turn[:, k, 0, :], g.turn[:, k, 1, :])

                for d in range(2):
                    ts(Bm[64:128, d, 1, :], Bm[64:128, d, 1, :], -1.0, None, ALU.mult)
                    col = lambda n: S[:, n, d:d + 1]
                    slot = (lambda e: 4 - e) if d == FWD else (lambda e: e)
                    at = lambda n, e: M[:, d, n, slot(e), :]

                    def times(o1, o2, a1, a2, cr, ci):
                        ts(tmp[:, 0, :], a2, ci, None, ALU.mult)
                        ts(tmp[:, 1, :], a1, ci, None, ALU.mult)
                        stt(o1, a1, cr, tmp[:, 0, :], ALU.mult, ALU.subtract)
                        stt(o2, a2, cr, tmp[:, 1, :], ALU.mult, ALU.add)

                    times(at(0, 0), at(1, 0), Bm[:, d, 0, :], Bm[:, d, 1, :], col(19), col(20))
                    for e in range(4):
                        times(at(0, e + 1), at(1, e + 1), at(0, e), at(1, e), col(11), col(12))
                    copy(M0[:, d, 0, :], at(0, 0))
                    copy(M0[:, d, 1, :], at(0, 0))
                count("M")
                v.wait_ge(c_turned, 1)
                for d in range(2):
                    col = lambda n: S[:, n, d:d + 1]
                    slot = (lambda k: k) if d == FWD else (lambda k: 4 - k)
                    n1 = lambda k: g.N1[:, d, slot(k), :]
                    n2 = lambda k: g.N2[:, d, slot(k), :]
                    ts(n1(0), pC[:, 2 * d, :], sgn[:, 0:1], None, ALU.mult)
                    ts(n2(0), pC[:, 2 * d + 1, :], -1.0, None, ALU.mult)
                    for k in range(4):
                        ts(tmp[:, 0, :], n2(k), col(12), None, ALU.mult)
                        ts(tmp[:, 1, :], n1(k), col(12), None, ALU.mult)
                        stt(n1(k + 1), n1(k), col(11), tmp[:, 0, :], ALU.mult, ALU.add)
                        stt(n2(k + 1), n2(k), col(11), tmp[:, 1, :], ALU.mult, ALU.subtract)
                count("N")
                v.wait_ge(conv_in, 16 * 8)
                copy(w1d[:], w1o[:].unsqueeze(1).broadcast_to([CR, 2, C]))
                copy(spread6[:], g.ident[0:CR, 0:CR].unsqueeze(1).broadcast_to([CR, 6, CR]))
                copy(wkd[:, 0:6 * CR].rearrange("k (r o) -> k r o", r=6), wk[:, 0:CR].unsqueeze(1).broadcast_to([TAPS, 6, CR]))
                copy(wkd[:, 6 * CR:], wk[:, CR:].broadcast_to([TAPS, 2]))
                count("conv_laid")
                v.wait_ge(w_spread, 1)
                copy(g.ysc[:, 0:5], pN[:])
                copy(w2[:], pB[:])
                fill(g.conv1L[:], 0.0)
                for b2 in range(2):
                    r = slice(C * b2, C * b2 + C)
                    copy(g.conv1L[r, :, CR * b2:CR * b2 + CR], pA[r, :].unsqueeze(1).broadcast_to([C, 3, CR]))
                copy(w2p[:, 0, :], w2[:])
                tt(w2p[:, 1, :], w2[:], w2p[:, 0, :], ALU.subtract)
                copy(w2s[:], w2p[:, 0, :])
                copy(w2s[32:64], w2p[32:64, 1, :])
                b2 = slice(3 * 2 * CR, YROWS)
                ts(w2s[b2], w2p[b2, 0, :], g.ident[b2, 96:97], None, ALU.mult)
                stt(w2s[b2], w2p[b2, 1, :], g.ident[b2, 97:98], w2s[b2], ALU.mult, ALU.add)
                cb, ga, be, mu, va = (g.ysc[:, n:n + 1] for n in range(5))
                ts(g.ysc[:, 5:6], va, BN_EPS, None, ALU.add)
                count("bnvar")
                v.wait_ge(sined, 3)
                link(vec.reciprocal(g.ysc[:, 7:8], g.ysc[:, 6:7]))
                tt(g.ysc[:, 6:7], ga, g.ysc[:, 7:8], ALU.mult)
                tt(g.ysc[:, 7:8], cb, mu, ALU.subtract)
                stt(g.ysc[:, 7:8], g.ysc[:, 7:8], g.ysc[:, 6:7], be, ALU.mult, ALU.add)
                fill(own[:], 1.0)
                link(vec.tensor_reduce(own[0:96], g.ident[0:96, 0:96].rearrange("p (r i o) -> p i r o", r=3, i=2),
                                       AX.XY, ALU.add))
                for i in range(2):
                    ts(g.conv2L[:, :, C * i:C * i + C], w2s[:].unsqueeze(2).broadcast_to([YROWS, TAPS, C]),
                       own[:, i:i + 1], None, ALU.mult)
                v.wait_ge(m_turned, 1)
                for n in range(3):
                    k = 4 if n < 2 else 3
                    copy(g.LV[:, 4 * n:4 * n + k, :], pT[n][:, 0:k, :])
                v.wait_ge(k_made, 1)
                for d in range(2):
                    kk = (lambda k: pK[:, FWD, k, :]) if d == FWD else (lambda k: pK[:, BWD, 3 - k, :])
                    for h in range(2):
                        r = slice(64 * h, 64 * h + 64)
                        stt(K0[r, d, :], g.ident[r, r], Dv[r, d:d + 1], kk(0)[r], ALU.mult, ALU.add)
                    lo, hi = slice(0, 64), slice(64, 128)
                    if d == FWD:
                        plan = [(lo, 0, 0, 0), (lo, 0, 1, 1), (hi, 0, 1, 0), (lo, 1, 0, 2), (lo, 1, 1, 3), (hi, 1, 0, 1), (hi, 1, 1, 2)]
                    else:
                        plan = [(lo, 0, 0, 0), (hi, 0, 0, 1), (hi, 0, 1, 0), (lo, 1, 0, 2), (lo, 1, 1, 1), (hi, 1, 0, 3), (hi, 1, 1, 2)]
                    for r, which, j, k in plan:
                        copy(g.KI[r, d, which, j, :], K0[r, d, :] if k == 0 else kk(k)[r])
                v.wait_ge(ffn_in, 16 * 11)
                for col in range(1, B):
                    copy(g.hC[0:F, col:col + 1], g.hC[0:F, 0:1])
                for n in range(1, 4):
                    copy(bfull[:, EX * (F + n):EX * (F + n + 1)], bfull[:, EX * F:EX * F + EX])
                copy(bpart[:, 0, :], bfull[:])
                tt(bpart[:, 1, :], bfull[:], bpart[:, 0, :], ALU.subtract)
                ts(bsel[:], bpart[:, 0, :], g.ident[0:2, 0:1], None, ALU.mult)
                stt(g.bias2[:], bpart[:, 1, :], g.ident[0:2, 1:2], bsel[:], ALU.mult, ALU.add)

            @block.sync
            def _(sp):
                dirs = (g.ssm_f, g.ssm_b)
                for d, (lr, im, ld, Br, Bi, Cr, Ci, D) in enumerate(dirs):
                    for half in (slice(0, 64), slice(64, 128)):
                        for n, v in enumerate((lr, im, ld)):
                            sp.dma_start(raw[half, d, n:n + 1], v.rearrange("(p a) -> p a", a=1)).then_inc(ssm_in, 16)
                        sp.dma_start(Dv[half, d:d + 1], D.rearrange("(p a) -> p a", a=1)).then_inc(ssm_in, 16)
                    sp.dma_start(Bm[0:64, d, 0, :], Br).then_inc(ssm_in, 16)
                    sp.dma_start(Bm[64:128, d, 0, :], Bi).then_inc(ssm_in, 16)
                    sp.dma_start(Bm[0:64, d, 1, :], Bi).then_inc(ssm_in, 16)
                    sp.dma_start(Bm[64:128, d, 1, :], Br).then_inc(ssm_in, 16)
                    sp.dma_start(Cin[:, d, 0, :], Cr).then_inc(ssm_in, 16)
                    sp.dma_start(Cin[:, d, 1, :], Ci).then_inc(ssm_in, 16)
                    sp.dma_start(Cin[:, d, 2, :], Cr).then_inc(ssm_in, 16)
                for bp in range(2):
                    sp.dma_start(img[:, bp, HW:HW + HW * HW],
                                 g.x[2 * bp:2 * bp + 2].rearrange("b c h w -> (b c) (h w)")).then_inc(img_in, 16)
                sp.wait_ge(img_in, 32)

            @block.gpsimd
            def _(pool):
                nc.gpsimd.memset(g.W1z[:], 0.0).then_inc(zeroed, 1)
                nc.gpsimd.memset(g.hC[:], 0.0).then_inc(zeroed, 1)
                nc.gpsimd.memset(g.ident[:], 0.0).then_inc(pool_const, 1)
                pool.wait_ge(pool_const, 1)
                nc.gpsimd.affine_select(out=g.ident[:], in_=g.ident[:], compare_op=ALU.not_equal, fill=1.0,
                                        base=0, pattern=[[-1, 128]], channel_multiplier=1).then_inc(pool_const, 1)
                nc.gpsimd.iota(g.rank[:], pattern=[[-1, EX]], base=EX, channel_multiplier=0,
                               allow_small_or_imprecise_dtypes=True).then_inc(pool_const, 1)
                for bp in range(2):
                    nc.gpsimd.memset(img[:, bp, 0:HW], 0.0)
                    nc.gpsimd.memset(img[:, bp, PROW - HW:PROW], 0.0).then_inc(pool_const, 1)

            @block.scalar
            def _(act):
                act.wait_ge(zeroed, 2)
                act.dma_start(w1o[:, :], g.conv1_w).then_inc(conv_in, 16)
                act.dma_start(wk[:, 0:CR], g.conv2_w).then_inc(conv_in, 16)
                act.dma_start(wk[:, CR:CR + 1], g.conv2_b.rearrange("(k a) -> k a", a=1)).then_inc(conv_in, 16)
                for n, v in enumerate((g.conv1_b, g.bn_gamma, g.bn_beta, g.bn_mean, g.bn_var)):
                    act.dma_start(bn5[:, n:n + 1], v.rearrange("(p a) -> p a", a=1)).then_inc(conv_in, 16)
                act.wait_ge(ssm_in, 16 * 30)
                nc.scalar.activation(S[:, 0, :], raw[:, :, 0], ACT.Exp).then_inc(exped, 1)
                nc.scalar.activation(S[:, 1, :], raw[:, :, 2], ACT.Exp).then_inc(exped, 1)
                act.wait_ge(dve, consts["ad"])
                nc.scalar.activation(S[:, 4, :], S[:, 2, :], ACT.Exp).then_inc(exped, 1)
                act.wait_ge(dve, consts["angle"])
                nc.scalar.activation(S[:, 8, :], S[:, 7, :], ACT.Sin).then_inc(sined, 1)
                nc.scalar.activation(S[:, 9, :], S[:, 7, :], ACT.Sin, scale=0.5).then_inc(sined, 1)
                act.wait_ge(dve, consts["bnvar"])
                nc.scalar.activation(g.ysc[:, 6:7], g.ysc[:, 5:6], ACT.Sqrt).then_inc(sined, 1)
                act.wait_ge(zeroed, 2)
                for par in range(2):
                    act.dma_start(g.W1z[F * par:F * par + F, par, :], g.W1).then_inc(ffn_in, 16)
                act.dma_start(g.hC[0:F, 0:1], g.cls_tok.rearrange("a b f -> f (a b)")).then_inc(ffn_in, 16)
                act.dma_start(g.b1c[:], g.b1.rearrange("(h p) -> p h", p=128), allow_slow_non_contiguous=True).then_inc(ffn_in, 16)
                act.dma_start(g.WgT[:], g.Wg.rearrange("(h p) e -> p h e", p=128)).then_inc(ffn_in, 16)
                for h in range(2):
                    act.dma_start(g.WdT[:, h], g.Wd[:, 128 * h:128 * h + 128, :].rearrange("e p f -> p e f")).then_inc(ffn_in, 16)
                for r in range(2):
                    act.dma_start(bfull[r:r + 1, 0:EX * F], g.bd.rearrange("(a e) f -> a (e f)", a=1)).then_inc(ffn_in, 16)
                    act.dma_start(bfull[r:r + 1, EX * F:EX * F + EX], g.bg.rearrange("(a e) -> a e", a=1)).then_inc(ffn_in, 16)
                act.wait_ge(ffn_in, 16 * 11)

            @block.tensor
            def _(pe):
                pe.wait_ge(ssm_in, 16 * 30)
                pe.wait_ge(pool_const, 2)
                for d in range(2):
                    nc.tensor.transpose(pC[:, 2 * d, :], Cin[:, d, 0:2, :], g.ident[0:F, 0:F])
                    last = nc.tensor.transpose(pC[:, 2 * d + 1, :], Cin[:, d, 1:3, :], g.ident[0:F, 0:F])
                last.then_inc(c_turned, 1)
                pe.wait_ge(dve, consts["M"])
                for n, (d, which, slot) in enumerate(LV_PLAN):
                    last = nc.tensor.transpose(pT[n // 4][:, n % 4, :], M[:, d, which, slot:slot + 2, :], g.ident[:])
                last.then_inc(m_turned, 1)
                pe.wait_ge(dve, consts["N"])
                for d in range(2):
                    first = 0 if d == FWD else 1
                    last = nc.tensor.matmul(pK[:, d, :, :], M0[:, d, :, :], g.N1[:, d, first:first + 4, :],
                                            start=(d == 0), stop=(d == 1), skip_group_check=True)
                last.then_inc(k_made, 1)
                pe.wait_ge(dve, consts["conv_laid"])
                nc.tensor.transpose(pA[:], w1d[:].rearrange("o b c -> o (b c)"), g.ident[0:CR, 0:CR])
                nc.tensor.transpose(pB[:], wkd[:], g.ident[0:TAPS, 0:TAPS])
                nc.tensor.matmul(pN[:], spread6[:].rearrange("o r p -> o (r p)"), bn5[:], start=True, stop=True).then_inc(w_spread, 1)


LV_PLAN = [(FWD, 0, 1), (FWD, 0, 3), (FWD, 1, 1), (FWD, 1, 3),
           (BWD, 0, 0), (BWD, 0, 2), (BWD, 1, 0), (BWD, 1, 2),
           (FWD, 0, 0), (FWD, 1, 0), (FWD, 0, 4)]
LV_CARRY, LV_CARRY_TURNED, LV_FIRST = 8, 9, 10



def involution(nc, g):
    CPI = HW * HW // CH
    ROWS = CH // HW
    NW = 3
    PIECE = 256
    with ExitStack() as ctx:
        def sem(name):
            return ctx.enter_context(nc.semaphore("inv_" + name))

        prod = ctx.enter_context(nc.sbuf_tensor("inv_prod", [128, TAPS, ROWS, HW], F32))
        yf = ctx.enter_context(nc.sbuf_tensor("inv_yf", [3 * 2 * CR, CH], F32))
        ysb = [ctx.enter_context(nc.sbuf_tensor(f"inv_ysb{n}", [YROWS, CH], F32R)) for n in range(2)]
        half = ctx.enter_context(nc.sbuf_tensor("inv_half", [128, 2, 2, PIECE], F32))
        pY = ctx.enter_context(nc.psum_tensor("inv_pY", [3 * 2 * CR, CH], F32))
        pW = [ctx.enter_context(nc.psum_tensor(f"inv_pW{n}", [128, ROWS, HW], F32)) for n in range(NW)]
        pS = ctx.enter_context(nc.psum_tensor("inv_pS", [128, CH], F32))
        reduced = sem("reduced")
        relued = sem("relued")
        parted = sem("parted")
        weighed = sem("weighed")
        filtered = sem("filtered")
        added = sem("added")
        moved = sem("moved")
        doubled = sem("doubled")
        multiplied = sem("multiplied")
        onesrow = sem("onesrow")

        def tap(k):
            dh, dw = k // 3 - 1, k % 3 - 1
            lo, hi = max(0, -dw), HW - max(0, dw)
            return dh, dw, lo, hi

        def starts(bp, hc):
            return bp == 0 and isinstance(hc, int) and hc == 0

        def chunks(eng, bp, body):
            body(bp, 0, 0, True)
            with eng.Fori(0, CPI // 2 - 1) as k:
                body(bp, 2 * k + 1, 1, True)
                body(bp, 2 * k + 2, 0, True)
            body(bp, CPI - 1, 1, False)

        with nc.Block() as block:
            @block.tensor
            def _(pe):
                def reduce(bp, hc):
                    n = bp * CPI + hc
                    pe.wait_ge(relued, n)
                    nc.tensor.matmul(pY[:], g.conv1L[:].rearrange("p r o -> p (r o)"),
                                     g.img[:, bp, bass.ds(HW + hc * CH, CH)], start=True, stop=True).then_inc(reduced, 1)

                def weigh(bp, hc, u, k):
                    n = bp * CPI + hc
                    if k == 0:
                        pe.wait_ge(parted, n + 1)
                    if k >= NW or not starts(bp, hc):
                        pe.wait_ge(filtered, n * TAPS + k - NW + 1)
                    nc.tensor.matmul(pW[k % NW][:], g.conv2L[:, k, :], ysb[u][:], start=True, stop=True).then_inc(weighed, 1)

                def body(bp, hc, u, more):
                    n = bp * CPI + hc
                    for k in range(TAPS):
                        if k == 0 and more:
                            reduce(bp, hc + 1)
                        pe.wait_ge(filtered, n * TAPS + k + 1)
                        if k == 0:
                            pe.wait_ge(moved, n)
                        for j in range(4):
                            last = nc.tensor.matmul(pS[:, 128 * j:128 * j + 128], prod[:, k, 2 * j:2 * j + 2, :], g.ident[:],
                                                    is_transpose=True, start=(k == 0 and j == 0),
                                                    stop=(k == TAPS - 1 and j == 3))
                        last.then_inc(added, 1)
                        if k + NW < TAPS:
                            weigh(bp, hc, u, k + NW)
                        elif more:
                            weigh(bp, hc + 1, 1 - u, k + NW - TAPS)

                for bp in range(2):
                    reduce(bp, 0)
                    for k in range(NW):
                        weigh(bp, 0, 0, k)
                    chunks(pe, bp, body)

            @block.scalar
            def _(act):
                act.wait_ge(onesrow, 1)

                def relu(bp, hc, u):
                    n = bp * CPI + hc
                    act.wait_ge(reduced, n + 1)
                    if not starts(bp, hc):
                        act.wait_ge(parted, n)
                    nc.scalar.activation(yf[:], pY[:], ACT.Relu, bias=g.ysc[:, 7:8], scale=g.ysc[:, 6:7])
                    if bp > 0 or not (isinstance(hc, int) and hc < 2):
                        act.wait_ge(weighed, (n - 1) * TAPS)
                    nc.scalar.activation(ysb[u][0:3 * 2 * CR, :], pY[:], ACT.Relu, bias=g.ysc[:, 7:8],
                                         scale=g.ysc[:, 6:7]).then_inc(relued, 1)

                def body(bp, hc, u, more):
                    n = bp * CPI + hc
                    if more:
                        relu(bp, hc + 1, 1 - u)
                    act.wait_ge(added, (n + 1) * TAPS)
                    src = pS[:].rearrange("p (j b c) -> p b c j", j=4, b=2)
                    dst = g.hT[:].rearrange("p (b c h) r -> p b c (h r)", b=B, c=C)
                    nc.scalar.copy(dst[:, 2 * bp:2 * bp + 2, :, bass.ds(4 * hc, 4)], src).then_inc(moved, 1)

                for bp in range(2):
                    relu(bp, 0, 0)
                    chunks(act, bp, body)

            @block.vector
            def _(v):
                for k in range(TAPS):
                    _, dw, lo, hi = tap(k)
                    if dw:
                        edge = prod[:, k, :, 0:1] if dw < 0 else prod[:, k, :, HW - 1:HW]
                        nc.vector.memset(edge, 0.0)
                for n in range(2):
                    last = nc.vector.memset(ysb[n][3 * 2 * CR:YROWS, :].bitcast(F32), 1.0)
                last.then_inc(onesrow, 1)

                def body(bp, hc, u, more):
                    n = bp * CPI + hc
                    for k in range(TAPS):
                        dh, dw, lo, hi = tap(k)
                        v.wait_ge(weighed, n * TAPS + k + 1)
                        if not starts(bp, hc):
                            v.wait_ge(added, (n - 1) * TAPS + k + 1)
                        rows = g.img[:, bp, bass.ds(hc * CH + (1 + dh) * HW, CH)].rearrange("p (r w) -> p r w", w=HW)
                        nc.vector.tensor_tensor(prod[:, k, :, lo:hi], pW[k % NW][:, :, lo:hi],
                                                rows[:, :, lo + dw:hi + dw], ALU.mult).then_inc(filtered, 1)

                for bp in range(2):
                    chunks(v, bp, body)

            @block.gpsimd
            def _(pool):
                def part(bp, hc, u, more):
                    pool.wait_ge(relued, bp * CPI + hc + 1)
                    low = slice(2 * 2 * CR, 3 * 2 * CR)
                    nc.gpsimd.tensor_tensor(ysb[u][low], yf[low], ysb[u][low], ALU.subtract).then_inc(parted, 1)

                turned_steps, done = [0], [1]

                def double(k, d, lo, hi):
                    m = 2 ** k
                    pool.wait_ge(doubled, done[0])
                    for i in range(2):
                        nc.gpsimd.tensor_scalar(half[:, i, :, 0:hi - lo], g.tab[:, d, :, lo:hi], g.turn[:, k, i, d:d + 1],
                                                None, ALU.mult).then_inc(multiplied, 1)
                    turned_steps[0] += 2
                    pool.wait_ge(multiplied, turned_steps[0])
                    nc.gpsimd.tensor_tensor(g.tab[:, d, 0, m + lo:m + hi], half[:, 0, 0, 0:hi - lo],
                                            half[:, 1, 1, 0:hi - lo], ALU.subtract)
                    nc.gpsimd.tensor_tensor(g.tab[:, d, 1, m + lo:m + hi], half[:, 0, 1, 0:hi - lo],
                                            half[:, 1, 0, 0:hi - lo], ALU.add).then_inc(doubled, 1)
                    done[0] += 1

                nc.gpsimd.memset(g.tab[:, :, 0, 0:1], 1.0)
                nc.gpsimd.memset(g.tab[:, :, 1, 0:1], 0.0).then_inc(doubled, 1)
                pieces = [(k, d, lo, min(lo + PIECE, 2 ** k)) for k in range(QUADS.bit_length() - 1)
                          for lo in range(0, 2 ** k, PIECE) for d in range(2)]
                small = len(pieces) - (2 * CPI - 1)
                for n in range(2 * CPI):
                    pool.wait_ge(doubled, done[0])
                    part(n // CPI, n % CPI, n % 2, None)
                    pool.wait_ge(parted, n + 1)
                    for k, d, lo, hi in (pieces[:small + 1] if n == 0 else pieces[small + n:small + n + 1]):
                        double(k, d, lo, hi)


def layer_norm(nc, g, which):
    NP, W = NCH // 2, 2 * 8 + 2
    with ExitStack() as ctx:
        def sem(name):
            return ctx.enter_context(nc.semaphore(f"ln{which}_{name}"))

        def sb(name, shape):
            return ctx.enter_context(nc.sbuf_tensor(f"ln{which}_{name}", shape, F32))

        def ps(name, shape):
            return ctx.enter_context(nc.psum_tensor(f"ln{which}_p{name}", shape, F32))

        sq = [sb(f"sq{n}", [128, CH]) for n in range(2)]
        st = [sb(f"st{n}", [128, 4, 2 * F]) for n in range(2)]
        sq_cls, st_cls = sb("sqc", [128, B]), sb("stc", [B, 2 * F])
        var, root, guess, corr, factor = (sb(n, [128, W]) for n in ("var", "root", "guess", "corr", "factor"))
        pM = [ps(f"M{n}", [128, CH]) for n in range(2)]
        pV = ps("V", [128, W])
        pR = [ps(f"R{n}", [128, CH]) for n in range(2)]
        pX = ps("X", [128, B])
        weights_parted = sem("weights_parted")
        centered = sem("centered")
        squared = sem("squared")
        summed = sem("summed")
        kept = sem("kept")
        rooted = sem("rooted")
        newton = sem("newton")
        picked = sem("picked")
        spread = sem("spread")
        scaled = sem("scaled")
        cls_made = sem("cls_made")
        beside_set = sem("beside_set")
        STEPS = 5
        hflat = g.hT[:].rearrange("p a r -> p (a r)")
        uflat = g.uT[:].rearrange("p a r -> p (a r)")

        def pipeline(eng, turn):
            turn(0, (True, False, False))
            turn(1, (True, True, False))
            turn(2, (True, True, True))
            with eng.Fori(3, NP) as i:
                turn(i, (True, True, True))
            turn(NP, (False, True, True))
            turn(NP + 1, (False, False, True))

        def at_least(i, n):
            return not isinstance(i, int) or i >= n

        with nc.Block() as block:
            @block.tensor
            def _(pe):
                def center(i):
                    for n in range(2):
                        if at_least(i, 1):
                            pe.wait_ge(squared, 2 * i + n - 1)
                        nc.tensor.matmul(pM[n][:], g.center[:], hflat[:, bass.ds((2 * i + n) * CH, CH)],
                                         start=True, stop=True).then_inc(centered, 1)

                def spreads(i):
                    for n in range(2):
                        pe.wait_ge(picked, 2 * i + n + 1)
                        if at_least(i, 1):
                            pe.wait_ge(scaled, 2 * i + n - 1)
                        for j in range(4):
                            last = nc.tensor.transpose(pR[n][:, 128 * j:128 * j + 128], st[n][:, j, :], g.ident[:])
                        last.then_inc(spread, 1)

                def sums(i):
                    if at_least(i, 1):
                        pe.wait_ge(kept, i)
                    for n in range(2):
                        pe.wait_ge(squared, 2 * i + n + 1)
                        for j in range(4):
                            last = nc.tensor.matmul(pV[:, 8 * n + 2 * j:8 * n + 2 * j + 2], sq[n][:, 128 * j:128 * j + 128],
                                                    g.mean2[:], start=True, stop=True)
                    last.then_inc(summed, 1)

                def turn(i, stages):
                    if stages[0]:
                        center(i)
                    if stages[2]:
                        spreads(i - 2)
                    if stages[0]:
                        sums(i)

                nc.tensor.matmul(pX[:], g.center[:], g.hC[:], start=True, stop=True).then_inc(cls_made, 1)
                pe.wait_ge(cls_made, 2)
                nc.tensor.matmul(pV[0:B, W - 2:W], sq_cls[:], g.mean2[:], start=True, stop=True)
                pipeline(pe, turn)
                pe.wait_ge(cls_made, 3)
                nc.tensor.transpose(pX[:], st_cls[:], g.ident[0:B, 0:B]).then_inc(cls_made, 1)

            @block.scalar
            def _(act):
                def squares(i):
                    for n in range(2):
                        act.wait_ge(centered, 2 * i + n + 1)
                        if at_least(i, 1):
                            act.wait_ge(summed, i)
                        nc.scalar.copy(uflat[:, bass.ds((2 * i + n) * CH, CH)], pM[n][:])
                        nc.scalar.activation(sq[n][:], pM[n][:], ACT.Square).then_inc(squared, 1)

                def roots(i):
                    act.wait_ge(kept, i + 1)
                    nc.scalar.activation(root[:], var[:], ACT.Sqrt).then_inc(rooted, 1)

                def pick(i):
                    act.wait_ge(newton, STEPS * (i + 1))
                    if at_least(i, 1):
                        act.wait_ge(spread, 2 * i)
                    for n in range(2):
                        nc.scalar.copy(st[n][:].rearrange("p j (r f) -> p (j r) f", r=2),
                                       factor[:, 8 * n:8 * n + 8].unsqueeze(2).broadcast_to([128, 8, F])).then_inc(picked, 1)

                def turn(i, stages):
                    if stages[1]:
                        roots(i - 1)
                    if stages[0]:
                        squares(i)
                    if stages[1]:
                        pick(i - 1)

                act.wait_ge(cls_made, 1)
                nc.scalar.copy(g.uC[:], pX[:])
                nc.scalar.activation(sq_cls[:], pX[:], ACT.Square).then_inc(cls_made, 1)
                pipeline(act, turn)

            @block.vector
            def _(v):
                def keep(i):
                    v.wait_ge(summed, i + 1)
                    if isinstance(i, int) and i == 0:
                        nc.vector.memset(var[:, W - 2:W], 1.0).then_inc(beside_set, 1)
                        v.wait_ge(beside_set, 1)
                        nc.vector.tensor_scalar(var[0:B, W - 2:W], pV[0:B, W - 2:W], LN_EPS, None, ALU.add)
                    nc.vector.tensor_scalar(var[:, 0:W - 2], pV[:, 0:W - 2], LN_EPS, None, ALU.add).then_inc(kept, 1)

                def factors(i):
                    k = STEPS * i
                    v.wait_ge(rooted, i + 1)
                    nc.vector.reciprocal(guess[:], root[:]).then_inc(newton, 1)
                    v.wait_ge(newton, k + 1)
                    nc.vector.tensor_tensor(corr[:], guess[:], guess[:], ALU.mult).then_inc(newton, 1)
                    v.wait_ge(newton, k + 2)
                    nc.vector.tensor_tensor(corr[:], corr[:], var[:], ALU.mult).then_inc(newton, 1)
                    v.wait_ge(newton, k + 3)
                    nc.vector.tensor_scalar(corr[:], corr[:], -0.5, 1.5, ALU.mult, ALU.add).then_inc(newton, 1)
                    v.wait_ge(newton, k + 4)
                    nc.vector.tensor_tensor(factor[:], guess[:], corr[:], ALU.mult).then_inc(newton, 1)

                def apply(i):
                    for n in range(2):
                        v.wait_ge(spread, 2 * i + n + 1)
                        u = uflat[:, bass.ds((2 * i + n) * CH, CH)]
                        nc.vector.tensor_tensor(u, pR[n][:], u, ALU.mult).then_inc(scaled, 1)

                def turn(i, stages):
                    if stages[1]:
                        factors(i - 1)
                    if stages[2]:
                        apply(i - 2)
                    if stages[0]:
                        keep(i)

                pipeline(v, turn)
                v.wait_ge(newton, STEPS * NP)
                nc.vector.tensor_copy(st_cls[:].rearrange("p (r f) -> p r f", r=2),
                                      factor[0:B, W - 2:W].unsqueeze(2).broadcast_to([B, 2, F])).then_inc(cls_made, 1)
                v.wait_ge(cls_made, 4)
                nc.vector.tensor_tensor(g.uC[:], pX[:], g.uC[:], ALU.mult)

            if which == "2":
                @block.gpsimd
                def _(pool):
                    high, low = g.WdP
                    nc.gpsimd.tensor_copy(high[:], g.WdT[:]).then_inc(weights_parted, 1)
                    pool.wait_ge(weights_parted, 1)
                    nc.gpsimd.tensor_tensor(low[:], g.WdT[:], high[:], ALU.subtract)


def state_space(nc, g):
    HALVES = QUADS // CH
    STEPS = 2 * HALVES
    YPB = 2 * STEPS + 1
    with ExitStack() as ctx:
        def sem(name):
            return ctx.enter_context(nc.semaphore("ssm_" + name))

        def sb(name, shape):
            return ctx.enter_context(nc.sbuf_tensor("ssm_" + name, shape, F32))

        pV = [[ctx.enter_context(nc.psum_tensor(f"ssm_v{n}{t}", [128, CH], F32)) for t in range(2)] for n in range(2)]
        pY = [ctx.enter_context(nc.psum_tensor(f"ssm_y{n}", [128, CH], F32)) for n in range(4)]
        rot = [sb(f"rot{n}", [128, 2, CH]) for n in range(2)]
        z = [sb(f"z{n}", [128, CH]) for n in range(2)]
        zc = sb("zc", [128, 2, QUADS + 1])
        zs = sb("zs", [128, 2, QUADS + 1])
        act_y = [sb(f"gelu{n}", [128, CH]) for n in range(4)]
        act_c = sb("geluc", [F, 2])
        entered = sem("entered")
        x0_made = sem("x0_made")
        turned = sem("turned")
        freed = sem("freed")
        scanned = sem("scanned")
        stated = sem("stated")
        yielded = sem("yielded")
        gelued = sem("gelued")
        summed = sem("summed")
        cls_y, cls_g, cls_a = sem("cls_y"), sem("cls_g"), sem("cls_a")
        start = sem("start")

        def part(d, h):
            return (h if d == FWD else HALVES - 1 - h) * CH

        def cols(t, b, d, h, q):
            return t[:, bass.ds(b * QUADS + part(d, h), CH), q]

        def scan_order(a, d):
            return a if d == FWD else a[:, ::-1]

        def before(t, d, h):
            a = part(d, h) + (0 if d == FWD else 1)
            return t[:, d, a:a + CH]

        def after(t, d, h):
            a = part(d, h) + (1 if d == FWD else 0)
            return scan_order(t[:, d, a:a + CH], d)

        ORDER = [(d, h) for d in (FWD, BWD) for h in range(HALVES)]
        LVI = {FWD: ((0, 1), (2, 3)), BWD: ((4, 5), (6, 7))}

        with nc.Block() as block:
            @block.tensor
            def _(pe):
                def enter(b, s, wait):
                    d, h = ORDER[s]
                    if wait:
                        pe.wait_ge(freed, b * STEPS + s - 1)
                    for t in range(2):
                        out = pV[s % 2][t]
                        carry = d == FWD and h == 0
                        for q in range(2):
                            last = nc.tensor.matmul(out[:], g.LV[:, LVI[d][t][q], :], cols(g.uT, b, d, h, q),
                                                    start=(q == 0), stop=(q == 1 and not carry))
                        if carry:
                            last = nc.tensor.matmul(out[:, 0:1], g.LV[:, (LV_CARRY, LV_CARRY_TURNED)[t], :], g.uC[:, 0:1],
                                                    start=False, stop=True)
                    last.then_inc(entered, 1)

                def leave(b, s):
                    d, h = ORDER[s]
                    for q in range(2):
                        n = 2 * s + q
                        out = pY[n % 4][:]
                        if isinstance(b, int) and b == 0:
                            if n >= 4:
                                pe.wait_ge(gelued, n - 3)
                        else:
                            pe.wait_ge(gelued, b * YPB + (n - 3 if n >= 4 else (0 if n == 0 else n - 4)))
                        nc.tensor.matmul(out, g.KI[:, d, 0, :, :], cols(g.uT, b, d, h, q), start=True, stop=False)
                        if q == (1 if d == FWD else 0):
                            nc.tensor.matmul(out, g.KI[:, d, 1, :, :], cols(g.uT, b, d, h, 1 - q), start=False, stop=False)
                        if q == 0:
                            pe.wait_ge(stated, b * STEPS + s + 1)
                        first = 1 + 2 * q if d == FWD else 2 * q
                        nc.tensor.matmul(out, g.N1[:, d, first:first + 2, :], before(zc, d, h),
                                         start=False, stop=False)
                        nc.tensor.matmul(out, g.N2[:, d, first:first + 2, :], before(zs, d, h),
                                         start=False, stop=True).then_inc(yielded, 1)

                def leave_class(b):
                    out = pY[0][0:F, 0:1]
                    pe.wait_ge(gelued, b * YPB + 2 * STEPS - 3)
                    nc.tensor.matmul(out, g.KI[:, BWD, 0, 0, :], g.uC[:, 0:1], start=True, stop=False)
                    nc.tensor.matmul(out, g.N1[:, BWD, 3, :], zc[:, BWD, 0:1], start=False, stop=False)
                    nc.tensor.matmul(out, g.N2[:, BWD, 3, :], zs[:, BWD, 0:1],
                                     start=False, stop=True).then_inc(yielded, 1)

                def batch(b, more):
                    for s in range(STEPS):
                        if s + 1 < STEPS:
                            enter(b, s + 1, not (isinstance(b, int) and b == 0 and s + 1 < 2))
                        elif more:
                            enter(b + 1, 0, True)
                        leave(b, s)
                    leave_class(b)

                nc.tensor.matmul(pY[0][:, 0:1], g.LV[:, LV_FIRST, :], g.uC[:, 0:1], start=True, stop=True)
                nc.tensor.matmul(pY[1][0:F, 0:1], g.KI[:, FWD, 0, 0, :], g.uC[:, 0:1],
                                 start=True, stop=True).then_inc(cls_y, 1)
                enter(0, 0, False)
                pe.wait_ge(cls_g, 2)
                batch(0, True)
                with pe.Fori(1, B - 1) as b:
                    batch(b, True)
                batch(B - 1, False)

            @block.vector
            def _(v):
                nc.vector.memset(zc[:, BWD, QUADS:], 0.0)
                nc.vector.memset(zs[:, BWD, QUADS:], 0.0)
                nc.vector.memset(zs[:, FWD, 0:1], 0.0).then_inc(start, 1)

                def step(b, s, n0):
                    d, h = ORDER[s]
                    n = b * STEPS + s
                    r, zz = rot[s % 2], z[s % 2]
                    cos, sin = (g.tab[:, d, k, h * CH:(h + 1) * CH] for k in range(2))
                    v.wait_ge(entered, n + 1)
                    nc.vector.tensor_tensor(r[:, 0, :], scan_order(pV[s % 2][0][:], d), cos, ALU.mult)
                    nc.vector.tensor_tensor(r[:, 1, :], scan_order(pV[s % 2][1][:], d), sin, ALU.mult).then_inc(freed, 1)
                    v.wait_ge(freed, n + 1)
                    nc.vector.tensor_tensor(r[:, 0, :], r[:, 0, :], r[:, 1, :], ALU.add).then_inc(turned, 1)
                    v.wait_ge(turned, n + 1)
                    initial = 0.0 if h == 0 else z[(s - 1) % 2][:, CH - 1:CH]
                    nc.vector.tensor_tensor_scan(zz[:], g.decay[:, d:d + 1].broadcast_to([128, CH]), r[:, 0, :], initial,
                                                 ALU.mult, ALU.add).then_inc(scanned, 1)
                    v.wait_ge(scanned, n + 1)
                    if not n0:
                        v.wait_ge(yielded, (b - 1) * YPB + min(2 * (s + 2), YPB) if s % 2 == 0 else (b - 1) * YPB + min(2 * (s + 1) + 1, YPB))
                    nc.vector.tensor_tensor(after(zc, d, h), zz[:], cos, ALU.mult)
                    nc.vector.tensor_tensor(after(zs, d, h), zz[:], sin, ALU.mult).then_inc(stated, 1)

                v.wait_ge(cls_g, 2)
                v.wait_ge(start, 1)
                for s in range(STEPS):
                    step(0, s, True)
                with v.Fori(1, B) as b:
                    for s in range(STEPS):
                        step(b, s, False)

            @block.scalar
            def _(act):
                act.wait_ge(cls_y, 1)
                nc.scalar.copy(zc[:, FWD, 0:1], pY[0][:, 0:1]).then_inc(cls_g, 1)
                nc.scalar.activation(act_c[:, 0:1], pY[1][0:F, 0:1], ACT.Gelu).then_inc(cls_g, 1)

                def batch(b, first):
                    for n in range(YPB):
                        act.wait_ge(yielded, b * YPB + n + 1)
                        if n < YPB - 1:
                            if first:
                                if n >= 4:
                                    act.wait_ge(summed, n - 3)
                            else:
                                act.wait_ge(summed, b * YPB + n - 3 - (1 if n < 4 else 0))
                            nc.scalar.activation(act_y[n % 4][:], pY[n % 4][:], ACT.Gelu).then_inc(gelued, 1)
                        else:
                            if not first:
                                act.wait_ge(summed, b * YPB)
                            nc.scalar.activation(act_c[:, 1:2], pY[0][0:F, 0:1], ACT.Gelu).then_inc(gelued, 1)

                batch(0, True)
                with act.Fori(1, B) as b:
                    batch(b, False)

            @block.gpsimd
            def _(pool):
                pool.wait_ge(cls_g, 2)
                nc.gpsimd.tensor_tensor(g.hC[0:F, :], g.hC[0:F, :], act_c[:, 0:1].broadcast_to([F, B]), ALU.add).then_inc(cls_a, 1)
                pool.wait_ge(cls_a, 1)

                def batch(b):
                    for n in range(YPB):
                        pool.wait_ge(gelued, b * YPB + n + 1)
                        if n < YPB - 1:
                            d, h = ORDER[n // 2]
                            if n == 2 * HALVES:
                                pool.wait_ge(summed, b * YPB + n)
                            t = cols(g.hT, b, d, h, n % 2)
                            nc.gpsimd.tensor_tensor(t, t, act_y[n % 4][:], ALU.add).then_inc(summed, 1)
                        else:
                            c = g.hC[0:F, bass.ds(b, 1)]
                            nc.gpsimd.tensor_tensor(c, c, act_c[:, 1:2], ALU.add).then_inc(summed, 1)

                for b in range(B):
                    batch(b)


def experts(nc, g):
    TILES = CH // 128
    with ExitStack() as ctx:
        def sem(name):
            return ctx.enter_context(nc.semaphore("ex_" + name))

        def sb(name, shape, dt=F32):
            return ctx.enter_context(nc.sbuf_tensor("ex_" + name, shape, dt))

        def ps(name, shape):
            return ctx.enter_context(nc.psum_tensor("ex_p" + name, shape, F32))

        pH = [ps(f"H{n}", [128, CH]) for n in range(2)]
        pE = [ps(f"E{n}", [128, EX, F]) for n in range(2)]
        pL = [ps(f"L{n}", [128, TILES, EX]) for n in range(2)]
        pR = ps("R", [128, TILES, 128])
        hidf = [sb(f"hidf{n}", [128, 2, CH]) for n in range(2)]
        hid = [[sb(f"hid{n}{t}", [128, 2, CH], F32R) for t in range(2)] for n in range(2)]
        hst = sb("hst", [128, CH])
        gl = sb("gl", [128, 5, TILES, EX])
        gs = sb("gs", [128, 4, TILES])
        ms = [sb(f"ms{n}", [128, EX, F]) for n in range(2)]
        s4 = [sb(f"s4{n}", [128, 4, F]) for n in range(2)]
        s2 = [sb(f"s2{n}", [128, 2, F]) for n in range(2)]
        picked = [sb(f"picked{n}", [128, TILES, F]) for n in range(2)]
        res = [sb(f"res{n}", [128, TILES, 2, F]) for n in range(2)]
        clsr = sb("clsr", [B, F])
        hidden = sem("hidden")
        gelued = sem("gelued")
        parted = sem("parted")
        staged = sem("staged")
        rested = sem("rested")
        gated = sem("gated")
        tanhed = sem("tanhed")
        dv = sem("dv")
        spoke = sem("spoke")
        chosen = sem("chosen")
        pl = sem("pl")
        reduced = sem("reduced")
        finished = sem("finished")
        stored = [sem(f"stored{n}") for n in range(2)]
        cls_sem = sem("cls")
        GATE = 12
        uflat = g.uT[:].rearrange("p a r -> p (a r)")
        hflat = g.hT[:].rearrange("p a r -> p (a r)")
        bd2, bg2 = g.bias2[:, 0:EX * F], g.bias2[:, EX * F:]

        def gate(v, logits, base, P, T, tanh):
            G = lambda n: gl[0:P, n, 0:T, :]
            s = lambda n: gs[0:P, n, 0:T]
            wide = lambda a: a.unsqueeze(2).broadcast_to([P, T, EX])
            k = [0]

            def link(ins):
                k[0] += 1
                ins.then_inc(dv, 1)
                v.wait_ge(dv, base + k[0])

            link(nc.vector.tensor_reduce(s(0), logits, AX.X, ALU.max))
            k[0] += 1
            nc.vector.tensor_tensor(G(0), logits, wide(s(0)), ALU.subtract).then_inc(dv, 1)
            v.wait_ge(dv, base + k[0])
            link(nc.vector.tensor_scalar(G(1), G(0), 0.0, None, ALU.is_ge))
            link(nc.vector.tensor_tensor(G(1), G(1), g.rank[0:P, :].unsqueeze(1).broadcast_to([P, T, EX]), ALU.mult))
            link(nc.vector.tensor_reduce(s(1), G(1), AX.X, ALU.max))
            link(nc.vector.tensor_tensor(G(1), G(1), wide(s(1)), ALU.is_equal))
            v.wait_ge(tanhed, tanh)
            link(nc.vector.tensor_scalar(G(3), G(2), -0.5, 0.5, ALU.mult, ALU.add))
            link(nc.vector.reciprocal(G(3), G(3)))
            link(nc.vector.tensor_reduce(s(2), G(3), AX.X, ALU.add))
            link(nc.vector.tensor_scalar(s(2), s(2), -float(EX), None, ALU.add))
            link(nc.vector.reciprocal(s(3), s(2)))
            link(nc.vector.tensor_tensor(G(4), G(1), wide(s(3)), ALU.mult))
            assert k[0] == GATE


        with nc.Block() as block:
            @block.tensor
            def _(pe):
                def hide(i, par, first):
                    n = 2 * i + par
                    for h in range(2):
                        if not first:
                            pe.wait_ge(gelued, 2 * (n - 1) + h + 1)
                        nc.tensor.matmul(pH[h][:], g.W1z[:, par, 128 * h:128 * h + 128], uflat[:, bass.ds(i * CH, CH)],
                                         start=True, stop=True).then_inc(hidden, 1)

                def rest(i, first):
                    pe.wait_ge(staged, i + 1)
                    if not first:
                        pe.wait_ge(finished, 2 * i)
                    for j in range(TILES):
                        last = nc.tensor.transpose(pR[:, j, :], hst[:, 128 * j:128 * j + 128], g.ident[:])
                    last.then_inc(rested, 1)

                def project(o, par, start, P):
                    nc.tensor.matmul(o, g.ones2[:, 0:P], bd2, start=True, stop=False)
                    for h in range(2):
                        for value, weight in ((0, 0), (0, 1), (1, 0)):
                            last = nc.tensor.matmul(o, hid[par][value][:, h, start:start + P], g.WdP[weight][:, h],
                                                    start=False, stop=(h == 1 and value == 1))
                    return last

                def gates(i, par, first):
                    n = 2 * i + par
                    pe.wait_ge(gelued, 2 * n + 2)
                    if not first:
                        pe.wait_ge(dv, (n - 1) * GATE)
                    nc.tensor.matmul(pL[par][:], g.ones2[:], bg2, start=True, stop=True)
                    for j in range(TILES):
                        for h in range(2):
                            last = nc.tensor.matmul(pL[par][:, j, :], hidf[par][:, h, 128 * j:128 * j + 128], g.WgT[:, h, :],
                                                    start=False, stop=(h == 1), skip_group_check=True)
                    last.then_inc(gated, 1)

                def speak(i, par, first):
                    n = 2 * i + par
                    pe.wait_ge(parted, n + 1)
                    for j in range(TILES):
                        if not (first and j < 2):
                            pe.wait_ge(chosen, n * TILES + j - 1)
                        project(pE[j % 2][:], par, 128 * j, 128).then_inc(spoke, 1)

                def chunk(i, first, more):
                    gates(i, 0, first)
                    hide(i, 1, False)
                    speak(i, 0, first)
                    gates(i, 1, False)
                    rest(i, first)
                    if more:
                        hide(i + 1, 0, False)
                    speak(i, 1, False)

                hide(0, 0, True)
                chunk(0, True, True)
                with pe.Fori(1, NCH - 1) as i:
                    chunk(i, False, True)
                chunk(NCH - 1, False, False)
                pe.wait_ge(gelued, 4 * NCH)
                for h in range(2):
                    nc.tensor.matmul(pH[h][:, 0:B], g.W1z[:, 0, 128 * h:128 * h + 128], g.uC[:],
                                     start=True, stop=True).then_inc(hidden, 1)
                pe.wait_ge(parted, 2 * NCH + 1)
                pe.wait_ge(finished, 2 * NCH)
                nc.tensor.matmul(pL[0][0:B, 0, :], g.ones2[:, 0:B], bg2[:, 0:EX], start=True, stop=False)
                for h in range(2):
                    last = nc.tensor.matmul(pL[0][0:B, 0, :], hidf[0][:, h, 0:B], g.WgT[:, h, :], start=False, stop=(h == 1))
                last.then_inc(gated, 1)
                project(pE[0][0:B], 0, 0, B).then_inc(spoke, 1)
                nc.tensor.transpose(pR[0:B, 0, :], g.hC[:], g.ident[:]).then_inc(rested, 1)

            @block.scalar
            def _(act):
                def stage(i):
                    act.wait_ge(rested, i)
                    nc.scalar.copy(hst[:], hflat[:, bass.ds(i * CH, CH)]).then_inc(staged, 1)

                def gelu(n, par, cols, first):
                    for h in range(2):
                        act.wait_ge(hidden, 2 * n + h + 1)
                        if not first:
                            act.wait_ge(spoke, (n - 1) * TILES)
                        for o in (hidf[par], hid[par][0]):
                            last = nc.scalar.activation(o[:, h, 0:cols], pH[h][:, 0:cols], ACT.Gelu, bias=g.b1c[:, h:h + 1])
                        last.then_inc(gelued, 1)

                def tanh(i, par):
                    n = 2 * i + par
                    act.wait_ge(dv, n * GATE + 2)
                    nc.scalar.activation(gl[:, 2], gl[:, 0], ACT.Tanh, scale=0.5).then_inc(tanhed, 1)

                def chunk(i, first, more):
                    stage(i)
                    tanh(i, 0)
                    gelu(2 * i + 1, 1, CH, first)
                    tanh(i, 1)
                    if more:
                        gelu(2 * i + 2, 0, CH, False)

                gelu(0, 0, CH, True)
                chunk(0, True, True)
                with act.Fori(1, NCH - 1) as i:
                    chunk(i, False, True)
                chunk(NCH - 1, False, False)
                gelu(2 * NCH, 0, B, False)
                act.wait_ge(dv, 2 * NCH * GATE + 2)
                nc.scalar.activation(gl[0:B, 2, 0:1], gl[0:B, 0, 0:1], ACT.Tanh, scale=0.5).then_inc(tanhed, 1)

            @block.vector
            def _(v):
                def part(n, par, cols):
                    v.wait_ge(gelued, 2 * n + 2)
                    nc.vector.tensor_tensor(hid[par][1][:, :, 0:cols], hidf[par][:, :, 0:cols], hid[par][0][:, :, 0:cols],
                                            ALU.subtract).then_inc(parted, 1)

                def finish(n, m, par, stores):
                    v.wait_ge(reduced, (n + 1) * TILES)
                    if par == 0:
                        v.wait_ge(rested, stores[0])
                        if stores[1] is not None:
                            v.wait_ge(stored[m], stores[1])
                    nc.vector.tensor_tensor(res[m][:, :, par, :], pR[:, :, F * par:F * par + F], picked[par][:],
                                            ALU.add).then_inc(finished, 1)

                def two(k, first, last):
                    for m in range(2):
                        for par in range(2):
                            i = 2 * k + m
                            n = 2 * i + par
                            begins, ends = first and m == 0 and par == 0, last and m == 1 and par == 1
                            v.wait_ge(gated, n + 1)
                            gate(v, pL[par][:], n * GATE, 128, TILES, n + 1)
                            for j in range(TILES):
                                v.wait_ge(spoke, n * TILES + j + 1)
                                if not (begins and j < 2):
                                    v.wait_ge(reduced, n * TILES + j - 1)
                                nc.vector.tensor_tensor(ms[j % 2][:], pE[j % 2][:],
                                                        gl[:, 4, j, :].unsqueeze(2).broadcast_to([128, EX, F]),
                                                        ALU.mult).then_inc(chosen, 1)
                                if j == 0 and not begins:
                                    finish(n - 1, m if par else 1 - m, 1 - par, (i + 1, None if first else 16 * k))
                                if j == 1 and not ends:
                                    part(n + 1, 1 - par, CH)

                part(0, 0, CH)
                two(0, True, False)
                with v.Fori(1, NCH // 2 - 1) as k:
                    two(k, False, False)
                two(NCH // 2 - 1, False, True)
                finish(2 * NCH - 1, 1, 1, None)
                part(2 * NCH, 0, B)
                v.wait_ge(gated, 2 * NCH + 1)
                gate(v, pL[0][0:B, 0:1, :], 2 * NCH * GATE, B, 1, 2 * NCH + 1)
                v.wait_ge(spoke, 2 * NCH * TILES + 1)
                nc.vector.tensor_tensor(ms[0][0:B], pE[0][0:B], gl[0:B, 4, 0, :].unsqueeze(2).broadcast_to([B, EX, F]), ALU.mult).then_inc(chosen, 1)
                v.wait_ge(reduced, 2 * NCH * TILES + 1)
                v.wait_ge(rested, NCH + 1)
                nc.vector.tensor_tensor(clsr[:], pR[0:B, 0, 0:F], picked[0][0:B, 0, :], ALU.add).then_inc(finished, 1)

            @block.gpsimd
            def _(pool):
                def tile(n, j, slot, par, P):
                    pool.wait_ge(chosen, n + 1)
                    m = ms[slot][0:P]
                    nc.gpsimd.tensor_tensor(s4[slot][0:P], m[:, 0:4], m[:, 4:8], ALU.add).then_inc(pl, 1)
                    pool.wait_ge(pl, 2 * n + 1)
                    nc.gpsimd.tensor_tensor(s2[slot][0:P], s4[slot][0:P, 0:2], s4[slot][0:P, 2:4], ALU.add).then_inc(pl, 1)
                    pool.wait_ge(pl, 2 * n + 2)
                    nc.gpsimd.tensor_tensor(picked[par][0:P, j, :], s2[slot][0:P, 0], s2[slot][0:P, 1], ALU.add).then_inc(reduced, 1)

                def unit(i, par, first):
                    n = 2 * i + par
                    if not first:
                        pool.wait_ge(finished, n - 1)
                    for j in range(TILES):
                        tile(n * TILES + j, j, j % 2, par, 128)

                for par in range(2):
                    unit(0, par, True)
                with pool.Fori(1, NCH) as i:
                    for par in range(2):
                        unit(i, par, False)
                tile(2 * NCH * TILES, 0, 0, 0, B)

            @block.sync
            def _(sp):
                rows = g.out[:, 1:, :].rearrange("b (q j p r) c -> b q p j (r c)", q=4, j=TILES, p=128, r=2)
                with sp.Fori(0, B) as b:
                    for q in range(4):
                        sp.wait_ge(finished, 8 * b + 2 * q + 2)
                        sp.dma_start(rows[bass.ds(b, 1), q].rearrange("b p j x -> (b p) j x"),
                                     res[q % 2][:].rearrange("p j r c -> p j (r c)")).then_inc(stored[q % 2], 16)
                sp.wait_ge(finished, 2 * NCH + 1)
                sp.dma_start(g.out[:, 0, :], clsr[:]).then_inc(cls_sem, 16)
                sp.wait_ge(cls_sem, 16)
                for n in range(2):
                    sp.wait_ge(stored[n], 16 * NCH // 2)


SSM_NAMES = ["log_real", "imag", "log_Delta", "B_real", "B_imag", "C_real", "C_imag", "D"]
_INS = (["x", "cls_tok"]
        + ["L0_tok_" + n for n in ("conv1_w", "conv1_b", "bn_gamma", "bn_beta", "bn_mean", "bn_var", "conv2_w", "conv2_b")]
        + ["L0_attn_fwd_" + n for n in SSM_NAMES] + ["L0_attn_bwd_" + n for n in SSM_NAMES]
        + ["L0_ffn_" + n for n in ("W1", "b1", "Wg", "bg", "Wd", "bd")])
_OUT = (B, C * HW + 1, F)


def kernel(**inputs):
    import concourse.bacc as bacc
    from concourse.bass_utils import run_bass_kernel_spmd

    nc = bacc.Bacc("TRN2", target_bir_lowering=False, num_devices=1)
    arrays, aps = {}, []
    for name in _INS:
        a = np.ascontiguousarray(inputs[name])
        arrays["in_" + name] = a
        aps.append(nc.dram_tensor("in_" + name, a.shape, mybir.dt.from_np(a.dtype), kind="ExternalInput").ap())
    out = nc.dram_tensor("out_0", _OUT, F32, kind="ExternalOutput").ap()
    vit_tower(nc, aps, out)
    r = run_bass_kernel_spmd(nc, [arrays], core_ids=[0])
    return r.results[0]["out_0"]
```

```python
from contextlib import ExitStack

import numpy as np
import concourse.bass as bass
from concourse import mybir

ALU = mybir.AluOpType
ACT = mybir.ActivationFunctionType
AX = mybir.AxisListType
F32 = mybir.dt.float32
F32R = mybir.dt.float32r

B, C, HW = 4, 64, 64
CR, TAPS = 16, 9
F = HW
NS = 64
HID, EX = 256, 8
PAIRS = C * HW // 2
CH = 512
NCH = B * PAIRS // CH
QUADS = PAIRS // 2
GRP = 4
PROW = (HW + 2) * HW
BN_EPS = LN_EPS = 1e-5
FWD, BWD = 0, 1
PARTS = ((0, 0), (0, 1), (1, 0))
YROWS = 3 * 2 * CR + 2


class Tower:

    def __init__(self, nc, ctx, arrays, out):
        (self.x, self.cls_tok, self.conv1_w, self.conv1_b, self.bn_gamma, self.bn_beta, self.bn_mean, self.bn_var,
         self.conv2_w, self.conv2_b) = arrays[:10]
        self.ssm_f, self.ssm_b = arrays[10:18], arrays[18:26]
        self.W1, self.b1, self.Wg, self.bg, self.Wd, self.bd = arrays[26:]
        self.out = out

        def sb(name, shape, dt=F32):
            return ctx.enter_context(nc.sbuf_tensor(name, shape, dt))

        self.hT = sb("hT", [128, B * QUADS, 2])
        self.hC = sb("hC", [128, B])
        self.uC = sb("uC", [128, B])
        self.ident = sb("ident", [128, 128])
        self.center = sb("center", [128, 128])
        self.mean2 = sb("mean2", [128, 2])
        self.LV = [sb(f"LV{n}", [128, 11, 128], F32R) for n in range(2)]
        self.N = [sb(f"N{n}", [128, 2, 2, 5, F], F32R) for n in range(2)]
        self.KI = [sb(f"KI{n}", [128, 2, 2, 2, F], F32R) for n in range(2)]
        self.decay = sb("decay", [128, 2])
        self.tab = sb("tab", [128, 2, 2, QUADS])
        self.W1z = sb("W1z", [128, 2, HID])
        self.b1c = sb("b1c", [128, 2])
        self.WgT = sb("WgT", [128, 2, EX])
        self.WdT = sb("WdT", [128, 2, EX, F])
        self.bias2 = sb("bias2", [2, EX * F], F32R)
        self.bgc = sb("bgc", [2 * EX, 1])
        self.ones2 = sb("ones2", [2, 128], F32R)
        self.rank = sb("rank", [128, EX])


    def add_norm(self, nc, ctx):
        self.u = [ctx.enter_context(nc.sbuf_tensor(f"u{n}", [128, B * QUADS, 2], F32R)) for n in range(2)]

    def add_weights(self, nc, ctx):
        self.W1P = [ctx.enter_context(nc.sbuf_tensor(f"W1P{n}", [128, 2, HID], F32R)) for n in range(2)]
        self.WgP = [ctx.enter_context(nc.sbuf_tensor(f"WgP{n}", [128, 2, 2, EX], F32R)) for n in range(2)]
        self.WdP = [ctx.enter_context(nc.sbuf_tensor(f"WdP{n}", [128, 2, EX, F], F32R)) for n in range(2)]


class Matrices:

    def __init__(self, nc, ctx):
        def sb(name, shape):
            return ctx.enter_context(nc.sbuf_tensor("m_" + name, shape, F32))

        self.img = sb("img", [128, 2, PROW])
        self.conv1L = sb("conv1L", [128, 3, 2 * CR])
        self.conv2L = ctx.enter_context(nc.sbuf_tensor("m_conv2L", [YROWS, TAPS, 128], F32R))
        self.ysc = sb("ysc", [3 * 2 * CR, 8])
        self.raw = sb("raw", [128, 4, 2])
        self.Bm = sb("Bm", [128, 2, 2, F])
        self.S = sb("S", [128, 40, 2])
        self.turn = sb("turn", [128, 10, 2, 2])
        self.M = sb("M", [128, 2, 2, 6, F])
        self.M0 = sb("M0", [128, 2, 2, F])
        self.by_re = sb("by_re", [128, 2, F])
        self.by_im = sb("by_im", [128, 2, F])
        self.half = sb("half", [128, 2, 2, QUADS // 2])
        self.bfull = sb("bfull", [2, EX * F])
        self.bpart = ctx.enter_context(nc.sbuf_tensor("m_bpart", [2, 2, EX * F], F32R))
        self.bsel = sb("bsel", [2, 2, EX * F])
        self.ffn_in = ctx.enter_context(nc.semaphore("ffn_in"))
        self.b_in = ctx.enter_context(nc.semaphore("b_in"))
        self.N = sb("N", [128, 2, 2, 5, F])


def vit_tower(nc, arrays, out):
    with ExitStack() as ctx:
        g = Tower(nc, ctx, arrays, out)
        with ExitStack() as making:
            m = Matrices(nc, making)
            setup(nc, g, m)
            involution(nc, g, m)
            matrices(nc, g, m)
        g.add_norm(nc, ctx)
        layer_norm(nc, g, "1")
        state_space(nc, g)
        g.add_weights(nc, ctx)
        layer_norm(nc, g, "2")
        experts(nc, g)


def setup(nc, g, m):
    with ExitStack() as ctx:
        def sb(name, shape, dt=F32):
            return ctx.enter_context(nc.sbuf_tensor("s0_" + name, shape, dt))

        def ps(name, shape):
            return ctx.enter_context(nc.psum_tensor("p0_" + name, shape, F32))

        def sem(name):
            return ctx.enter_context(nc.semaphore("s0_" + name))

        rows = sb("rows", [8, 2, NS])
        Cin = sb("Cin", [F, 2, 3, NS])
        sgn = sb("sgn", [128, 1])
        w1o = sb("w1o", [CR, C])
        wk = sb("wk", [TAPS, CR + 1])
        w1d = sb("w1d", [CR, 2, C])
        wkd = sb("wkd", [TAPS, YROWS])
        bn5 = sb("bn5", [CR, 5])
        spread6 = sb("spread6", [CR, 6, CR])
        w2 = sb("w2", [YROWS, TAPS])
        w2p = sb("w2p", [YROWS, 2, TAPS], F32R)
        w2s = sb("w2s", [YROWS, TAPS])
        own = sb("own", [YROWS, 2])
        pC = ps("C", [128, 4, F])
        pS = ps("S", [128, 4, 2])
        pA = ps("A", [128, CR])
        pB = ps("B", [YROWS, TAPS])
        pN = ps("N", [3 * 2 * CR, 5])

        img_in = sem("img_in")
        ssm_in = sem("ssm_in")
        c_in = sem("c_in")
        conv_in = sem("conv_in")
        pool_const = sem("pool_const")
        dve = sem("dve")
        exped = sem("exped")
        sined = sem("sined")
        ssm_turned = sem("ssm_turned")
        c_turned = sem("c_turned")
        w_spread = sem("w_spread")
        consts = {}
        img, raw, S = m.img, m.raw, m.S

        with nc.Block() as block:
            vec = nc.vector
            steps = [0]

            def count(name):
                consts[name] = steps[0]

            @block.vector
            def _(v):
                def link(ins):
                    steps[0] += 1
                    ins.then_inc(dve, 1)
                    v.wait_ge(dve, steps[0])

                def tt(o, a, b, op):
                    link(vec.tensor_tensor(o, a, b, op))

                def ts(o, a, s1, s2, op0, op1=ALU.bypass):
                    link(vec.tensor_scalar(o, a, s1, s2, op0, op1) if s2 is not None
                         else vec.tensor_scalar(o, a, s1, None, op0))

                def stt(o, a, s, b, op0, op1):
                    link(vec.scalar_tensor_tensor(out=o, in0=a, scalar=s, in1=b, op0=op0, op1=op1))

                def copy(o, a):
                    link(vec.tensor_copy(o, a))

                def fill(o, c):
                    link(vec.memset(o, c))

                fill(sgn[0:64], 1.0)
                fill(sgn[64:128], -1.0)
                fill(g.ones2[:].bitcast(F32), 1.0)
                fill(g.mean2[:], 0.0)
                fill(g.mean2[0:64, 0:1], 1.0 / F)
                fill(g.mean2[64:128, 1:2], 1.0 / F)
                fill(m.M[:, :, :, 5, :], 0.0)
                fill(m.conv1L[:], 0.0)
                fill(own[:], 1.0)
                v.wait_ge(pool_const, POOL_CONST)
                copy(spread6[:], g.ident[0:CR, 0:CR].unsqueeze(1).broadcast_to([CR, 6, CR]))
                link(vec.tensor_reduce(own[0:96], g.ident[0:96, 0:96].rearrange("p (r i o) -> p i r o", r=3, i=2),
                                       AX.XY, ALU.add))
                copy(g.center[:], g.ident[:])
                for h in range(2):
                    s = slice(64 * h, 64 * h + 64)
                    ts(g.center[s, s], g.ident[s, s], -1.0 / F, None, ALU.add)
                v.wait_ge(conv_in, 16 * 8)
                copy(w1d[:], w1o[:].unsqueeze(1).broadcast_to([CR, 2, C]))
                copy(wkd[:, 0:6 * CR].rearrange("k (r o) -> k r o", r=6), wk[:, 0:CR].unsqueeze(1).broadcast_to([TAPS, 6, CR]))
                copy(wkd[:, 6 * CR:], wk[:, CR:].broadcast_to([TAPS, 2]))
                count("conv_laid")
                v.wait_ge(ssm_in, 16 * 8)
                copy(rows[:, 1, :], rows[:, 0, :])
                count("ssm_laid")
                v.wait_ge(w_spread, 1)
                copy(m.ysc[:, 0:5], pN[:])
                cb, ga, be, mu, va = (m.ysc[:, n:n + 1] for n in range(5))
                ts(m.ysc[:, 5:6], va, BN_EPS, None, ALU.add)
                count("bnvar")
                copy(w2[:], pB[:])
                for b2 in range(2):
                    r = slice(C * b2, C * b2 + C)
                    copy(m.conv1L[r, :, CR * b2:CR * b2 + CR], pA[r, :].unsqueeze(1).broadcast_to([C, 3, CR]))
                copy(w2p[:, 0, :], w2[:])
                tt(w2p[:, 1, :], w2[:], w2p[:, 0, :], ALU.subtract)
                copy(w2s[:], w2p[:, 0, :])
                copy(w2s[32:64], w2p[32:64, 1, :])
                b2 = slice(3 * 2 * CR, YROWS)
                ts(w2s[b2], w2p[b2, 0, :], g.ident[b2, 96:97], None, ALU.mult)
                stt(w2s[b2], w2p[b2, 1, :], g.ident[b2, 97:98], w2s[b2], ALU.mult, ALU.add)
                for i in range(2):
                    ts(m.conv2L[:, :, C * i:C * i + C], w2s[:].unsqueeze(2).broadcast_to([YROWS, TAPS, C]),
                       own[:, i:i + 1], None, ALU.mult)
                v.wait_ge(sined, 1)
                link(vec.reciprocal(m.ysc[:, 7:8], m.ysc[:, 6:7]))
                tt(m.ysc[:, 6:7], ga, m.ysc[:, 7:8], ALU.mult)
                tt(m.ysc[:, 7:8], cb, mu, ALU.subtract)
                stt(m.ysc[:, 7:8], m.ysc[:, 7:8], m.ysc[:, 6:7], be, ALU.mult, ALU.add)
                s = lambda n: S[:, n, :]
                v.wait_ge(ssm_turned, 1)
                copy(raw[:], pS[:])
                count("raw")
                imag = raw[:, 1, :]
                v.wait_ge(exped, 2)
                stt(s(2), s(0), -1.0, s(1), ALU.mult, ALU.mult)
                count("ad")
                tt(s(3), imag, s(1), ALU.mult)
                magic = 1.5 * 2.0 ** 23
                ts(s(5), s(3), 1.0 / (2 * np.pi), magic, ALU.mult, ALU.add)
                ts(s(6), s(5), -magic, None, ALU.add)
                p1 = 6.28125
                p2 = float(np.float32(2 * np.pi - p1))
                p3 = float(2 * np.pi - p1 - p2)
                stt(s(7), s(6), -p1, s(3), ALU.mult, ALU.add)
                stt(s(7), s(6), -p2, s(7), ALU.mult, ALU.add)
                stt(s(7), s(6), -p3, s(7), ALU.mult, ALU.add)
                edge = float(np.nextafter(np.float32(np.pi), np.float32(0)))
                ts(s(7), s(7), edge, -edge, ALU.min, ALU.max)
                count("angle")
                ts(s(13), s(0), -1.0, None, ALU.mult)
                tt(s(14), s(13), s(13), ALU.mult)
                tt(s(15), imag, imag, ALU.mult)
                tt(s(14), s(14), s(15), ALU.add)
                ts(s(14), s(14), 1e-12, None, ALU.max)
                link(vec.reciprocal(s(15), s(14)))
                tt(s(16), s(13), s(15), ALU.mult)
                stt(s(17), imag, -1.0, s(15), ALU.mult, ALU.mult)
                v.wait_ge(c_in, 16 * 4)
                for d in range(2):
                    copy(Cin[:, d, 2, :], Cin[:, d, 0, :])
                count("c_laid")
                v.wait_ge(exped, 3)
                v.wait_ge(sined, 3)
                tt(s(10), s(9), s(9), ALU.mult)
                ts(s(10), s(10), -2.0, 1.0, ALU.mult, ALU.add)
                tt(s(11), s(4), s(10), ALU.mult)
                tt(s(12), s(4), s(8), ALU.mult)
                ts(s(18), s(11), -1.0, None, ALU.add)
                tt(s(19), s(16), s(18), ALU.mult)
                tt(s(20), s(17), s(12), ALU.mult)
                tt(s(19), s(19), s(20), ALU.subtract)
                tt(s(20), s(16), s(12), ALU.mult)
                tt(s(21), s(17), s(18), ALU.mult)
                tt(s(20), s(20), s(21), ALU.add)
                tt(s(21), s(4), s(4), ALU.mult)
                tt(g.decay[:], s(21), s(21), ALU.mult)
                v.wait_ge(c_turned, 1)
                for d in range(2):
                    ts(m.N[:, 0, d, slot_n(d, 0), :], pC[:, 2 * d, :], sgn[:, 0:1], None, ALU.mult)
                    ts(m.N[:, 1, d, slot_n(d, 0), :], pC[:, 2 * d + 1, :], -1.0, None, ALU.mult)

            @block.sync
            def _(sp):
                def image(bp):
                    sp.dma_start(img[:, bp, HW:HW + HW * HW],
                                 g.x[2 * bp:2 * bp + 2].rearrange("b c h w -> (b c) (h w)")).then_inc(img_in, 16)

                sp.dma_start(w1o[:, :], g.conv1_w).then_inc(conv_in, 16)
                sp.dma_start(wk[:, 0:CR], g.conv2_w).then_inc(conv_in, 16)
                sp.dma_start(wk[:, CR:CR + 1], g.conv2_b.rearrange("(k a) -> k a", a=1)).then_inc(conv_in, 16)
                for n, v in enumerate((g.conv1_b, g.bn_gamma, g.bn_beta, g.bn_mean, g.bn_var)):
                    sp.dma_start(bn5[:, n:n + 1], v.rearrange("(p a) -> p a", a=1)).then_inc(conv_in, 16)
                image(0)
                for d, (_, _, _, _, _, Cr, Ci, _) in enumerate((g.ssm_f, g.ssm_b)):
                    sp.dma_start(Cin[:, d, 0, :], Cr).then_inc(c_in, 16)
                    sp.dma_start(Cin[:, d, 1, :], Ci).then_inc(c_in, 16)
                image(1)
                sp.wait_ge(img_in, 32)

            @block.gpsimd
            def _(pool):
                nc.gpsimd.memset(g.ident[:], 0.0).then_inc(pool_const, 1)
                pool.wait_ge(pool_const, 1)
                nc.gpsimd.affine_select(out=g.ident[:], in_=g.ident[:], compare_op=ALU.not_equal, fill=1.0,
                                        base=0, pattern=[[-1, 128]], channel_multiplier=1).then_inc(pool_const, 1)
                nc.gpsimd.iota(g.rank[:], pattern=[[-1, EX]], base=EX, channel_multiplier=0,
                               allow_small_or_imprecise_dtypes=True)
                nc.gpsimd.memset(g.W1z[:], 0.0)
                nc.gpsimd.memset(g.hC[:], 0.0)
                nc.gpsimd.memset(g.bgc[:], 0.0)
                for bp in range(2):
                    nc.gpsimd.memset(img[:, bp, 0:HW], 0.0)
                    nc.gpsimd.memset(img[:, bp, PROW - HW:PROW], 0.0)

            @block.scalar
            def _(act):
                dirs = (g.ssm_f, g.ssm_b)
                for n, at in enumerate((0, 1, 2, 7)):
                    for d in range(2):
                        act.dma_start(rows[2 * n + d:2 * n + d + 1, 0, :], dirs[d][at].rearrange("(a p) -> a p", a=1)).then_inc(ssm_in, 16)
                act.wait_ge(dve, consts["bnvar"])
                nc.scalar.activation(m.ysc[:, 6:7], m.ysc[:, 5:6], ACT.Sqrt).then_inc(sined, 1)
                act.wait_ge(dve, consts["raw"])
                nc.scalar.activation(S[:, 0, :], raw[:, 0, :], ACT.Exp).then_inc(exped, 1)
                nc.scalar.activation(S[:, 1, :], raw[:, 2, :], ACT.Exp).then_inc(exped, 1)
                act.wait_ge(dve, consts["ad"])
                nc.scalar.activation(S[:, 4, :], S[:, 2, :], ACT.Exp).then_inc(exped, 1)
                act.wait_ge(dve, consts["angle"])
                nc.scalar.activation(S[:, 8, :], S[:, 7, :], ACT.Sin).then_inc(sined, 1)
                nc.scalar.activation(S[:, 9, :], S[:, 7, :], ACT.Sin, scale=0.5).then_inc(sined, 1)

            @block.tensor
            def _(pe):
                pe.wait_ge(pool_const, POOL_CONST)
                pe.wait_ge(dve, consts["conv_laid"])
                nc.tensor.transpose(pA[:], w1d[:].rearrange("o b c -> o (b c)"), g.ident[0:CR, 0:CR])
                nc.tensor.transpose(pB[:], wkd[:], g.ident[0:TAPS, 0:TAPS])
                nc.tensor.matmul(pN[:], spread6[:].rearrange("o r p -> o (r p)"), bn5[:], start=True, stop=True).then_inc(w_spread, 1)
                pe.wait_ge(dve, consts["ssm_laid"])
                nc.tensor.transpose(pS[:].rearrange("p n d -> p (n d)"), rows[:].rearrange("n r s -> n (r s)"),
                                    g.ident[0:8, 0:8]).then_inc(ssm_turned, 1)
                pe.wait_ge(dve, consts["c_laid"])
                for d in range(2):
                    nc.tensor.transpose(pC[:, 2 * d, :], Cin[:, d, 0:2, :], g.ident[0:F, 0:F])
                    last = nc.tensor.transpose(pC[:, 2 * d + 1, :], Cin[:, d, 1:3, :], g.ident[0:F, 0:F])
                last.then_inc(c_turned, 1)


POOL_CONST = 2


def slot_m(d, e):
    return 4 - e if d == FWD else e


def slot_n(d, k):
    return k if d == FWD else 4 - k


def state_matrices(nc, pool, g, m, sem):
    S, turn, M = m.S, m.turn, m.M
    step = sem("step")
    gp, steps = nc.gpsimd, [0]

    def link(ins):
        steps[0] += 1
        ins.then_inc(step, 1)
        pool.wait_ge(step, steps[0])

    def tt(o, a, b, op):
        link(gp.tensor_tensor(o, a, b, op))

    def ts(o, a, s1, s2=None, op0=ALU.mult, op1=ALU.bypass):
        link(gp.tensor_scalar(o, a, s1, s2, op0, op1) if s2 is not None else gp.tensor_scalar(o, a, s1, None, op0))

    def square(to, z):
        s = lambda n: S[:, n, :]
        gp.tensor_tensor(s(32), z[:, 0, :], z[:, 1, :], ALU.mult)
        tt(S[:, 30:32, :], z, z, ALU.mult)
        gp.tensor_tensor(s(33), s(30), s(31), ALU.subtract)
        gp.tensor_scalar(s(35), s(32), 2.0, None, ALU.mult)
        tt(s(34), s(30), s(31), ALU.add)
        ts(s(34), s(34), -1.0, 2.0, ALU.mult, ALU.add)
        gp.tensor_tensor(to[:, 0, :], s(33), s(34), ALU.mult)
        tt(to[:, 1, :], s(35), s(34), ALU.mult)

    ts(S[:, 36, :], S[:, 10, :], 1.0)
    ts(S[:, 37, :], S[:, 8, :], 1.0)
    square(S[:, 22:24, :], S[:, 36:38, :])
    square(turn[:, 0], S[:, 22:24, :])
    for k in range(9):
        square(turn[:, k + 1], turn[:, k])

    link(gp.memset(g.tab[:, :, 0, 0:1], 1.0))
    link(gp.memset(g.tab[:, :, 1, 0:1], 0.0))
    for k in range(QUADS.bit_length() - 1):
        n = 2 ** k
        for d in range(2):
            t, half = g.tab[:, d, :, 0:n], [m.half[:, i, :, 0:n] for i in range(2)]
            gp.tensor_scalar(half[0], t, turn[:, k, 0, d:d + 1], None, ALU.mult)
            ts(half[1], t, turn[:, k, 1, d:d + 1])
            gp.tensor_tensor(g.tab[:, d, 0, n:2 * n], half[0][:, 0], half[1][:, 1], ALU.subtract)
            tt(g.tab[:, d, 1, n:2 * n], half[0][:, 1], half[1][:, 0], ALU.add)

    turned, kept = m.by_im, m.by_re

    def times(o, a, re, im, sign):
        gp.tensor_scalar(turned[:], a, im, None, ALU.mult)
        ts(kept[:], a, re)
        gp.tensor_tensor(o[:, 0], kept[:, 0], turned[:, 1], ALU.subtract if sign > 0 else ALU.add)
        tt(o[:, 1], kept[:, 1], turned[:, 0], ALU.add if sign > 0 else ALU.subtract)

    pool.wait_ge(m.b_in, 16 * 8)
    for d in range(2):
        ts(m.Bm[64:128, d, 1, :], m.Bm[64:128, d, 1, :], -1.0)
    for d in range(2):
        col = lambda n: S[:, n, d:d + 1]
        at = lambda e: M[:, d, :, slot_m(d, e), :]
        times(at(0), m.Bm[:, d], col(19), col(20), 1)
        for e in range(4):
            times(at(e + 1), at(e), col(11), col(12), 1)
        gp.tensor_copy(m.M0[:, d], at(0)[:, 0:1].broadcast_to([128, 2, F]))
        at = lambda k: m.N[:, :, d, slot_n(d, k), :]
        for k in range(4):
            times(at(k + 1), at(k), col(11), col(12), -1)


FFN_LOADS = 10


def load_rest(sp, g, m):
    for d, (_, _, _, Br, Bi, _, _, _) in enumerate((g.ssm_f, g.ssm_b)):
        sp.dma_start(m.Bm[0:64, d, 0, :], Br).then_inc(m.b_in, 16)
        sp.dma_start(m.Bm[64:128, d, 0, :], Bi).then_inc(m.b_in, 16)
        sp.dma_start(m.Bm[0:64, d, 1, :], Bi).then_inc(m.b_in, 16)
        sp.dma_start(m.Bm[64:128, d, 1, :], Br).then_inc(m.b_in, 16)
    for par in range(2):
        sp.dma_start(g.W1z[F * par:F * par + F, par, :], g.W1).then_inc(m.ffn_in, 16)
    sp.dma_start(g.hC[0:F, 0:1], g.cls_tok.rearrange("a b f -> f (a b)")).then_inc(m.ffn_in, 16)
    sp.dma_start(g.b1c[:], g.b1.rearrange("(h p) -> p h", p=128), allow_slow_non_contiguous=True).then_inc(m.ffn_in, 16)
    sp.dma_start(g.WgT[:], g.Wg.rearrange("(h p) e -> p h e", p=128)).then_inc(m.ffn_in, 16)
    for h in range(2):
        sp.dma_start(g.WdT[:, h], g.Wd[:, 128 * h:128 * h + 128, :].rearrange("e p f -> p e f")).then_inc(m.ffn_in, 16)
    sp.dma_start(g.bgc[0:EX, :], g.bg.rearrange("(e a) -> e a", a=1)).then_inc(m.ffn_in, 16)
    for r in range(2):
        sp.dma_start(m.bfull[r:r + 1, :], g.bd.rearrange("(a e) f -> a (e f)", a=1)).then_inc(m.ffn_in, 16)
    sp.wait_ge(m.ffn_in, 16 * FFN_LOADS)


def matrices(nc, g, m):
    with ExitStack() as ctx:
        def ps(name, shape):
            return ctx.enter_context(nc.psum_tensor("mat_" + name, shape, F32))

        K0 = ctx.enter_context(nc.sbuf_tensor("mat_K0", [128, 2, F], F32))
        pT = [ps(f"T{i}", [128, 4, 128]) for i in range(3)]
        pK = ps("K", [128, 2, 4, F])
        turned = ctx.enter_context(nc.semaphore("mat_turned"))
        k_made = ctx.enter_context(nc.semaphore("mat_k_made"))
        step = ctx.enter_context(nc.semaphore("mat_step"))
        zeroed = ctx.enter_context(nc.semaphore("mat_zeroed"))
        highs = ctx.enter_context(nc.semaphore("mat_highs"))
        bias = ctx.enter_context(nc.semaphore("mat_bias"))

        with nc.Block() as block:
            @block.tensor
            def _(pe):
                for d in range(2):
                    first = 0 if d == FWD else 1
                    last = nc.tensor.matmul(pK[:, d, :, :], m.M0[:, d, :, :], m.N[:, 0, d, first:first + 4, :],
                                            start=(d == 0), stop=(d == 1), skip_group_check=True)
                last.then_inc(k_made, 1)
                for n, (d, which, slot) in enumerate(LV_PLAN):
                    last = nc.tensor.transpose(pT[n // 4][:, n % 4, :], m.M[:, d, which, slot:slot + 2, :], g.ident[:])
                    if n % 4 == 3 or n == len(LV_PLAN) - 1:
                        last.then_inc(turned, 1)

            @block.scalar
            def _(act):
                for n in range(3):
                    k = 4 if n < 2 else 3
                    act.wait_ge(turned, n + 1)
                    nc.scalar.copy(g.LV[0][:, 4 * n:4 * n + k, :], pT[n][:, 0:k, :]).then_inc(highs, 1)
                nc.scalar.copy(g.N[0][:], m.N[:]).then_inc(highs, 1)

            @block.vector
            def _(v):
                for n in range(2):
                    nc.vector.memset(g.KI[n][:].bitcast(F32), 0.0).then_inc(zeroed, 1)
                v.wait_ge(zeroed, 2)
                lo, hi = slice(0, 64), slice(64, 128)
                full, part, chosen = m.bfull, m.bpart, m.bsel
                nc.vector.tensor_copy(g.hC[0:F, 1:B], g.hC[0:F, 0:1].broadcast_to([F, B - 1]))
                nc.vector.tensor_copy(part[:, 0, :], full[:]).then_inc(bias, 1)
                v.wait_ge(bias, 1)
                nc.vector.tensor_tensor(part[:, 1, :], full[:], part[:, 0, :], ALU.subtract).then_inc(bias, 1)
                v.wait_ge(bias, 2)
                for n in range(2):
                    last = nc.vector.tensor_scalar(chosen[:, n, :], part[:, n, :], g.ident[0:2, n:n + 1], None, ALU.mult)
                last.then_inc(bias, 1)
                v.wait_ge(bias, 3)
                nc.vector.tensor_tensor(g.bias2[:], chosen[:, 0, :], chosen[:, 1, :], ALU.add)
                power = lambda d, k: pK[:, d, k if d == FWD else 3 - k, :]
                v.wait_ge(k_made, 1)
                for d in range(2):
                    for r in (lo, hi):
                        last = nc.vector.scalar_tensor_tensor(out=K0[r, d, :], in0=g.ident[r, r], scalar=m.raw[r, 3, d:d + 1],
                                                              in1=power(d, 0)[r], op0=ALU.mult, op1=ALU.add)
                last.then_inc(step, 1)
                v.wait_ge(step, 1)
                plans = ([(lo, 0, 0, 0), (lo, 0, 1, 1), (hi, 0, 1, 0), (lo, 1, 0, 2), (lo, 1, 1, 3), (hi, 1, 0, 1), (hi, 1, 1, 2)],
                         [(lo, 0, 0, 0), (hi, 0, 0, 1), (hi, 0, 1, 0), (lo, 1, 0, 2), (lo, 1, 1, 1), (hi, 1, 0, 3), (hi, 1, 1, 2)])
                value = lambda d, r, k: K0[r, d, :] if k == 0 else power(d, k)[r]
                for d in range(2):
                    for r, which, j, k in plans[d]:
                        last = nc.vector.tensor_copy(g.KI[0][r, d, which, j, :], value(d, r, k))
                last.then_inc(step, 1)
                v.wait_ge(step, 2)
                for d in range(2):
                    for r, which, j, k in plans[d]:
                        nc.vector.tensor_tensor(g.KI[1][r, d, which, j, :], value(d, r, k), g.KI[0][r, d, which, j, :],
                                                ALU.subtract)
                for n in range(3):
                    k = 4 if n < 2 else 3
                    v.wait_ge(highs, n + 1)
                    nc.vector.tensor_tensor(g.LV[1][:, 4 * n:4 * n + k, :], pT[n][:, 0:k, :], g.LV[0][:, 4 * n:4 * n + k, :],
                                            ALU.subtract)
                v.wait_ge(highs, 4)
                nc.vector.tensor_tensor(g.N[1][:], m.N[:], g.N[0][:], ALU.subtract)


LV_PLAN = [(FWD, 0, 1), (FWD, 0, 3), (FWD, 1, 1), (FWD, 1, 3),
           (BWD, 0, 0), (BWD, 0, 2), (BWD, 1, 0), (BWD, 1, 2),
           (FWD, 0, 0), (FWD, 1, 0), (FWD, 0, 4)]
LV_CARRY, LV_CARRY_TURNED, LV_FIRST = 8, 9, 10



def involution(nc, g, m):
    CPI = HW * HW // CH
    ROWS = CH // HW
    NW = 3
    PART_AT = 5
    with ExitStack() as ctx:
        def sem(name):
            return ctx.enter_context(nc.semaphore("inv_" + name))

        prod = ctx.enter_context(nc.sbuf_tensor("inv_prod", [128, TAPS, ROWS, HW], F32))
        yf = ctx.enter_context(nc.sbuf_tensor("inv_yf", [3 * 2 * CR, CH], F32))
        ysb = [ctx.enter_context(nc.sbuf_tensor(f"inv_ysb{n}", [YROWS, CH], F32R)) for n in range(2)]
        pY = ctx.enter_context(nc.psum_tensor("inv_pY", [3 * 2 * CR, CH], F32))
        pW = [ctx.enter_context(nc.psum_tensor(f"inv_pW{n}", [128, ROWS, HW], F32)) for n in range(NW)]
        pS = ctx.enter_context(nc.psum_tensor("inv_pS", [128, CH], F32))
        reduced = sem("reduced")
        relued = sem("relued")
        parted = sem("parted")
        weighed = sem("weighed")
        filtered = sem("filtered")
        added = sem("added")
        moved = sem("moved")
        onesrow = sem("onesrow")

        def tap(k):
            dh, dw = k // 3 - 1, k % 3 - 1
            lo, hi = max(0, -dw), HW - max(0, dw)
            return dh, dw, lo, hi

        def starts(bp, hc):
            return bp == 0 and isinstance(hc, int) and hc == 0

        def chunks(eng, bp, body):
            body(bp, 0, 0, (bp, 1))
            with eng.Fori(0, CPI // 2 - 1) as k:
                body(bp, 2 * k + 1, 1, (bp, 2 * k + 2))
                body(bp, 2 * k + 2, 0, (bp, 2 * k + 3))
            body(bp, CPI - 1, 1, (1, 0) if bp == 0 else None)

        with nc.Block() as block:
            @block.tensor
            def _(pe):
                def reduce(bp, hc):
                    n = bp * CPI + hc
                    pe.wait_ge(relued, n)
                    nc.tensor.matmul(pY[:], m.conv1L[:].rearrange("p r o -> p (r o)"),
                                     m.img[:, bp, bass.ds(HW + hc * CH, CH)], start=True, stop=True).then_inc(reduced, 1)

                def weigh(bp, hc, u, k):
                    n = bp * CPI + hc
                    if k == 0:
                        pe.wait_ge(parted, n + 1)
                    if k >= NW or not starts(bp, hc):
                        pe.wait_ge(filtered, n * TAPS + k - NW + 1)
                    nc.tensor.matmul(pW[k % NW][:], m.conv2L[:, k, :], ysb[u][:], start=True, stop=True).then_inc(weighed, 1)

                def body(bp, hc, u, following):
                    n = bp * CPI + hc
                    for k in range(TAPS):
                        if k == 0 and following:
                            reduce(*following)
                        pe.wait_ge(filtered, n * TAPS + k + 1)
                        if k == 0:
                            pe.wait_ge(moved, n)
                        for j in range(4):
                            last = nc.tensor.matmul(pS[:, 128 * j:128 * j + 128], prod[:, k, 2 * j:2 * j + 2, :], g.ident[:],
                                                    is_transpose=True, start=(k == 0 and j == 0),
                                                    stop=(k == TAPS - 1 and j == 3))
                        last.then_inc(added, 1)
                        if k + NW < TAPS:
                            weigh(bp, hc, u, k + NW)
                        elif following:
                            weigh(*following, 1 - u, k + NW - TAPS)

                reduce(0, 0)
                for k in range(NW):
                    weigh(0, 0, 0, k)
                for bp in range(2):
                    chunks(pe, bp, body)

            @block.scalar
            def _(act):
                act.wait_ge(onesrow, 1)

                def relu(bp, hc, u):
                    n = bp * CPI + hc
                    act.wait_ge(reduced, n + 1)
                    if not starts(bp, hc):
                        act.wait_ge(parted, n)
                    nc.scalar.activation(yf[:], pY[:], ACT.Relu, bias=m.ysc[:, 7:8], scale=m.ysc[:, 6:7])
                    if bp > 0 or not (isinstance(hc, int) and hc < 2):
                        act.wait_ge(weighed, (n - 1) * TAPS)
                    nc.scalar.activation(ysb[u][0:3 * 2 * CR, :], pY[:], ACT.Relu, bias=m.ysc[:, 7:8],
                                         scale=m.ysc[:, 6:7]).then_inc(relued, 1)

                def body(bp, hc, u, following):
                    n = bp * CPI + hc
                    if following:
                        relu(*following, 1 - u)
                    act.wait_ge(added, (n + 1) * TAPS)
                    src = pS[:].rearrange("p (j b c) -> p b c j", j=4, b=2)
                    dst = g.hT[:].rearrange("p (b c h) r -> p b c (h r)", b=B, c=C)
                    nc.scalar.copy(dst[:, 2 * bp:2 * bp + 2, :, bass.ds(4 * hc, 4)], src).then_inc(moved, 1)

                relu(0, 0, 0)
                for bp in range(2):
                    chunks(act, bp, body)

            @block.vector
            def _(v):
                for k in range(TAPS):
                    _, dw, lo, hi = tap(k)
                    if dw:
                        edge = prod[:, k, :, 0:1] if dw < 0 else prod[:, k, :, HW - 1:HW]
                        nc.vector.memset(edge, 0.0)
                for n in range(2):
                    last = nc.vector.memset(ysb[n][3 * 2 * CR:YROWS, :].bitcast(F32), 1.0)
                last.then_inc(onesrow, 1)

                def part(bp, hc, u):
                    v.wait_ge(relued, bp * CPI + hc + 1)
                    low = slice(2 * 2 * CR, 3 * 2 * CR)
                    nc.vector.tensor_tensor(ysb[u][low], yf[low], ysb[u][low], ALU.subtract).then_inc(parted, 1)

                def body(bp, hc, u, following):
                    n = bp * CPI + hc
                    for k in range(TAPS):
                        if k == PART_AT and following:
                            part(*following, 1 - u)
                        dh, dw, lo, hi = tap(k)
                        v.wait_ge(weighed, n * TAPS + k + 1)
                        if not starts(bp, hc):
                            v.wait_ge(added, (n - 1) * TAPS + k + 1)
                        rows = m.img[:, bp, bass.ds(hc * CH + (1 + dh) * HW, CH)].rearrange("p (r w) -> p r w", w=HW)
                        nc.vector.tensor_tensor(prod[:, k, :, lo:hi], pW[k % NW][:, :, lo:hi],
                                                rows[:, :, lo + dw:hi + dw], ALU.mult).then_inc(filtered, 1)

                part(0, 0, 0)
                for bp in range(2):
                    chunks(v, bp, body)

            @block.gpsimd
            def _(pool):
                state_matrices(nc, pool, g, m, sem)

            @block.sync
            def _(sp):
                load_rest(sp, g, m)


def layer_norm(nc, g, which):
    NP, W = NCH // 2, 2 * 8 + 2
    with ExitStack() as ctx:
        def sem(name):
            return ctx.enter_context(nc.semaphore(f"ln{which}_{name}"))

        def sb(name, shape):
            return ctx.enter_context(nc.sbuf_tensor(f"ln{which}_{name}", shape, F32))

        def ps(name, shape):
            return ctx.enter_context(nc.psum_tensor(f"ln{which}_p{name}", shape, F32))

        uflat = sb("u", [128, NCH * CH])
        sq = [sb(f"sq{n}", [128, CH]) for n in range(2)]
        st = [sb(f"st{n}", [128, 4, 2 * F]) for n in range(2)]
        sq_cls, st_cls = sb("sqc", [128, B]), sb("stc", [B, 2 * F])
        var, root, guess, corr, factor = (sb(n, [128, W]) for n in ("var", "root", "guess", "corr", "factor"))
        pM = [ps(f"M{n}", [128, CH]) for n in range(2)]
        pV = ps("V", [128, W])
        pR = [ps(f"R{n}", [128, CH]) for n in range(2)]
        pX = ps("X", [128, B])
        centered = sem("centered")
        squared = sem("squared")
        summed = sem("summed")
        kept = sem("kept")
        rooted = sem("rooted")
        newton = sem("newton")
        picked = sem("picked")
        spread = sem("spread")
        scaled = sem("scaled")
        high_made = sem("high_made")
        weights_parted = sem("weights_parted")
        cls_made = sem("cls_made")
        beside_set = sem("beside_set")
        STEPS = 5
        hflat = g.hT[:].rearrange("p a r -> p (a r)")
        high_flat, low_flat = (u[:].rearrange("p a r -> p (a r)") for u in g.u)

        def pipeline(eng, turn):
            def one(i):
                turn(i, [0 <= i - n < NP for n in range(4)], i < NP - 1)

            for i in range(3):
                one(i)
            with eng.Fori(3, NP - 1) as i:
                turn(i, [True] * 4, True)
            for i in range(NP - 1, NP + 3):
                one(i)

        def at_least(i, n):
            return not isinstance(i, int) or i >= n

        with nc.Block() as block:
            @block.tensor
            def _(pe):
                def center(i, n):
                    if at_least(i, 1):
                        pe.wait_ge(squared, 2 * i + n - 1)
                    nc.tensor.matmul(pM[n][:], g.center[:], hflat[:, bass.ds((2 * i + n) * CH, CH)],
                                     start=True, stop=True).then_inc(centered, 1)

                def spreads(i):
                    for n in range(2):
                        pe.wait_ge(picked, 2 * i + n + 1)
                        if at_least(i, 1):
                            pe.wait_ge(scaled, 2 * i + n - 1)
                        for j in range(4):
                            last = nc.tensor.transpose(pR[n][:, 128 * j:128 * j + 128], st[n][:, j, :], g.ident[:])
                        last.then_inc(spread, 1)

                def sums(i, n):
                    if n == 0 and at_least(i, 1):
                        pe.wait_ge(kept, i)
                    pe.wait_ge(squared, 2 * i + n + 1)
                    for j in range(4):
                        last = nc.tensor.matmul(pV[:, 8 * n + 2 * j:8 * n + 2 * j + 2], sq[n][:, 128 * j:128 * j + 128],
                                                g.mean2[:], start=True, stop=True)
                    last.then_inc(summed, 1)

                def turn(i, stages, more):
                    if stages[2]:
                        spreads(i - 2)
                    for n in range(2):
                        if stages[0]:
                            sums(i, n)
                        if more:
                            center(i + 1, n)

                nc.tensor.matmul(pX[:], g.center[:], g.hC[:], start=True, stop=True).then_inc(cls_made, 1)
                pe.wait_ge(cls_made, 2)
                nc.tensor.matmul(pV[0:B, W - 2:W], sq_cls[:], g.mean2[:], start=True, stop=True)
                for n in range(2):
                    center(0, n)
                pipeline(pe, turn)
                pe.wait_ge(cls_made, 3)
                nc.tensor.transpose(pX[:], st_cls[:], g.ident[0:B, 0:B]).then_inc(cls_made, 1)

            @block.scalar
            def _(act):
                def squares(i, n):
                    act.wait_ge(centered, 2 * i + n + 1)
                    if at_least(i, 1):
                        act.wait_ge(summed, 2 * i + n - 1)
                    nc.scalar.copy(uflat[:, bass.ds((2 * i + n) * CH, CH)], pM[n][:])
                    nc.scalar.activation(sq[n][:], pM[n][:], ACT.Square).then_inc(squared, 1)

                def roots(i):
                    act.wait_ge(kept, i + 1)
                    nc.scalar.activation(root[:], var[:], ACT.Sqrt).then_inc(rooted, 1)

                def high(i):
                    for n in range(2):
                        act.wait_ge(scaled, 2 * i + n + 1)
                        cols = bass.ds((2 * i + n) * CH, CH)
                        nc.scalar.copy(high_flat[:, cols], uflat[:, cols]).then_inc(high_made, 1)

                def turn(i, stages, more):
                    for n in range(2):
                        if stages[0]:
                            squares(i, n)
                        if n == 0 and stages[1]:
                            roots(i - 1)
                    if stages[3]:
                        high(i - 3)

                act.wait_ge(cls_made, 1)
                nc.scalar.copy(g.uC[:], pX[:])
                nc.scalar.activation(sq_cls[:], pX[:], ACT.Square).then_inc(cls_made, 1)
                pipeline(act, turn)

            @block.vector
            def _(v):
                def keep(i):
                    v.wait_ge(summed, 2 * i + 2)
                    if isinstance(i, int) and i == 0:
                        nc.vector.memset(var[:, W - 2:W], 1.0).then_inc(beside_set, 1)
                        v.wait_ge(beside_set, 1)
                        nc.vector.tensor_scalar(var[0:B, W - 2:W], pV[0:B, W - 2:W], LN_EPS, None, ALU.add)
                    nc.vector.tensor_scalar(var[:, 0:W - 2], pV[:, 0:W - 2], LN_EPS, None, ALU.add).then_inc(kept, 1)

                def factors(i):
                    k = STEPS * i
                    v.wait_ge(rooted, i + 1)
                    nc.vector.reciprocal(guess[:], root[:]).then_inc(newton, 1)
                    v.wait_ge(newton, k + 1)
                    nc.vector.tensor_tensor(corr[:], guess[:], guess[:], ALU.mult).then_inc(newton, 1)
                    v.wait_ge(newton, k + 2)
                    nc.vector.tensor_tensor(corr[:], corr[:], var[:], ALU.mult).then_inc(newton, 1)
                    v.wait_ge(newton, k + 3)
                    nc.vector.tensor_scalar(corr[:], corr[:], -0.5, 1.5, ALU.mult, ALU.add).then_inc(newton, 1)
                    v.wait_ge(newton, k + 4)
                    nc.vector.tensor_tensor(factor[:], guess[:], corr[:], ALU.mult).then_inc(newton, 1)

                def apply(i):
                    for n in range(2):
                        v.wait_ge(spread, 2 * i + n + 1)
                        u = uflat[:, bass.ds((2 * i + n) * CH, CH)]
                        nc.vector.tensor_tensor(u, pR[n][:], u, ALU.mult).then_inc(scaled, 1)

                def pick(i):
                    v.wait_ge(newton, STEPS * (i + 1))
                    if at_least(i, 1):
                        v.wait_ge(spread, 2 * i)
                    for n in range(2):
                        nc.vector.tensor_copy(st[n][:].rearrange("p j (r f) -> p (j r) f", r=2),
                                              factor[:, 8 * n:8 * n + 8].unsqueeze(2).broadcast_to([128, 8, F])).then_inc(picked, 1)

                def turn(i, stages, more):
                    if stages[1]:
                        factors(i - 1)
                    if stages[2]:
                        apply(i - 2)
                    if stages[1]:
                        pick(i - 1)
                    if stages[0]:
                        keep(i)

                pipeline(v, turn)
                v.wait_ge(newton, STEPS * NP)
                nc.vector.tensor_copy(st_cls[:].rearrange("p (r f) -> p r f", r=2),
                                      factor[0:B, W - 2:W].unsqueeze(2).broadcast_to([B, 2, F])).then_inc(cls_made, 1)
                v.wait_ge(cls_made, 4)
                nc.vector.tensor_tensor(g.uC[:], pX[:], g.uC[:], ALU.mult)

            @block.gpsimd
            def _(pool):
                if which == "2":
                    weights = ((g.W1z, g.W1P), (g.WdT, g.WdP))
                    for whole, (high, low) in weights:
                        nc.gpsimd.tensor_copy(high[:], whole[:]).then_inc(weights_parted, 1)
                    for n in range(2):
                        nc.gpsimd.tensor_copy(g.WgP[n][:, :, 0, :], g.WgT[:]).then_inc(weights_parted, 1)
                    nc.gpsimd.memset(g.WgP[1][:, :, 1, :].bitcast(F32), 0.0)
                    pool.wait_ge(weights_parted, 4)
                    for whole, (high, low) in weights:
                        nc.gpsimd.tensor_tensor(low[:], whole[:], high[:], ALU.subtract)
                    nc.gpsimd.tensor_tensor(g.WgP[0][:, :, 1, :], g.WgT[:], g.WgP[0][:, :, 0, :], ALU.subtract)
                for n in range(NCH):
                    pool.wait_ge(high_made, n + 1)
                    cols = slice(n * CH, n * CH + CH)
                    nc.gpsimd.tensor_tensor(low_flat[:, cols], uflat[:, cols], high_flat[:, cols], ALU.subtract)


def state_space(nc, g):
    HALVES = QUADS // CH
    STEPS = 2 * HALVES
    YPB = 2 * STEPS + 1
    with ExitStack() as ctx:
        def sem(name):
            return ctx.enter_context(nc.semaphore("ssm_" + name))

        def sb(name, shape):
            return ctx.enter_context(nc.sbuf_tensor("ssm_" + name, shape, F32))

        pV = [[ctx.enter_context(nc.psum_tensor(f"ssm_v{n}{t}", [128, CH], F32)) for t in range(2)] for n in range(2)]
        pY = [ctx.enter_context(nc.psum_tensor(f"ssm_y{n}", [128, CH], F32)) for n in range(4)]
        rot = [sb(f"rot{n}", [128, 2, CH]) for n in range(2)]
        z = [sb(f"z{n}", [128, CH]) for n in range(2)]
        back = [sb(f"back{n}", [128, CH]) for n in range(2)]
        zP = [[ctx.enter_context(nc.sbuf_tensor(f"ssm_z{n}{t}", [128, 2, QUADS + 1], F32R)) for t in range(2)] for n in range(2)]
        act_y = [sb(f"gelu{n}", [128, CH]) for n in range(4)]
        act_c = sb("geluc", [F, 2])
        entered = sem("entered")
        x0_made = sem("x0_made")
        turned = sem("turned")
        freed = sem("freed")
        scanned = sem("scanned")
        backed = sem("backed")
        highs = sem("highs")
        stated = sem("stated")
        yielded = sem("yielded")
        gelued = sem("gelued")
        summed = sem("summed")
        cls_y, cls_g, cls_a = sem("cls_y"), sem("cls_g"), sem("cls_a")
        start = sem("start")

        def part(d, h):
            return (h if d == FWD else HALVES - 1 - h) * CH

        def cols(t, b, d, h, q):
            return t[:, bass.ds(b * QUADS + part(d, h), CH), q]

        def scan_order(a, d):
            return a if d == FWD else a[:, ::-1]

        def before(t, d, h):
            a = part(d, h) + (0 if d == FWD else 1)
            return t[:, d, a:a + CH]

        def after(t, d, h):
            a = part(d, h) + (1 if d == FWD else 0)
            return scan_order(t[:, d, a:a + CH], d)

        ORDER = [(d, h) for d in (FWD, BWD) for h in range(HALVES)]
        LVI = {FWD: ((0, 1), (2, 3)), BWD: ((4, 5), (6, 7))}

        def whole(out, parts, moving, start, stop):
            for n in range(2):
                last = nc.tensor.matmul(out, parts[n].bitcast(F32), moving, start=(start and n == 0), stop=(stop and n == 1))
            return last

        with nc.Block() as block:
            @block.tensor
            def _(pe):
                def enter(b, s, wait):
                    d, h = ORDER[s]
                    if wait:
                        pe.wait_ge(freed, b * STEPS + s - 1)
                    for t in range(2):
                        out = pV[s % 2][t]
                        carry = d == FWD and h == 0
                        for q in range(2):
                            for value, weight in PARTS:
                                last = nc.tensor.matmul(out[:], g.LV[weight][:, LVI[d][t][q], :], cols(g.u[value], b, d, h, q),
                                                        start=(q == 0 and (value, weight) == PARTS[0]),
                                                        stop=(q == 1 and (value, weight) == PARTS[-1] and not carry))
                        if carry:
                            carry_in = [lv[:, (LV_CARRY, LV_CARRY_TURNED)[t], :] for lv in g.LV]
                            last = whole(out[:, 0:1], carry_in, g.uC[:, 0:1], False, True)
                    last.then_inc(entered, 1)

                def leave(b, s):
                    d, h = ORDER[s]
                    for q in range(2):
                        n = 2 * s + q
                        out = pY[n % 4][:]
                        if isinstance(b, int) and b == 0:
                            if n >= 4:
                                pe.wait_ge(gelued, n - 3)
                        else:
                            pe.wait_ge(gelued, b * YPB + (n - 3 if n >= 4 else (0 if n == 0 else n - 4)))
                        for value, weight in PARTS:
                            nc.tensor.matmul(out, g.KI[weight][:, d, 0, :, :], cols(g.u[value], b, d, h, q),
                                             start=((value, weight) == PARTS[0]), stop=False)
                        if q == (1 if d == FWD else 0):
                            for value, weight in PARTS:
                                nc.tensor.matmul(out, g.KI[weight][:, d, 1, :, :], cols(g.u[value], b, d, h, 1 - q),
                                                 start=False, stop=False)
                        if q == 0:
                            pe.wait_ge(stated, b * STEPS + s + 1)
                        first = 1 + 2 * q if d == FWD else 2 * q
                        for n in range(2):
                            for value, weight in PARTS:
                                last = nc.tensor.matmul(out, g.N[weight][:, n, d, first:first + 2, :], before(zP[n][value], d, h),
                                                        start=False, stop=(n == 1 and (value, weight) == PARTS[-1]))
                        last.then_inc(yielded, 1)

                def leave_class(b):
                    out = pY[0][0:F, 0:1]
                    pe.wait_ge(gelued, b * YPB + 2 * STEPS - 3)
                    whole(out, [k[:, BWD, 0, 0, :] for k in g.KI], g.uC[:, 0:1], True, False)
                    for n in range(2):
                        for value in range(2):
                            last = whole(out, [w[:, n, BWD, 3, :] for w in g.N], zP[n][value][:, BWD, 0:1].bitcast(F32),
                                         False, n == 1 and value == 1)
                    last.then_inc(yielded, 1)

                def batch(b, more):
                    for s in range(STEPS):
                        if s + 1 < STEPS:
                            enter(b, s + 1, not (isinstance(b, int) and b == 0 and s + 1 < 2))
                        elif more:
                            enter(b + 1, 0, True)
                        leave(b, s)
                    leave_class(b)

                whole(pY[0][:, 0:1], [lv[:, LV_FIRST, :] for lv in g.LV], g.uC[:, 0:1], True, True)
                whole(pY[1][0:F, 0:1], [k[:, FWD, 0, 0, :] for k in g.KI], g.uC[:, 0:1], True, True).then_inc(cls_y, 1)
                enter(0, 0, False)
                pe.wait_ge(cls_g, 2)
                pe.wait_ge(start, 2)
                batch(0, True)
                with pe.Fori(1, B - 1) as b:
                    batch(b, True)
                batch(B - 1, False)

            @block.vector
            def _(v):
                for value in range(2):
                    for n in range(2):
                        nc.vector.memset(zP[n][value][:, BWD, QUADS:].bitcast(F32), 0.0)
                    last = nc.vector.memset(zP[1][value][:, FWD, 0:1].bitcast(F32), 0.0)
                last.then_inc(start, 1)

                def step(b, s, n0):
                    d, h = ORDER[s]
                    n = b * STEPS + s
                    r, zz = rot[s % 2], z[s % 2]
                    cos, sin = (g.tab[:, d, k, h * CH:(h + 1) * CH] for k in range(2))
                    v.wait_ge(entered, n + 1)
                    nc.vector.tensor_tensor(r[:, 0, :], scan_order(pV[s % 2][0][:], d), cos, ALU.mult)
                    nc.vector.tensor_tensor(r[:, 1, :], scan_order(pV[s % 2][1][:], d), sin, ALU.mult).then_inc(freed, 1)
                    v.wait_ge(freed, n + 1)
                    nc.vector.tensor_tensor(r[:, 0, :], r[:, 0, :], r[:, 1, :], ALU.add).then_inc(turned, 1)
                    v.wait_ge(turned, n + 1)
                    initial = 0.0 if h == 0 else z[(s - 1) % 2][:, CH - 1:CH]
                    nc.vector.tensor_tensor_scan(zz[:], g.decay[:, d:d + 1].broadcast_to([128, CH]), r[:, 0, :], initial,
                                                 ALU.mult, ALU.add).then_inc(scanned, 1)
                    v.wait_ge(scanned, n + 1)
                    if not n0:
                        v.wait_ge(yielded, (b - 1) * YPB + min(2 * (s + 2), YPB) if s % 2 == 0 else (b - 1) * YPB + min(2 * (s + 1) + 1, YPB))
                    nc.vector.tensor_tensor(back[0][:], zz[:], cos, ALU.mult)
                    nc.vector.tensor_tensor(back[1][:], zz[:], sin, ALU.mult).then_inc(backed, 1)
                    v.wait_ge(highs, n + 1)
                    for t in range(2):
                        last = nc.vector.tensor_tensor(after(zP[t][1], d, h), back[t][:], after(zP[t][0], d, h), ALU.subtract)
                    last.then_inc(stated, 1)

                v.wait_ge(cls_g, 2)
                nc.vector.tensor_tensor(zP[0][1][:, FWD, 0:1], pY[0][:, 0:1], zP[0][0][:, FWD, 0:1], ALU.subtract).then_inc(start, 1)
                v.wait_ge(start, 2)
                for s in range(STEPS):
                    step(0, s, True)
                with v.Fori(1, B) as b:
                    for s in range(STEPS):
                        step(b, s, False)

            @block.scalar
            def _(act):
                act.wait_ge(cls_y, 1)
                nc.scalar.copy(zP[0][0][:, FWD, 0:1], pY[0][:, 0:1]).then_inc(cls_g, 1)
                nc.scalar.activation(act_c[:, 0:1], pY[1][0:F, 0:1], ACT.Gelu).then_inc(cls_g, 1)

                def high(b, s):
                    act.wait_ge(backed, b * STEPS + s + 1)
                    for t in range(2):
                        last = nc.scalar.copy(after(zP[t][0], *ORDER[s]), back[t][:])
                    last.then_inc(highs, 1)

                def batch(b, first, more):
                    for n in range(YPB):
                        if n % 2 == 0 and n // 2 + 1 < STEPS:
                            high(b, n // 2 + 1)
                        elif n == 2 * (STEPS - 1) and more:
                            high(b + 1, 0)
                        act.wait_ge(yielded, b * YPB + n + 1)
                        if n < YPB - 1:
                            if first:
                                if n >= 4:
                                    act.wait_ge(summed, n - 3)
                            else:
                                act.wait_ge(summed, b * YPB + n - 3 - (1 if n < 4 else 0))
                            nc.scalar.activation(act_y[n % 4][:], pY[n % 4][:], ACT.Gelu).then_inc(gelued, 1)
                        else:
                            if not first:
                                act.wait_ge(summed, b * YPB)
                            nc.scalar.activation(act_c[:, 1:2], pY[0][0:F, 0:1], ACT.Gelu).then_inc(gelued, 1)

                high(0, 0)
                batch(0, True, True)
                with act.Fori(1, B - 1) as b:
                    batch(b, False, True)
                batch(B - 1, False, False)

            @block.gpsimd
            def _(pool):
                pool.wait_ge(cls_g, 2)
                nc.gpsimd.tensor_tensor(g.hC[0:F, :], g.hC[0:F, :], act_c[:, 0:1].broadcast_to([F, B]), ALU.add).then_inc(cls_a, 1)
                pool.wait_ge(cls_a, 1)

                def batch(b):
                    for n in range(YPB):
                        pool.wait_ge(gelued, b * YPB + n + 1)
                        if n < YPB - 1:
                            d, h = ORDER[n // 2]
                            if n == 2 * HALVES:
                                pool.wait_ge(summed, b * YPB + n)
                            t = cols(g.hT, b, d, h, n % 2)
                            nc.gpsimd.tensor_tensor(t, t, act_y[n % 4][:], ALU.add).then_inc(summed, 1)
                        else:
                            c = g.hC[0:F, bass.ds(b, 1)]
                            nc.gpsimd.tensor_tensor(c, c, act_c[:, 1:2], ALU.add).then_inc(summed, 1)

                for b in range(B):
                    batch(b)

def experts(nc, g):
    TILES = CH // 128
    with ExitStack() as ctx:
        def sem(name):
            return ctx.enter_context(nc.semaphore("ex_" + name))

        def sb(name, shape, dt=F32):
            return ctx.enter_context(nc.sbuf_tensor("ex_" + name, shape, dt))

        def ps(name, shape):
            return ctx.enter_context(nc.psum_tensor("ex_p" + name, shape, F32))

        pH = [ps(f"H{n}", [128, CH]) for n in range(2)]
        pE = [ps(f"E{n}", [128, EX, F]) for n in range(3)]
        pG = ps("G", [2 * EX, CH])
        pL = ps("L", [128, TILES, 2, EX])
        pR = ps("R", [128, TILES, 128])
        hidf = [sb(f"hidf{n}", [128, 2, CH]) for n in range(2)]
        hid = [[sb(f"hid{n}{t}", [128, 2, CH], F32R) for t in range(2)] for n in range(2)]
        hst = sb("hst", [128, CH])
        level = sb("level", [2 * EX, CH])
        gl = sb("gl", [128, 6, TILES, EX])
        inverse = sb("inverse", [128, TILES, EX + 1])
        gs = sb("gs", [128, 4, TILES])
        ms = [sb(f"ms{n}", [128, EX, F]) for n in range(2)]
        s4 = [sb(f"s4{n}", [128, 4, F]) for n in range(2)]
        s2 = [sb(f"s2{n}", [128, 2, F]) for n in range(2)]
        picked = [sb(f"picked{n}", [128, TILES, F]) for n in range(2)]
        res = [sb(f"res{n}", [128, TILES, 2, F]) for n in range(2)]
        clsr = sb("clsr", [B, F])
        hidden = sem("hidden")
        gelued = sem("gelued")
        parted = sem("parted")
        staged = sem("staged")
        rested = sem("rested")
        judged = sem("judged")
        leveled = sem("leveled")
        gated = sem("gated")
        tanhed = sem("tanhed")
        dv = sem("dv")
        dv_start = sem("dv_start")
        spoke = sem("spoke")
        chosen = sem("chosen")
        pl = sem("pl")
        reduced = sem("reduced")
        finished = sem("finished")
        stored = [sem(f"stored{n}") for n in range(2)]
        cls_sem = sem("cls")
        BANK = ((0, 1, 2, 0), (1, 2, 0, 1))
        BEFORE = ((2, 2, 5, 3), (3, 3, 3, 3))
        GATE = 11
        uflat = [u[:].rearrange("p a r -> p (a r)") for u in g.u]
        hflat = g.hT[:].rearrange("p a r -> p (a r)")

        def gate(v, base, P, T, tanh):
            G = lambda n: gl[0:P, n, 0:T, :]
            s = lambda n: gs[0:P, n, 0:T]
            wide = lambda a: a.unsqueeze(2).broadcast_to([P, T, EX])
            k = [0]

            def link(ins):
                k[0] += 1
                ins.then_inc(dv, 1)
                v.wait_ge(dv, base + k[0])

            logits = G(5)
            link(nc.vector.tensor_reduce(logits, pL[0:P, 0:T].rearrange("p t v e -> p t e v"), AX.X, ALU.add))
            link(nc.vector.tensor_reduce(s(0), logits, AX.X, ALU.max))
            k[0] += 1
            nc.vector.tensor_tensor(G(0), logits, wide(s(0)), ALU.subtract).then_inc(dv, 1)
            v.wait_ge(dv, base + k[0])
            link(nc.vector.scalar_tensor_tensor(out=G(1), in0=G(0), scalar=0.0, in1=g.rank[0:P, :].unsqueeze(1).broadcast_to([P, T, EX]),
                                                op0=ALU.is_ge, op1=ALU.mult))
            link(nc.vector.tensor_reduce(s(1), G(1), AX.X, ALU.max))
            link(nc.vector.tensor_tensor(G(1), G(1), wide(s(1)), ALU.is_equal))
            v.wait_ge(tanhed, tanh)
            link(nc.vector.tensor_scalar(G(3), G(2), -0.5, 0.5, ALU.mult, ALU.add))
            link(nc.vector.reciprocal(inverse[0:P, 0:T, 0:EX], G(3)))
            link(nc.vector.tensor_reduce(s(2), inverse[0:P, 0:T, :], AX.X, ALU.add))
            link(nc.vector.reciprocal(s(3), s(2)))
            link(nc.vector.tensor_tensor(G(4), G(1), wide(s(3)), ALU.mult))
            assert k[0] == GATE


        with nc.Block() as block:
            @block.tensor
            def _(pe):
                def hide(i, par, first, ready=None):
                    n = 2 * i + par
                    for h in range(2):
                        if not first:
                            pe.wait_ge(gelued, 2 * (n - 1) + h + 1)
                        for value, weight in PARTS:
                            if ready and (h, value, weight) == READY_AT:
                                ready()
                            last = nc.tensor.matmul(pH[h][:], g.W1P[weight][:, par, 128 * h:128 * h + 128],
                                                    uflat[value][:, bass.ds(i * CH, CH)],
                                                    start=((value, weight) == PARTS[0]), stop=((value, weight) == PARTS[-1]))
                        last.then_inc(hidden, 1)

                def rest(i, first):
                    pe.wait_ge(staged, i + 1)
                    if not first:
                        pe.wait_ge(finished, 2 * i)
                    for j in range(TILES):
                        last = nc.tensor.transpose(pR[:, j, :], hst[:, 128 * j:128 * j + 128], g.ident[:])
                    last.then_inc(rested, 1)

                def project(o, par, start, P):
                    nc.tensor.matmul(o, g.ones2[:, 0:P], g.bias2[:], start=True, stop=False)
                    for h in range(2):
                        for value, weight in PARTS:
                            last = nc.tensor.matmul(o, hid[par][value][:, h, start:start + P], g.WdP[weight][:, h],
                                                    start=False, stop=(h == 1 and value == 1))
                    return last

                def judge(n, par, cols, first):
                    pe.wait_ge(parted, n + 1)
                    if not first:
                        pe.wait_ge(leveled, n)
                    for value in range(2):
                        for h in range(2):
                            last = nc.tensor.matmul(pG[:, 0:cols], g.WgP[value][:, h], hid[par][value][:, h, 0:cols],
                                                    start=(value == 0 and h == 0), stop=(value == 1 and h == 1))
                    last.then_inc(judged, 1)

                READY_AT = (1,) + PARTS[-1]

                def ready(n, first):
                    pe.wait_ge(leveled, n + 1)
                    if not first:
                        pe.wait_ge(dv, (n - 1) * GATE + 1)

                def gates():
                    for j in range(TILES):
                        last = nc.tensor.transpose(pL[:, j], level[:, 128 * j:128 * j + 128], g.ident[0:2 * EX, 0:2 * EX])
                    last.then_inc(gated, 1)

                def speak(i, par, first):
                    n = 2 * i + par
                    pe.wait_ge(parted, n + 1)
                    for j in range(TILES):
                        if not (first and j < 3):
                            pe.wait_ge(chosen, n * TILES + j - BEFORE[par][j] + 1)
                        project(pE[BANK[par][j]][:], par, 128 * j, 128).then_inc(spoke, 1)

                def chunk(i, first, more):
                    for par in range(2):
                        n = 2 * i + par
                        judge(n, par, CH, first and par == 0)
                        if par == 1:
                            rest(i, first)
                        following = (i + par, 1 - par, False)
                        if par == 0 or more:
                            hide(*following, ready=lambda: ready(n, first and par == 0))
                        else:
                            ready(n, False)
                        gates()
                        speak(i, par, first and par == 0)

                hide(0, 0, True)
                chunk(0, True, True)
                with pe.Fori(1, NCH - 1) as i:
                    chunk(i, False, True)
                chunk(NCH - 1, False, False)
                pe.wait_ge(gelued, 4 * NCH)
                for h in range(2):
                    nc.tensor.matmul(pH[h][:, 0:B], g.W1z[:, 0, 128 * h:128 * h + 128], g.uC[:],
                                     start=True, stop=True).then_inc(hidden, 1)
                pe.wait_ge(parted, 2 * NCH + 1)
                pe.wait_ge(finished, 2 * NCH)
                judge(2 * NCH, 0, B, False)
                pe.wait_ge(leveled, 2 * NCH + 1)
                nc.tensor.transpose(pL[0:B, 0], level[:, 0:B], g.ident[0:2 * EX, 0:2 * EX]).then_inc(gated, 1)
                project(pE[0][0:B], 0, 0, B).then_inc(spoke, 1)
                nc.tensor.transpose(pR[0:B, 0, :], g.hC[:], g.ident[:]).then_inc(rested, 1)

            @block.scalar
            def _(act):
                def stage(i):
                    act.wait_ge(rested, i)
                    nc.scalar.copy(hst[:], hflat[:, bass.ds(i * CH, CH)]).then_inc(staged, 1)

                def gelu(n, par, cols, first):
                    for h in range(2):
                        act.wait_ge(hidden, 2 * n + h + 1)
                        if not first:
                            act.wait_ge(spoke, (n - 1) * TILES)
                        for o in (hidf[par], hid[par][0]):
                            last = nc.scalar.activation(o[:, h, 0:cols], pH[h][:, 0:cols], ACT.Gelu, bias=g.b1c[:, h:h + 1])
                        last.then_inc(gelued, 1)

                def add_bg(n, cols):
                    act.wait_ge(judged, n + 1)
                    nc.scalar.activation(level[:, 0:cols], pG[:, 0:cols], ACT.Identity, bias=g.bgc[:, 0:1]).then_inc(leveled, 1)

                def tanh(i, par):
                    n = 2 * i + par
                    add_bg(n, CH)
                    act.wait_ge(dv, n * GATE + 3)
                    nc.scalar.activation(gl[:, 2], gl[:, 0], ACT.Tanh, scale=0.5).then_inc(tanhed, 1)

                def chunk(i, first, more):
                    stage(i)
                    tanh(i, 0)
                    gelu(2 * i + 1, 1, CH, first)
                    tanh(i, 1)
                    if more:
                        gelu(2 * i + 2, 0, CH, False)

                gelu(0, 0, CH, True)
                chunk(0, True, True)
                with act.Fori(1, NCH - 1) as i:
                    chunk(i, False, True)
                chunk(NCH - 1, False, False)
                gelu(2 * NCH, 0, B, False)
                add_bg(2 * NCH, B)
                act.wait_ge(dv, 2 * NCH * GATE + 3)
                nc.scalar.activation(gl[0:B, 2, 0:1], gl[0:B, 0, 0:1], ACT.Tanh, scale=0.5).then_inc(tanhed, 1)

            @block.vector
            def _(v):
                def part(n, par, cols):
                    v.wait_ge(gelued, 2 * n + 2)
                    nc.vector.tensor_tensor(hid[par][1][:, :, 0:cols], hidf[par][:, :, 0:cols], hid[par][0][:, :, 0:cols],
                                            ALU.subtract).then_inc(parted, 1)

                def finish(n, m, par, stores):
                    v.wait_ge(reduced, (n + 1) * TILES)
                    if par == 0:
                        v.wait_ge(rested, stores[0])
                        if stores[1] is not None:
                            v.wait_ge(stored[m], stores[1])
                    nc.vector.tensor_tensor(res[m][:, :, par, :], pR[:, :, F * par:F * par + F], picked[par][:],
                                            ALU.add).then_inc(finished, 1)

                def two(k, first, last):
                    for m in range(2):
                        for par in range(2):
                            i = 2 * k + m
                            n = 2 * i + par
                            begins, ends = first and m == 0 and par == 0, last and m == 1 and par == 1
                            v.wait_ge(gated, n + 1)
                            gate(v, n * GATE, 128, TILES, n + 1)
                            for j in range(TILES):
                                v.wait_ge(spoke, n * TILES + j + 1)
                                if not (begins and j < 2):
                                    v.wait_ge(reduced, n * TILES + j - 1)
                                nc.vector.tensor_tensor(ms[j % 2][:], pE[BANK[par][j]][:],
                                                        gl[:, 4, j, :].unsqueeze(2).broadcast_to([128, EX, F]),
                                                        ALU.mult).then_inc(chosen, 1)
                                if j == 0 and not begins:
                                    finish(n - 1, m if par else 1 - m, 1 - par, (i + 1, None if first else 16 * k))
                                if j == 1 and not ends:
                                    part(n + 1, 1 - par, CH)

                nc.vector.memset(inverse[:, :, EX:], -float(EX)).then_inc(dv_start, 1)
                v.wait_ge(dv_start, 1)
                part(0, 0, CH)
                two(0, True, False)
                with v.Fori(1, NCH // 2 - 1) as k:
                    two(k, False, False)
                two(NCH // 2 - 1, False, True)
                finish(2 * NCH - 1, 1, 1, None)
                part(2 * NCH, 0, B)
                v.wait_ge(gated, 2 * NCH + 1)
                gate(v, 2 * NCH * GATE, B, 1, 2 * NCH + 1)
                v.wait_ge(spoke, 2 * NCH * TILES + 1)
                nc.vector.tensor_tensor(ms[0][0:B], pE[0][0:B], gl[0:B, 4, 0, :].unsqueeze(2).broadcast_to([B, EX, F]), ALU.mult).then_inc(chosen, 1)
                v.wait_ge(reduced, 2 * NCH * TILES + 1)
                v.wait_ge(rested, NCH + 1)
                nc.vector.tensor_tensor(clsr[:], pR[0:B, 0, 0:F], picked[0][0:B, 0, :], ALU.add).then_inc(finished, 1)

            @block.gpsimd
            def _(pool):
                def tile(n, j, slot, par, P):
                    pool.wait_ge(chosen, n + 1)
                    m = ms[slot][0:P]
                    nc.gpsimd.tensor_tensor(s4[slot][0:P], m[:, 0:4], m[:, 4:8], ALU.add).then_inc(pl, 1)
                    pool.wait_ge(pl, 2 * n + 1)
                    nc.gpsimd.tensor_tensor(s2[slot][0:P], s4[slot][0:P, 0:2], s4[slot][0:P, 2:4], ALU.add).then_inc(pl, 1)
                    pool.wait_ge(pl, 2 * n + 2)
                    nc.gpsimd.tensor_tensor(picked[par][0:P, j, :], s2[slot][0:P, 0], s2[slot][0:P, 1], ALU.add).then_inc(reduced, 1)

                def unit(i, par, first):
                    n = 2 * i + par
                    if not first:
                        pool.wait_ge(finished, n - 1)
                    for j in range(TILES):
                        tile(n * TILES + j, j, j % 2, par, 128)

                for par in range(2):
                    unit(0, par, True)
                with pool.Fori(1, NCH) as i:
                    for par in range(2):
                        unit(i, par, False)
                tile(2 * NCH * TILES, 0, 0, 0, B)

            @block.sync
            def _(sp):
                rows = g.out[:, 1:, :].rearrange("b (q j p r) c -> b q p j (r c)", q=4, j=TILES, p=128, r=2)
                with sp.Fori(0, B) as b:
                    for q in range(4):
                        sp.wait_ge(finished, 8 * b + 2 * q + 2)
                        sp.dma_start(rows[bass.ds(b, 1), q].rearrange("b p j x -> (b p) j x"),
                                     res[q % 2][:].rearrange("p j r c -> p j (r c)")).then_inc(stored[q % 2], 16)
                sp.wait_ge(finished, 2 * NCH + 1)
                sp.dma_start(g.out[:, 0, :], clsr[:]).then_inc(cls_sem, 16)
                sp.wait_ge(cls_sem, 16)
                for n in range(2):
                    sp.wait_ge(stored[n], 16 * NCH // 2)


SSM_NAMES = ["log_real", "imag", "log_Delta", "B_real", "B_imag", "C_real", "C_imag", "D"]
_INS = (["x", "cls_tok"]
        + ["L0_tok_" + n for n in ("conv1_w", "conv1_b", "bn_gamma", "bn_beta", "bn_mean", "bn_var", "conv2_w", "conv2_b")]
        + ["L0_attn_fwd_" + n for n in SSM_NAMES] + ["L0_attn_bwd_" + n for n in SSM_NAMES]
        + ["L0_ffn_" + n for n in ("W1", "b1", "Wg", "bg", "Wd", "bd")])
_OUT = (B, C * HW + 1, F)


def kernel(**inputs):
    import concourse.bacc as bacc
    from concourse.bass_utils import run_bass_kernel_spmd

    nc = bacc.Bacc("TRN2", target_bir_lowering=False, num_devices=1)
    arrays, aps = {}, []
    for name in _INS:
        a = np.ascontiguousarray(inputs[name])
        arrays["in_" + name] = a
        aps.append(nc.dram_tensor("in_" + name, a.shape, mybir.dt.from_np(a.dtype), kind="ExternalInput").ap())
    out = nc.dram_tensor("out_0", _OUT, F32, kind="ExternalOutput").ap()
    vit_tower(nc, aps, out)
    r = run_bass_kernel_spmd(nc, [arrays], core_ids=[0])
    return r.results[0]["out_0"]
```
